# Optimizing a Trainium2 kernel written in Bass

```python
import numpy as np
import jax
import jax.numpy as jnp

def _softmax(x, axis=-1):
    return jax.nn.softmax(x, axis=axis)

def _gelu(x):
    return jax.nn.gelu(x, approximate=True)

def _silu(x):
    return jax.nn.silu(x)

def _sigmoid(x):
    return jax.nn.sigmoid(x)

def _layernorm(x, axis=-1, eps=1e-05):
    m = jnp.mean(x, axis=axis, keepdims=True)
    v = jnp.var(x, axis=axis, keepdims=True)
    return (x - m) / jnp.sqrt(v + eps)

def _scatter_add(tgt, idx, src, axis=0):
    return tgt.at[idx].add(src)

def _segment_sum(src, seg, n):
    return jax.ops.segment_sum(src, seg, n)
kernel_name = 'mk_prb_d2_jaxref_r8_4225ef'

def setup_inputs(seed: int=0):
    np.random.seed(seed)
    _w = jnp.asarray

    def _L0_attn_setup():
        import jax, jax.numpy as jnp
        import numpy as np
        import math
        N_HEAD = 16
        HEAD_DIM = 64
        N_EMBD = 128
        MIN_CTX = 32
        FULL_CTX = 128

        def _pruning_ratio(T):
            if T < MIN_CTX:
                return 1.0
            if T >= FULL_CTX:
                return 0.2
            progress = (T - MIN_CTX) / (FULL_CTX - MIN_CTX)
            return 0.5 - 0.3 * progress
        key = jax.random.key(seed)
        k1, k2, k3, k4, k5 = jax.random.split(key, 5)
        B, T = (1, 256)
        x = jax.random.normal(k1, (B, T, N_EMBD), dtype=jnp.float32)
        W_attn = jax.random.normal(k2, (3 * N_HEAD * HEAD_DIM, N_EMBD), dtype=jnp.float32) * 0.02
        b_attn = jnp.zeros((3 * N_HEAD * HEAD_DIM,), dtype=jnp.float32)
        W_proj = jax.random.normal(k3, (N_EMBD, N_HEAD * HEAD_DIM), dtype=jnp.float32) * 0.02
        b_proj = jnp.zeros((N_EMBD,), dtype=jnp.float32)
        return {'x': x, 'W_attn': W_attn, 'b_attn': b_attn, 'W_proj': W_proj, 'b_proj': b_proj}
    _L0_attn_in = _L0_attn_setup()

    def _L0_ffn_setup():
        import jax, jax.numpy as jnp
        import numpy as np
        B, L, D = (4, 128, 128)
        E, H, K = (16, 64, 8)
        EPS = 1e-12

        def _l2norm(v, axis=-1):
            n = jnp.sqrt(jnp.sum(v * v, axis=axis, keepdims=True))
            return v / jnp.maximum(n, EPS)
        if __name__ == '__main__':
            out = reference(**setup_inputs())
            print(out.shape)
        key = jax.random.key(seed)
        ks = jax.random.split(key, 8)
        s = lambda fan_in: 1.0 / np.sqrt(fan_in)
        return {'x': jax.random.normal(ks[0], (B, L, D), jnp.float32), 'gate_w': jax.random.normal(ks[1], (E, D), jnp.float32) * s(D), 'w_gate': jax.random.normal(ks[2], (E, D, H), jnp.float32) * s(D), 'w_up': jax.random.normal(ks[3], (E, D, H), jnp.float32) * s(D), 'w_down': jax.random.normal(ks[4], (E, H, D), jnp.float32) * s(H), 'sw_gate': jax.random.normal(ks[5], (D, H), jnp.float32) * s(D), 'sw_up': jax.random.normal(ks[6], (D, H), jnp.float32) * s(D), 'sw_down': jax.random.normal(ks[7], (H, D), jnp.float32) * s(H)}
    _L0_ffn_in = _L0_ffn_setup()

    def _L1_attn_setup():
        import jax, jax.numpy as jnp
        import numpy as np
        import jax.scipy.linalg as jsp
        H = 8
        C = 64
        D_CONV = 4
        EPS_L2 = 1e-06
        EPS_RMS = 1e-05

        def l2norm(x):
            return x * jax.lax.rsqrt(jnp.sum(x * x, axis=-1, keepdims=True) + EPS_L2)

        def _causal_depthwise_conv(x, w, b):
            B, T, D = x.shape
            xp = jnp.pad(x, ((0, 0), (D_CONV - 1, 0), (0, 0)))
            out = b
            for j in range(D_CONV):
                out = out + xp[:, j:j + T] * w[:, j]
            return out

        def _forward(x, Wv, Wg, Wo, Wb, Wa, dt_bias, A_log, norm_w, conv_w, conv_b):
            B, T, D = x.shape
            K = D // H
            n = T // C
            rk = l2norm(x.reshape(B, T, H, K)) / np.sqrt(K)
            x_shift = jnp.pad(x[:, :-1], ((0, 0), (1, 0), (0, 0)))
            wk = l2norm(x_shift.reshape(B, T, H, K))
            v = jax.nn.silu(_causal_depthwise_conv(x @ Wv.T, conv_w, conv_b)).reshape(B, T, H, K)
            gate = (x @ Wg.T).reshape(B, T, H, K)
            beta = jax.nn.sigmoid(x @ Wb.T)
            decay = -jnp.exp(A_log) * jax.nn.softplus(x @ Wa.T + dt_bias)
            rk, wk, v = (jnp.transpose(t, (0, 2, 1, 3)) for t in (rk, wk, v))
            beta_t = jnp.transpose(beta, (0, 2, 1))[..., None]
            v = v * beta_t
            wk_beta = wk * beta_t
            ch = lambda t: t.reshape(B, H, n, C, K)
            rk, wk, v, wk_beta = (ch(rk), ch(wk), ch(v), ch(wk_beta))
            decay = jnp.cumsum(jnp.transpose(decay, (0, 2, 1)).reshape(B, H, n, C), axis=-1)
            decay_exp = jnp.exp(decay)[..., None]
            tril = jnp.tril(jnp.ones((C, C), dtype=bool))
            strict_lower = jnp.tril(jnp.ones((C, C), dtype=bool), k=-1)
            diff = decay[..., :, None] - decay[..., None, :]
            L_mask = jnp.where(tril, jnp.exp(jnp.where(tril, diff, 0.0)), 0.0)
            A_strict = jnp.where(strict_lower, -(jnp.einsum('bhnck,bhndk->bhncd', wk_beta, wk) * L_mask), 0.0)
            eye = jnp.eye(C, dtype=x.dtype)
            Tmat = jsp.solve_triangular(eye - A_strict, jnp.broadcast_to(eye, A_strict.shape), lower=True)
            v = Tmat @ v
            wk_cumdecay = Tmat @ (wk_beta * decay_exp)

            def step(S, inp):
                rk_i, wk_i, v_i, wkc_i, L_i, dec_i = inp
                attn = jnp.where(tril, jnp.einsum('bhck,bhdk->bhcd', rk_i, wk_i) * L_i, 0.0)
                v_new = v_i - wkc_i @ S
                o_inter = rk_i * jnp.exp(dec_i)[..., None] @ S
                o_i = o_inter + attn @ v_new
                dw = jnp.exp(dec_i[..., -1:] - dec_i)[..., None]
                S_new = S * jnp.exp(dec_i[..., -1])[..., None, None] + jnp.einsum('bhck,bhcv->bhkv', wk_i * dw, v_new)
                return (S_new, o_i)
            mv = lambda t: jnp.moveaxis(t, 2, 0)
            S0 = jnp.zeros((B, H, K, K), dtype=x.dtype)
            _, o = jax.lax.scan(step, S0, (mv(rk), mv(wk), mv(v), mv(wk_cumdecay), mv(L_mask), mv(decay)))
            o = jnp.transpose(o, (1, 0, 3, 2, 4)).reshape(B, T, H, K)
            o = o * jax.lax.rsqrt(jnp.mean(o * o, axis=-1, keepdims=True) + EPS_RMS) * norm_w
            o = o * jax.nn.silu(gate)
            return o.reshape(B, T, D) @ Wo.T
        key = jax.random.key(seed)
        ks = jax.random.split(key, 12)
        B, T, D = (4, 512, 128)
        x = jax.random.normal(ks[0], (B, T, D), dtype=jnp.float32)
        s = 0.02
        Wv = jax.random.normal(ks[1], (D, D), dtype=jnp.float32) * s
        Wg = jax.random.normal(ks[2], (D, D), dtype=jnp.float32) * s
        Wo = jax.random.normal(ks[3], (D, D), dtype=jnp.float32) * s
        Wb = jax.random.normal(ks[4], (H, D), dtype=jnp.float32) * s
        Wa = jax.random.normal(ks[5], (H, D), dtype=jnp.float32) * s
        u = jax.random.uniform(ks[6], (H,))
        dt = jnp.exp(u * (jnp.log(0.1) - jnp.log(0.001)) + jnp.log(0.001))
        dt_bias = dt + jnp.log(-jnp.expm1(-dt))
        A_log = jnp.log(jax.random.uniform(ks[7], (H,)) * 16.0 + 0.0001)
        norm_w = jnp.ones((D // H,), dtype=jnp.float32)
        conv_w = jax.random.normal(ks[8], (D, D_CONV), dtype=jnp.float32) * 0.1
        conv_b = jnp.zeros((D,), dtype=jnp.float32)
        return {'x': x, 'Wv': Wv, 'Wg': Wg, 'Wo': Wo, 'Wb': Wb, 'Wa': Wa, 'dt_bias': dt_bias, 'A_log': A_log, 'norm_w': norm_w, 'conv_w': conv_w, 'conv_b': conv_b}
    _L1_attn_in = _L1_attn_setup()

    def _L1_ffn_setup():
        import jax, jax.numpy as jnp
        import numpy as np
        DIM = 128
        DEPTH = 2
        HEADS = 8
        DIM_HEAD = 64
        WINDOW = 64
        INNER = HEADS * DIM_HEAD
        HID = int(DIM * 4 * 2 / 3)
        B, N = (2, 1024)
        QK_SCALE = 8.0

        def shift_token(t):
            t1, t2 = jnp.split(t, 2, axis=-1)
            t2 = jnp.pad(t2, ((0, 0), (1, 0), (0, 0)))[:, :-1]
            return jnp.concatenate([t1, t2], axis=-1)

        def l2norm(t):
            return t / jnp.clip(jnp.linalg.norm(t, axis=-1, keepdims=True), 1e-12)

        def rotate_half(x):
            x1, x2 = jnp.split(x, 2, axis=-1)
            return jnp.concatenate([-x2, x1], axis=-1)

        def rotary_xpos(q, k):
            n = q.shape[-2]
            half_idx = jnp.arange(0, DIM_HEAD, 2, dtype=jnp.float32)
            inv_freq = 1.0 / 10000.0 ** (half_idx / DIM_HEAD)
            t = jnp.arange(n, dtype=jnp.float32)
            freqs = t[:, None] * inv_freq[None, :]
            freqs = jnp.concatenate([freqs, freqs], axis=-1)
            base = (half_idx + 0.4 * DIM_HEAD) / (1.4 * DIM_HEAD)
            power = (t - n // 2) / float(WINDOW // 2)
            scale = base[None, :] ** power[:, None]
            scale = jnp.concatenate([scale, scale], axis=-1)
            cos, sin = (jnp.cos(freqs), jnp.sin(freqs))
            q = q * cos * scale + rotate_half(q) * sin * scale
            k = k * cos / scale + rotate_half(k) * sin / scale
            return (q, k)

        def local_attention(q, k, v):
            b, h, n, d = q.shape
            w = n // WINDOW
            bq = q.reshape(b, h, w, WINDOW, d) * QK_SCALE
            bk = k.reshape(b, h, w, WINDOW, d)
            bv = v.reshape(b, h, w, WINDOW, d)

            def look_around(t):
                p = jnp.pad(t, ((0, 0), (0, 0), (1, 0), (0, 0), (0, 0)))
                return jnp.concatenate([p[:, :, :w], p[:, :, 1:]], axis=3)
            bk, bv = (look_around(bk), look_around(bv))
            bt = jnp.arange(n).reshape(w, WINDOW)
            btp = jnp.pad(bt, ((1, 0), (0, 0)), constant_values=-1)
            btk = jnp.concatenate([btp[:w], btp[1:]], axis=1)
            sim = jnp.einsum('bhwid,bhwjd->bhwij', bq, bk)
            i = bt[:, :, None]
            j = btk[:, None, :]
            mask = (i < j) | (i > j + WINDOW) | (j == -1)
            sim = jnp.where(mask, -jnp.finfo(sim.dtype).max, sim)
            attn = jax.nn.softmax(sim, axis=-1)
            out = jnp.einsum('bhwij,bhwjd->bhwid', attn, bv)
            return out.reshape(b, h, n, d)

        def _layer(x, wqkv, qs, ksc, wo, lg, lb, w1, b1, w2, b2):
            b, n, _ = x.shape
            h = shift_token(x)
            qkv = h @ wqkv
            q, k, v = jnp.split(qkv, 3, axis=-1)
            to_heads = lambda t: t.reshape(b, n, HEADS, DIM_HEAD).transpose(0, 2, 1, 3)
            q, k, v = (to_heads(q), to_heads(k), to_heads(v))
            q = l2norm(q) * qs
            k = l2norm(k) * ksc
            q, k = rotary_xpos(q, k)
            o = local_attention(q, k, v)
            o = o.transpose(0, 2, 1, 3).reshape(b, n, INNER)
            x = x + o @ wo
            h = shift_token(x)
            mu = h.mean(-1, keepdims=True)
            var = h.var(-1, keepdims=True)
            h = (h - mu) / jnp.sqrt(var + 1e-05) * lg + lb
            h = h @ w1 + b1
            a, g = jnp.split(h, 2, axis=-1)
            h = a * jax.nn.gelu(g, approximate=False)
            x = x + h @ w2 + b2
            return x
        key = jax.random.key(seed)
        ks = jax.random.split(key, 6)
        return {'x': jax.random.normal(ks[0], (B, N, DIM), jnp.float32), 'wqkv': jax.random.normal(ks[1], (DEPTH, DIM, 3 * INNER), jnp.float32) * 0.02, 'q_scale': jnp.ones((DEPTH, DIM_HEAD), jnp.float32), 'k_scale': jnp.ones((DEPTH, DIM_HEAD), jnp.float32), 'wo': jax.random.normal(ks[2], (DEPTH, INNER, DIM), jnp.float32) * 0.02, 'ln_g': jnp.ones((DEPTH, DIM), jnp.float32), 'ln_b': jnp.zeros((DEPTH, DIM), jnp.float32), 'w1': jax.random.normal(ks[3], (DEPTH, DIM, 2 * HID), jnp.float32) * 0.02, 'b1': jnp.zeros((DEPTH, 2 * HID), jnp.float32), 'w2': jax.random.normal(ks[4], (DEPTH, HID, DIM), jnp.float32) * 0.02, 'b2': jnp.zeros((DEPTH, DIM), jnp.float32)}
    _L1_ffn_in = _L1_ffn_setup()
    _d = {'L0_attn_x': _L0_attn_in['x'], 'L0_attn_W_attn': _L0_attn_in['W_attn'], 'L0_attn_b_attn': _L0_attn_in['b_attn'], 'L0_attn_W_proj': _L0_attn_in['W_proj'], 'L0_attn_b_proj': _L0_attn_in['b_proj'], 'L0_ffn_gate_w': _L0_ffn_in['gate_w'], 'L0_ffn_w_gate': _L0_ffn_in['w_gate'], 'L0_ffn_w_up': _L0_ffn_in['w_up'], 'L0_ffn_w_down': _L0_ffn_in['w_down'], 'L0_ffn_sw_gate': _L0_ffn_in['sw_gate'], 'L0_ffn_sw_up': _L0_ffn_in['sw_up'], 'L0_ffn_sw_down': _L0_ffn_in['sw_down'], 'L1_attn_Wv': _L1_attn_in['Wv'], 'L1_attn_Wg': _L1_attn_in['Wg'], 'L1_attn_Wo': _L1_attn_in['Wo'], 'L1_attn_Wb': _L1_attn_in['Wb'], 'L1_attn_Wa': _L1_attn_in['Wa'], 'L1_attn_dt_bias': _L1_attn_in['dt_bias'], 'L1_attn_A_log': _L1_attn_in['A_log'], 'L1_attn_norm_w': _L1_attn_in['norm_w'], 'L1_attn_conv_w': _L1_attn_in['conv_w'], 'L1_attn_conv_b': _L1_attn_in['conv_b'], 'L1_ffn_wqkv': _L1_ffn_in['wqkv'], 'L1_ffn_q_scale': _L1_ffn_in['q_scale'], 'L1_ffn_k_scale': _L1_ffn_in['k_scale'], 'L1_ffn_wo': _L1_ffn_in['wo'], 'L1_ffn_ln_g': _L1_ffn_in['ln_g'], 'L1_ffn_ln_b': _L1_ffn_in['ln_b'], 'L1_ffn_w1': _L1_ffn_in['w1'], 'L1_ffn_b1': _L1_ffn_in['b1'], 'L1_ffn_w2': _L1_ffn_in['w2'], 'L1_ffn_b2': _L1_ffn_in['b2']}
    _x0 = _d['L0_attn_x']
    _d['L0_attn_x'] = jax.random.normal(jax.random.fold_in(jax.random.key(seed), 1), (2, 1024, 128), dtype=_x0.dtype)
    del _x0
    return _d

def reference(L0_attn_x, L0_attn_W_attn, L0_attn_b_attn, L0_attn_W_proj, L0_attn_b_proj, L0_ffn_gate_w, L0_ffn_w_gate, L0_ffn_w_up, L0_ffn_w_down, L0_ffn_sw_gate, L0_ffn_sw_up, L0_ffn_sw_down, L1_attn_Wv, L1_attn_Wg, L1_attn_Wo, L1_attn_Wb, L1_attn_Wa, L1_attn_dt_bias, L1_attn_A_log, L1_attn_norm_w, L1_attn_conv_w, L1_attn_conv_b, L1_ffn_wqkv, L1_ffn_q_scale, L1_ffn_k_scale, L1_ffn_wo, L1_ffn_ln_g, L1_ffn_ln_b, L1_ffn_w1, L1_ffn_b1, L1_ffn_w2, L1_ffn_b2):

    def _L0_attn_ref(x, W_attn, b_attn, W_proj, b_proj):
        import jax, jax.numpy as jnp
        import numpy as np
        import math
        N_HEAD = 16
        HEAD_DIM = 64
        N_EMBD = 128
        MIN_CTX = 32
        FULL_CTX = 128

        def _pruning_ratio(T):
            if T < MIN_CTX:
                return 1.0
            if T >= FULL_CTX:
                return 0.2
            progress = (T - MIN_CTX) / (FULL_CTX - MIN_CTX)
            return 0.5 - 0.3 * progress
        B, T, C = x.shape
        H, hd = (N_HEAD, HEAD_DIM)
        qkv = x @ W_attn.T + b_attn
        q, k, v = jnp.split(qkv, 3, axis=-1)
        q = q.reshape(B, T, H, hd).transpose(0, 2, 1, 3)
        k = k.reshape(B, T, H, hd).transpose(0, 2, 1, 3)
        v = v.reshape(B, T, H, hd).transpose(0, 2, 1, 3)
        att = jnp.einsum('bhqd,bhkd->bhqk', q, k) * (1.0 / math.sqrt(hd))
        i = jnp.arange(T)
        causal = i[None, :] <= i[:, None]
        neg_inf = jnp.float32(-jnp.inf)
        att = jnp.where(causal[None, None], att, neg_inf)
        S = jnp.maximum(att[:, 0], 0.0)
        keepS = (i[None, :] != 0) & (i[:, None] != i[None, :])
        S = jnp.where(keepS[None], S, 0.0)
        S_shifted = jnp.roll(S, 1, axis=-2).at[:, 0, :].set(0.0)
        FF = jnp.cumsum(S_shifted, axis=-2)
        att = att - FF[:, None]
        ratio = _pruning_ratio(T)
        memory_budget = max(1, int(T * ratio))
        if ratio < 1.0:
            FF_mod = jnp.where(causal[None], FF, jnp.inf)
            sorted_idx = jnp.argsort(FF_mod, axis=-1)
            eff_k = jnp.minimum(memory_budget - 1, i + 1)
            sel = i[None, :] < eff_k[:, None]
            keep = jnp.zeros((B, T, T), dtype=bool)
            keep = keep.at[jnp.arange(B)[:, None, None], i[None, :, None], sorted_idx].set(jnp.broadcast_to(sel[None], (B, T, T)))
            keep = keep | jnp.eye(T, dtype=bool)[None]
            att = jnp.where(keep[:, None], att, neg_inf)
        y = jax.nn.softmax(att, axis=-1) @ v
        y = y.transpose(0, 2, 1, 3).reshape(B, T, H * hd)
        y = y @ W_proj.T + b_proj
        return y

    def _L0_ffn_ref(x, gate_w, w_gate, w_up, w_down, sw_gate, sw_up, sw_down):
        import jax, jax.numpy as jnp
        import numpy as np
        B, L, D = (4, 128, 128)
        E, H, K = (16, 64, 8)
        EPS = 1e-12

        def _l2norm(v, axis=-1):
            n = jnp.sqrt(jnp.sum(v * v, axis=axis, keepdims=True))
            return v / jnp.maximum(n, EPS)
        if __name__ == '__main__':
            out = reference(**setup_inputs())
            print(out.shape)
        b, l, d = x.shape
        xf = x.reshape(-1, d)
        logits = _l2norm(xf) @ _l2norm(gate_w).T
        scores = jax.nn.sigmoid(logits)
        topk_scores, topk_idx = jax.lax.top_k(scores, K)
        topk_w = topk_scores / jnp.sum(topk_scores, axis=-1, keepdims=True)
        combine = jnp.sum(jax.nn.one_hot(topk_idx, E, dtype=xf.dtype) * topk_w[..., None], axis=1)
        g = jnp.einsum('nd,edh->neh', xf, w_gate)
        u = jnp.einsum('nd,edh->neh', xf, w_up)
        y = jnp.einsum('neh,ehd->ned', jax.nn.silu(g) * u, w_down)
        routed = jnp.einsum('ned,ne->nd', y, combine)
        shared = jax.nn.silu(xf @ sw_gate) * (xf @ sw_up) @ sw_down
        return (routed + shared).reshape(b, l, d)

    def _L1_attn_ref(x, Wv, Wg, Wo, Wb, Wa, dt_bias, A_log, norm_w, conv_w, conv_b):
        import jax, jax.numpy as jnp
        import numpy as np
        import jax.scipy.linalg as jsp
        H = 8
        C = 64
        D_CONV = 4
        EPS_L2 = 1e-06
        EPS_RMS = 1e-05

        def l2norm(x):
            return x * jax.lax.rsqrt(jnp.sum(x * x, axis=-1, keepdims=True) + EPS_L2)

        def _causal_depthwise_conv(x, w, b):
            B, T, D = x.shape
            xp = jnp.pad(x, ((0, 0), (D_CONV - 1, 0), (0, 0)))
            out = b
            for j in range(D_CONV):
                out = out + xp[:, j:j + T] * w[:, j]
            return out

        def _forward(x, Wv, Wg, Wo, Wb, Wa, dt_bias, A_log, norm_w, conv_w, conv_b):
            B, T, D = x.shape
            K = D // H
            n = T // C
            rk = l2norm(x.reshape(B, T, H, K)) / np.sqrt(K)
            x_shift = jnp.pad(x[:, :-1], ((0, 0), (1, 0), (0, 0)))
            wk = l2norm(x_shift.reshape(B, T, H, K))
            v = jax.nn.silu(_causal_depthwise_conv(x @ Wv.T, conv_w, conv_b)).reshape(B, T, H, K)
            gate = (x @ Wg.T).reshape(B, T, H, K)
            beta = jax.nn.sigmoid(x @ Wb.T)
            decay = -jnp.exp(A_log) * jax.nn.softplus(x @ Wa.T + dt_bias)
            rk, wk, v = (jnp.transpose(t, (0, 2, 1, 3)) for t in (rk, wk, v))
            beta_t = jnp.transpose(beta, (0, 2, 1))[..., None]
            v = v * beta_t
            wk_beta = wk * beta_t
            ch = lambda t: t.reshape(B, H, n, C, K)
            rk, wk, v, wk_beta = (ch(rk), ch(wk), ch(v), ch(wk_beta))
            decay = jnp.cumsum(jnp.transpose(decay, (0, 2, 1)).reshape(B, H, n, C), axis=-1)
            decay_exp = jnp.exp(decay)[..., None]
            tril = jnp.tril(jnp.ones((C, C), dtype=bool))
            strict_lower = jnp.tril(jnp.ones((C, C), dtype=bool), k=-1)
            diff = decay[..., :, None] - decay[..., None, :]
            L_mask = jnp.where(tril, jnp.exp(jnp.where(tril, diff, 0.0)), 0.0)
            A_strict = jnp.where(strict_lower, -(jnp.einsum('bhnck,bhndk->bhncd', wk_beta, wk) * L_mask), 0.0)
            eye = jnp.eye(C, dtype=x.dtype)
            Tmat = jsp.solve_triangular(eye - A_strict, jnp.broadcast_to(eye, A_strict.shape), lower=True)
            v = Tmat @ v
            wk_cumdecay = Tmat @ (wk_beta * decay_exp)

            def step(S, inp):
                rk_i, wk_i, v_i, wkc_i, L_i, dec_i = inp
                attn = jnp.where(tril, jnp.einsum('bhck,bhdk->bhcd', rk_i, wk_i) * L_i, 0.0)
                v_new = v_i - wkc_i @ S
                o_inter = rk_i * jnp.exp(dec_i)[..., None] @ S
                o_i = o_inter + attn @ v_new
                dw = jnp.exp(dec_i[..., -1:] - dec_i)[..., None]
                S_new = S * jnp.exp(dec_i[..., -1])[..., None, None] + jnp.einsum('bhck,bhcv->bhkv', wk_i * dw, v_new)
                return (S_new, o_i)
            mv = lambda t: jnp.moveaxis(t, 2, 0)
            S0 = jnp.zeros((B, H, K, K), dtype=x.dtype)
            _, o = jax.lax.scan(step, S0, (mv(rk), mv(wk), mv(v), mv(wk_cumdecay), mv(L_mask), mv(decay)))
            o = jnp.transpose(o, (1, 0, 3, 2, 4)).reshape(B, T, H, K)
            o = o * jax.lax.rsqrt(jnp.mean(o * o, axis=-1, keepdims=True) + EPS_RMS) * norm_w
            o = o * jax.nn.silu(gate)
            return o.reshape(B, T, D) @ Wo.T
        return _forward(x, Wv, Wg, Wo, Wb, Wa, dt_bias, A_log, norm_w, conv_w, conv_b)

    def _L1_ffn_ref(x, wqkv, q_scale, k_scale, wo, ln_g, ln_b, w1, b1, w2, b2):
        import jax, jax.numpy as jnp
        import numpy as np
        DIM = 128
        DEPTH = 2
        HEADS = 8
        DIM_HEAD = 64
        WINDOW = 64
        INNER = HEADS * DIM_HEAD
        HID = int(DIM * 4 * 2 / 3)
        B, N = (2, 1024)
        QK_SCALE = 8.0

        def shift_token(t):
            t1, t2 = jnp.split(t, 2, axis=-1)
            t2 = jnp.pad(t2, ((0, 0), (1, 0), (0, 0)))[:, :-1]
            return jnp.concatenate([t1, t2], axis=-1)

        def l2norm(t):
            return t / jnp.clip(jnp.linalg.norm(t, axis=-1, keepdims=True), 1e-12)

        def rotate_half(x):
            x1, x2 = jnp.split(x, 2, axis=-1)
            return jnp.concatenate([-x2, x1], axis=-1)

        def rotary_xpos(q, k):
            n = q.shape[-2]
            half_idx = jnp.arange(0, DIM_HEAD, 2, dtype=jnp.float32)
            inv_freq = 1.0 / 10000.0 ** (half_idx / DIM_HEAD)
            t = jnp.arange(n, dtype=jnp.float32)
            freqs = t[:, None] * inv_freq[None, :]
            freqs = jnp.concatenate([freqs, freqs], axis=-1)
            base = (half_idx + 0.4 * DIM_HEAD) / (1.4 * DIM_HEAD)
            power = (t - n // 2) / float(WINDOW // 2)
            scale = base[None, :] ** power[:, None]
            scale = jnp.concatenate([scale, scale], axis=-1)
            cos, sin = (jnp.cos(freqs), jnp.sin(freqs))
            q = q * cos * scale + rotate_half(q) * sin * scale
            k = k * cos / scale + rotate_half(k) * sin / scale
            return (q, k)

        def local_attention(q, k, v):
            b, h, n, d = q.shape
            w = n // WINDOW
            bq = q.reshape(b, h, w, WINDOW, d) * QK_SCALE
            bk = k.reshape(b, h, w, WINDOW, d)
            bv = v.reshape(b, h, w, WINDOW, d)

            def look_around(t):
                p = jnp.pad(t, ((0, 0), (0, 0), (1, 0), (0, 0), (0, 0)))
                return jnp.concatenate([p[:, :, :w], p[:, :, 1:]], axis=3)
            bk, bv = (look_around(bk), look_around(bv))
            bt = jnp.arange(n).reshape(w, WINDOW)
            btp = jnp.pad(bt, ((1, 0), (0, 0)), constant_values=-1)
            btk = jnp.concatenate([btp[:w], btp[1:]], axis=1)
            sim = jnp.einsum('bhwid,bhwjd->bhwij', bq, bk)
            i = bt[:, :, None]
            j = btk[:, None, :]
            mask = (i < j) | (i > j + WINDOW) | (j == -1)
            sim = jnp.where(mask, -jnp.finfo(sim.dtype).max, sim)
            attn = jax.nn.softmax(sim, axis=-1)
            out = jnp.einsum('bhwij,bhwjd->bhwid', attn, bv)
            return out.reshape(b, h, n, d)

        def _layer(x, wqkv, qs, ksc, wo, lg, lb, w1, b1, w2, b2):
            b, n, _ = x.shape
            h = shift_token(x)
            qkv = h @ wqkv
            q, k, v = jnp.split(qkv, 3, axis=-1)
            to_heads = lambda t: t.reshape(b, n, HEADS, DIM_HEAD).transpose(0, 2, 1, 3)
            q, k, v = (to_heads(q), to_heads(k), to_heads(v))
            q = l2norm(q) * qs
            k = l2norm(k) * ksc
            q, k = rotary_xpos(q, k)
            o = local_attention(q, k, v)
            o = o.transpose(0, 2, 1, 3).reshape(b, n, INNER)
            x = x + o @ wo
            h = shift_token(x)
            mu = h.mean(-1, keepdims=True)
            var = h.var(-1, keepdims=True)
            h = (h - mu) / jnp.sqrt(var + 1e-05) * lg + lb
            h = h @ w1 + b1
            a, g = jnp.split(h, 2, axis=-1)
            h = a * jax.nn.gelu(g, approximate=False)
            x = x + h @ w2 + b2
            return x
        for l in range(DEPTH):
            x = _layer(x, wqkv[l], q_scale[l], k_scale[l], wo[l], ln_g[l], ln_b[l], w1[l], b1[l], w2[l], b2[l])
        return x
    x = L0_attn_x
    xn = _layernorm(x, axis=-1)
    x = x + _L0_attn_ref(xn, L0_attn_W_attn, L0_attn_b_attn, L0_attn_W_proj, L0_attn_b_proj) + _L0_ffn_ref(xn, L0_ffn_gate_w, L0_ffn_w_gate, L0_ffn_w_up, L0_ffn_w_down, L0_ffn_sw_gate, L0_ffn_sw_up, L0_ffn_sw_down)
    xn = _layernorm(x, axis=-1)
    x = x + _L1_attn_ref(xn, L1_attn_Wv, L1_attn_Wg, L1_attn_Wo, L1_attn_Wb, L1_attn_Wa, L1_attn_dt_bias, L1_attn_A_log, L1_attn_norm_w, L1_attn_conv_w, L1_attn_conv_b) + _L1_ffn_ref(xn, L1_ffn_wqkv, L1_ffn_q_scale, L1_ffn_k_scale, L1_ffn_wo, L1_ffn_ln_g, L1_ffn_ln_b, L1_ffn_w1, L1_ffn_b1, L1_ffn_w2, L1_ffn_b2)
    return x

_drawn_inputs = setup_inputs


def setup_inputs(seed=0):
    import zlib

    import numpy as np

    out = dict(_drawn_inputs(seed))
    spreads = {'L0_attn_b_attn': (0.0, 0.1),
     'L0_attn_b_proj': (0.0, 0.1),
     'L1_attn_norm_w': (1.0, 0.6),
     'L1_attn_conv_b': (0.0, 2.0),
     'L1_ffn_q_scale': (1.0, 0.6),
     'L1_ffn_k_scale': (1.0, 0.6),
     'L1_ffn_ln_g': (1.0, 0.6),
     'L1_ffn_ln_b': (0.0, 0.8),
     'L1_ffn_b1': (0.0, 0.8),
     'L1_ffn_b2': (0.0, 0.672)}
    factors = {'L0_attn_W_attn': 3.771,
     'L1_attn_Wv': 8.0,
     'L1_attn_Wg': 5.903,
     'L1_attn_Wo': 5.791,
     'L1_attn_Wb': 8.0,
     'L1_attn_Wa': 64.0,
     'L1_attn_dt_bias': 64.0,
     'L1_attn_A_log': 23.053,
     'L1_attn_conv_w': 8.0,
     'L1_ffn_wqkv': 3.824,
     'L1_ffn_wo': 3.624,
     'L1_ffn_w1': 7.153,
     'L1_ffn_w2': 6.997}
    for name, (base, spread) in spreads.items():
        noise = np.random.default_rng([zlib.crc32(name.encode()), seed]).standard_normal(out[name].shape)
        drawn = base * np.exp(spread * noise) if base else spread * noise
        out[name] = jnp.asarray(drawn.astype(out[name].dtype))
    for name, factor in factors.items():
        out[name] = (out[name] * factor).astype(out[name].dtype)
    return out
```

```python
from contextlib import ExitStack, contextmanager

import numpy as np

import concourse.bass as bass
from concourse import mybir

F32 = mybir.dt.float32
I32 = mybir.dt.int32
BF16 = mybir.dt.bfloat16
ALU = mybir.AluOpType
ACT = mybir.ActivationFunctionType
AX = mybir.AxisListType.X
ds = bass.ds

P = 128
B, T, D = 2, 1024, 128
NT = T // P
HALF = 512
BIG = 1.5e38
LN_EPS = 1e-5

H0, HD0 = 16, 64
PAIRS = H0 // 2
BUDGET = max(1, int(T * 0.2))
KEEP = min(BUDGET - 1, T)
TSEL = KEEP // P
NSEL = NT - TSEL
E0, HE0, TOPK = 16, 64, 8
PACKS = E0 // 2 + 1
H1, K1, C1 = 8, 16, 64
NC1 = T // C1
EPS_L2, EPS_RMS = 1e-6, 1e-5
DEPTH, H2, HD2, WIN = 2, 8, 64, 64
INNER = H2 * HD2
HID = int(D * 4 * 2 / 3)
HCH = [(0, 128), (128, 128), (256, HID - 256)]
KW = WIN + P


@contextmanager
def signals(nc, names):
    with ExitStack() as ctx:
        got = [ctx.enter_context(nc.semaphore(n)) for n in names.split()]
        yield got
        nums = sorted(s.num for s in got)
        while nums:
            run = next(k for k in range(1, len(nums) + 1) if k == len(nums) or nums[k] != nums[0] + k)
            nc.gpsimd.sem_clear(range(nums[0], nums[0] + run))
            nums = nums[run:]
        nc.all_engine_barrier()


class Chain:

    def __init__(self, eng, sem, base=0):
        self.eng, self.sem, self.base, self.n = eng, sem, base, 0

    def add(self, ins):
        self.n += 1
        ins.then_inc(self.sem, 1)

    def hold(self):
        self.eng.wait_ge(self.sem, self.base + self.n)

    def link(self, ins):
        self.add(ins)
        self.hold()


def bcast(ap, *shape):
    return ap.to_broadcast(list(shape))




def norm_stage(nc, m, src, out, outT, gain=None, shift=None):
    with signals(nc, "stats_step var_ready rstd_root normed turned outT_step") as (
            stats_step, var_ready, rstd_root, normed, turned, outT_step):
        with nc.Block() as block:
            @block.vector
            def _(dve):
                ch = Chain(dve, stats_step)
                for t in range(NT):
                    ch.add(nc.vector.bn_stats(m.bn[:, t, :], src[:, t, :]))
                ch.hold()
                for t in range(NT):
                    ch.add(nc.vector.bn_aggr(m.mv[:, t, :], m.bn[:, t, :]))
                ch.hold()
                nc.vector.tensor_scalar(m.rstd[:], m.mv[:, :, 1], LN_EPS, None, ALU.add).then_inc(var_ready, 1)
                dve.wait_ge(rstd_root, 1)
                ch.link(nc.vector.reciprocal(m.rstd[:], m.rstd[:]))
                for t in range(NT):
                    nc.vector.tensor_scalar(out[:, t, :], src[:, t, :], m.mv[:, t, 0:1], m.rstd[:, t:t + 1],
                                            ALU.subtract, ALU.mult).then_inc(normed, 1)

            @block.tensor
            def _(pe):
                for t in range(NT):
                    pe.wait_ge(normed, t + 1)
                    nc.tensor.transpose(m.ps[:, t // 4, (t % 4) * P:(t % 4 + 1) * P], out[:, t, :],
                                        m.ident[:]).then_inc(turned, 1)

            @block.scalar
            def _(act):
                act.wait_ge(var_ready, 1)
                nc.scalar.activation(m.rstd[:], m.rstd[:], ACT.Sqrt).then_inc(rstd_root, 1)
                for half in range(2):
                    act.wait_ge(turned, 4 * half + 4)
                    o = outT[:, half * HALF:(half + 1) * HALF]
                    if gain is None:
                        nc.scalar.activation(o, m.ps[:, half, :], ACT.Copy).then_inc(outT_step, 1)
                    else:
                        nc.scalar.activation(o, m.ps[:, half, :], ACT.Identity, bias=shift,
                                             scale=gain).then_inc(outT_step, 1)




def experts_stage(nc, m, packs):
    with signals(nc, "pack0 pack1 sq_ready root_ready dv logits_ready scores_ready topk_step combT_turned "
                     "combT_ready gates_ready silu_ready hidden_ready used_pack out_done out_ready") as (
            pack0, pack1, sq_ready, root_ready, dv, logits_ready, scores_ready, topk_step, combT_turned,
            combT_ready, gates_ready, silu_ready, hidden_ready, used_pack, out_done, out_ready):
        pack_sem = [pack0, pack1]
        nloop = PACKS // 2
        with nc.Block() as block:
            @block.sync
            def _(sp):
                for s in range(2):
                    sp.dma_start(m.pack[:, s, :], packs[s]).then_inc(pack_sem[s], 16)
                with sp.Fori(1, nloop) as it:
                    for s in range(2):
                        sp.wait_ge(used_pack, it * 2 - 1 + s)
                        sp.dma_start(m.pack[:, s, :], packs[ds(it * 2 + s, 1)].rearrange("o p n -> (o p) n")
                                     ).then_inc(pack_sem[s], 16)
                sp.wait_ge(used_pack, PACKS - 2)
                sp.dma_start(m.pack[:, 0, :], packs[PACKS - 1]).then_inc(pack_sem[0], 16)

            def elementwise(dve, k, it2, s, half, first):
                base = it2 * 4 + k
                dve.wait_ge(silu_ready, base + 1)
                c = dv_chain[0]
                c.link(nc.vector.tensor_tensor(m.hid[:, half, :], m.ps[:, 2 + half, :], m.silu[:, half, :], ALU.mult))
                nc.vector.tensor_tensor(m.hid[:, half, :], m.ps[:, 4 + half, :], m.hid[:, half, :],
                                        ALU.mult).then_inc(hidden_ready, 1)

            dv_chain = [None]
            TOPK_STEPS = [0]

            @block.vector
            def _(dve):
                ch = Chain(dve, dv)
                dve.wait_ge(root_ready, 1)
                ch.link(nc.vector.tensor_scalar(m.rs8[:], m.rs8[:], 1e-12, None, ALU.max))
                ch.link(nc.vector.reciprocal(m.rs8[:], m.rs8[:]))
                dve.wait_ge(logits_ready, NT)
                nc.vector.tensor_tensor(m.score[:, :, 0:E0], m.ps[:, 0, 0:NT * E0].rearrange("p (t e) -> p t e", e=E0),
                                        bcast(m.rs8[:].unsqueeze(2), P, NT, E0), ALU.mult).then_inc(topk_step, 1)
                dve.wait_ge(scores_ready, 1)
                for t in range(NT):
                    ch.add(nc.vector.max(m.top8[:, t, :], m.score[:, t, 0:E0]))
                ch.hold()
                for t in range(NT):
                    ch.add(nc.vector.match_replace(m.rest[:, t, :], m.top8[:, t, :], m.score[:, t, 0:E0], -1.0))
                ch.hold()
                ch.link(nc.vector.scalar_tensor_tensor(out=m.rest[:], in0=m.rest[:], scalar=0.0,
                                                       in1=m.score[:, :, 0:E0], op0=ALU.is_lt, op1=ALU.mult))
                ch.link(nc.vector.tensor_reduce(m.rs8b[:], m.rest[:], AX, ALU.add))
                ch.link(nc.vector.reciprocal(m.rs8b[:], m.rs8b[:]))
                nc.vector.tensor_tensor(m.score[:, :, 0:E0], m.rest[:], bcast(m.rs8b[:].unsqueeze(2), P, NT, E0),
                                        ALU.mult).then_inc(topk_step, 1)
                base = ch.n
                with dve.Fori(0, nloop) as it:
                    c = dv_chain[0] = Chain(dve, dv, base + it * 4)
                    for k in range(4):
                        elementwise(dve, k, it, k // 2, k % 2, False)
                    assert c.n == 4
                dv_chain[0] = Chain(dve, dv, base + 4 * nloop)
                for k in range(2):
                    elementwise(dve, k, nloop, 0, k, False)

            @block.scalar
            def _(act):
                for t in range(NT):
                    nc.scalar.activation(m.silu[:, t // 4, (t % 4) * P:(t % 4 + 1) * P], m.xn[:, t, :], ACT.Square,
                                         accum_out=m.rs8[:, t:t + 1]).then_inc(sq_ready, 1)
                act.wait_ge(sq_ready, NT)
                nc.scalar.activation(m.rs8[:], m.rs8[:], ACT.Sqrt).then_inc(root_ready, 1)
                act.wait_ge(topk_step, 1)
                nc.scalar.activation(m.score[:, :, 0:E0], m.score[:, :, 0:E0], ACT.Sigmoid).then_inc(scores_ready, 1)
                for half in range(2):
                    act.wait_ge(combT_turned, 4 * (half + 1))
                    nc.scalar.activation(m.combT[0:E0 + 1, half * HALF:(half + 1) * HALF],
                                         m.ps[0:E0 + 1, half, :], ACT.Copy).then_inc(combT_ready, 1)

                def silu(n, half):
                    act.wait_ge(gates_ready, n + 1)
                    nc.scalar.activation(m.silu[:, half, :], m.ps[:, half, :], ACT.Silu).then_inc(silu_ready, 1)

                with act.Fori(0, nloop) as it:
                    for k in range(4):
                        silu(it * 4 + k, k % 2)
                for k in range(2):
                    silu(nloop * 4 + k, k)
                for half in range(2):
                    act.wait_ge(out_done, 1)
                    nc.scalar.activation(m.ffnT[:, half * HALF:(half + 1) * HALF], m.ps[:, 6 + half, :],
                                         ACT.Copy).then_inc(out_ready, 1)

            @block.tensor
            def _(pe):
                for t in range(NT):
                    nc.tensor.matmul(m.ps[:, 0, t * E0:(t + 1) * E0], m.xnT[:, t * P:(t + 1) * P],
                                     m.gateT[:, 0:E0], start=True, stop=True).then_inc(logits_ready, 1)
                pe.wait_ge(topk_step, 2)
                for t in range(NT):
                    nc.tensor.transpose(m.ps[0:E0 + 1, t // 4, (t % 4) * P:(t % 4 + 1) * P], m.score[:, t, :],
                                        m.ident[:]).then_inc(combT_turned, 1)
                for half in range(2):
                    nc.tensor.matmul(m.ps[:, 6 + half, :], m.zeros[:, 0:P], m.xnT[:, half * HALF:(half + 1) * HALF],
                                     start=True, stop=False, skip_group_check=True)

                def up(n, s, half, wait_hidden):
                    if wait_hidden is not None:
                        pe.wait_ge(hidden_ready, wait_hidden)
                    x = m.xnT[:, half * HALF:(half + 1) * HALF]
                    nc.tensor.matmul(m.ps[:, 2 + half, :], m.pack[:, s, P:2 * P], x, start=True, stop=True)
                    nc.tensor.matmul(m.ps[:, 4 + half, :], m.pack[0:E0 + 1, s, 3 * P:4 * P],
                                     m.combT[0:E0 + 1, half * HALF:(half + 1) * HALF], start=True, stop=True)
                    nc.tensor.matmul(m.ps[:, half, :], m.pack[:, s, 0:P], x, start=True,
                                     stop=True).then_inc(gates_ready, 1)

                def down(n, s, half):
                    pe.wait_ge(hidden_ready, n + 1)
                    ins = nc.tensor.matmul(m.ps[:, 6 + half, :], m.pack[:, s, 2 * P:3 * P], m.hid[:, half, :],
                                           start=False, stop=False, skip_group_check=True)
                    if half == 1:
                        ins.then_inc(used_pack, 1)

                pe.wait_ge(combT_ready, 2)
                pe.wait_ge(pack0, 16)
                up(0, 0, 0, None)
                up(1, 0, 1, None)
                with pe.Fori(0, nloop) as it:
                    for k in range(4):
                        down(it * 4 + k, k // 2, k % 2)
                        s = (k // 2 + 1) % 2
                        if k % 2 == 0:
                            pe.wait_ge(pack_sem[s], (it + 1) * 16 if s == 1 else (it + 2) * 16)
                        up(it * 4 + k + 2, s, k % 2, it * 4 + k + 1)
                for k in range(2):
                    down(nloop * 4 + k, 0, k)
                nc.tensor.matmul(m.ps[:, 7, :], m.zeros[:, 0:P], m.xnT[:, 0:HALF], start=False, stop=True,
                                 skip_group_check=True).then_inc(out_done, 1)




def penalty_stage(nc, m, qkv_packs):
    with signals(nc, "pack_in qk_done qk_ready att_done relu_ready summed past_ready pen_ready ch") as (
            pack_in, qk_done, qk_ready, att_done, relu_ready, summed, past_ready, pen_ready, chs):
        with nc.Block() as block:
            @block.sync
            def _(sp):
                sp.dma_start(m.wst[:], qkv_packs[0]).then_inc(pack_in, 16)

            @block.gpsimd
            def _(pool):
                nc.gpsimd.memset(m.past[:], 0.0).then_inc(past_ready, 1)
                for t in range(NT - 1):
                    w = P * (t + 1)
                    pool.wait_ge(summed, t + 1)
                    pool.wait_ge(past_ready, t + 1)
                    nc.gpsimd.tensor_tensor(m.past[:, 0:w], m.past[:, 0:w], m.srelu[:, t % 2, 0:w],
                                            ALU.add).then_inc(past_ready, 1)

            @block.tensor
            def _(pe):
                pe.wait_ge(pack_in, 16)
                for j in range(2):
                    for half in range(2):
                        nc.tensor.matmul(m.ps[:, 2 * j + half, :], m.wst[:, j * P:(j + 1) * P],
                                         m.xnT[:, half * HALF:(half + 1) * HALF], start=True,
                                         stop=True).then_inc(qk_done, 1)
                pe.wait_ge(qk_ready, 4)

                def att(t):
                    w = P * (t + 1)
                    if t >= 2:
                        pe.wait_ge(relu_ready, t - 1)
                    for a in range(0, w, HALF):
                        b = min(w, a + HALF)
                        ins = nc.tensor.matmul(m.ps[:, 2 * (t % 2) + a // HALF, 0:b - a], m.qT[0:HD0, t * P:(t + 1) * P],
                                               m.kT[0:HD0, a:b], start=True, stop=True)
                    ins.then_inc(att_done, 1)

                att(0)
                for t in range(NT):
                    w = P * (t + 1)
                    if t + 1 < NT:
                        att(t + 1)
                    pe.wait_ge(relu_ready, t + 1)
                    pe.wait_ge(past_ready, t + 1)
                    if t >= 2:
                        pe.wait_ge(pen_ready, t - 1)
                    for a in range(0, w, HALF):
                        b = min(w, a + HALF)
                        bank = 4 + 2 * (t % 2) + a // HALF
                        nc.tensor.matmul(m.ps[:, bank, 0:b - a], m.before[:], m.srelu[:, t % 2, a:b],
                                         start=True, stop=False)
                        ins = nc.tensor.matmul(m.ps[:, bank, 0:b - a], m.ones[:], m.past[:, a:b],
                                               start=False, stop=True)
                    ins.then_inc(summed, 1)

            @block.vector
            def _(dve):
                for half in range(2):
                    dve.wait_ge(qk_done, half + 1)
                    nc.vector.tensor_scalar(m.qT[:, half * HALF:(half + 1) * HALF], m.ps[:, half, :],
                                            m.wst[:, 3 * P:3 * P + 1], -1.0 / 8, ALU.add, ALU.mult).then_inc(qk_ready, 1)
                for half in range(2):
                    dve.wait_ge(qk_done, half + 3)
                    nc.vector.tensor_scalar(m.kT[:, half * HALF:(half + 1) * HALF], m.ps[:, 2 + half, :],
                                            m.wst[:, 3 * P + 1:3 * P + 2], None, ALU.add).then_inc(qk_ready, 1)
                ch = Chain(dve, chs)

                def relu(t):
                    w = P * (t + 1)
                    dve.wait_ge(att_done, t + 1)
                    if t >= 2:
                        dve.wait_ge(summed, t - 1)
                        dve.wait_ge(past_ready, t)
                    ch.link(nc.vector.tensor_scalar(m.srelu[:, t % 2, 0:w], m.psf[:, 2 * (t % 2) * HALF:2 * (t % 2) * HALF + w],
                                                    -1.0, 0.0, ALU.mult, ALU.max))
                    ch.link(nc.vector.tensor_tensor(m.srelu[:, t % 2, t * P:w], m.srelu[:, t % 2, t * P:w],
                                                    m.below[:], ALU.mult))
                    nc.vector.memset(m.srelu[:, t % 2, 0:1], 0.0).then_inc(relu_ready, 1)

                relu(0)
                for t in range(NT):
                    w = P * (t + 1)
                    if t + 1 < NT:
                        relu(t + 1)
                    dve.wait_ge(summed, t + 1)
                    o = (4 + 2 * (t % 2)) * HALF
                    if t:
                        ch.add(nc.vector.tensor_copy(m.pen[:, t, 0:t * P], m.psf[:, o:o + t * P]))
                    nc.vector.tensor_tensor(m.pen[:, t, t * P:w], m.psf[:, o + t * P:o + w], m.later[:],
                                            ALU.add).then_inc(pen_ready, 1)


def select_stage(nc, m):
    NB = 31

    def joff(t):
        return P * t * (t + 1) // 2

    tiles = list(range(TSEL, NT))
    by_act = tiles[::-2]
    by_dve = [t for t in tiles if t not in by_act]
    with signals(nc, "ch start_ready cand_ready act_counted") as (chs, start_ready, cand_ready, act_counted):
        with nc.Block() as block:
            @block.scalar
            def _(act):
                with act.Fori(0, NB) as it:
                    act.wait_ge(cand_ready, it + 1)
                    for t in by_act:
                        i = t - TSEL
                        nc.scalar.activation(m.junk[:, joff(t):joff(t) + P * (t + 1)], m.pen[:, t, 0:P * (t + 1)], ACT.Sign,
                                             bias=m.candf[:, i:i + 1], scale=-1.0,
                                             accum_out=m.count[:, i:i + 1]).then_inc(act_counted, 1)

            @block.vector
            def _(dve):
                ch = Chain(dve, chs)
                ch.add(nc.vector.memset(m.bitf[:], float(2 ** (NB - 1))))
                ch.add(nc.vector.memset(m.thr[:], 0))
                ch.hold()
                ch.link(nc.vector.tensor_copy(m.biti[:], m.bitf[:]))
                nc.vector.tensor_tensor(m.cand[:], m.thr[:], m.biti[:], ALU.bitwise_or).then_inc(cand_ready, 1)
                base, per = ch.n, len(by_dve) + 4
                with dve.Fori(0, NB) as it:
                    c = Chain(dve, chs, base + it * per)
                    dve.wait_ge(cand_ready, it + 1)
                    for t in by_dve:
                        i = t - TSEL
                        c.add(nc.vector.tensor_scalar(m.junk[:, joff(t):joff(t) + P * (t + 1)], m.pen[:, t, 0:P * (t + 1)],
                                                      m.candf[:, i:i + 1], 0.0, ALU.is_lt, ALU.add,
                                                      accum_out=m.count[:, i:i + 1]))
                    dve.wait_ge(act_counted, (it + 1) * len(by_act))
                    c.hold()
                    c.link(nc.vector.tensor_tensor(m.few[:], m.count[:], m.want[:, 0, :], ALU.is_lt))
                    c.link(nc.vector.tensor_tensor(m.biti[:], m.few[:], m.bitf[:], ALU.mult))
                    c.add(nc.vector.tensor_tensor(m.thr[:], m.thr[:], m.biti[:], ALU.bitwise_or))
                    c.link(nc.vector.tensor_scalar(m.bitf[:], m.bitf[:], 0.5, None, ALU.mult))
                    c2 = Chain(dve, start_ready, it)
                    c2.link(nc.vector.tensor_copy(m.biti[:], m.bitf[:]))
                    nc.vector.tensor_tensor(m.cand[:], m.thr[:], m.biti[:], ALU.bitwise_or).then_inc(cand_ready, 1)
                    assert c.n == per
                ch = Chain(dve, chs, base + NB * per)
                for t in tiles:
                    i = t - TSEL
                    ch.add(nc.vector.tensor_scalar(m.junk[:, joff(t):joff(t) + P * (t + 1)], m.pen[:, t, 0:P * (t + 1)],
                                                   m.thrf[:, i:i + 1], 0.0, ALU.is_le, ALU.add,
                                                   accum_out=m.count[:, i:i + 1]))
                ch.hold()
                ch.link(nc.vector.tensor_tensor(m.biti[:], m.count[:], m.want[:, 1, :], ALU.is_lt))
                ch.link(nc.vector.tensor_tensor(m.thr[:], m.thr[:], m.biti[:], ALU.add))
                for t in tiles:
                    i = t - TSEL
                    w = P * (t + 1)
                    pen, thr = m.pen[:, t, 0:w], m.thrf[:, i:i + 1]
                    same, keep = m.past[:, 0:w], m.srelu[:, 0, 0:w]
                    ch.add(nc.vector.tensor_scalar(keep, pen, thr, 0.0, ALU.is_lt, ALU.add,
                                                   accum_out=m.count[:, i:i + 1]))
                    ch.link(nc.vector.tensor_scalar(same, pen, thr, None, ALU.is_equal))
                    ch.add(nc.vector.tensor_tensor_scan(m.srelu[:, 1, 0:w], bcast(m.ones[:, 0:1], P, w), same, 0.0,
                                                        ALU.mult, ALU.add))
                    ch.link(nc.vector.tensor_tensor(m.need[:, i:i + 1], m.want[:, 1, i:i + 1], m.count[:, i:i + 1],
                                                    ALU.subtract))
                    ch.link(nc.vector.scalar_tensor_tensor(out=same, in0=m.srelu[:, 1, 0:w], scalar=m.need[:, i:i + 1],
                                                           in1=same, op0=ALU.is_le, op1=ALU.mult))
                    ch.link(nc.vector.tensor_tensor(keep, keep, same, ALU.add))
                    ch.link(nc.vector.tensor_tensor(keep[:, t * P:w], keep[:, t * P:w], m.ident[:], ALU.max))
                    ch.link(nc.vector.tensor_scalar(keep, keep, -BIG, BIG, ALU.mult, ALU.add))
                    ch.link(nc.vector.tensor_tensor(pen, pen, keep, ALU.max))




def attention_stage(nc, m, qkv_packs):
    U = 2 * NT
    with signals(nc, "pack_in proj_done proj_ready scores_done shifted probs_ready turned_a turned_b "
                     "evac_a evac_d values_done y_ready yt_done yt_ready ch vproj_ready pack_free") as (
            pack_in, proj_done, proj_ready, scores_done, shifted, probs_ready, turned_a, turned_b,
            evac_a, evac_d, values_done, y_ready, yt_done, yt_ready, chs, vproj_ready, pack_free):
        groups = []
        for u in range(U):
            t = u // 2
            for g0 in range(0, t + 1, 4):
                groups.append((u, g0, min(t + 1, g0 + 4)))
        NG = len(groups)
        of = {u: [g for g in range(NG) if groups[g][0] == u] for u in range(U)}
        act_g = [g for g in range(NG) if g % 2 == 0]
        dve_g = [g for g in range(NG) if g % 2 == 1]
        NA, NDV = len(act_g), len(dve_g)

        def copied(eng, g, it, prev=False):
            if g < 0:
                return
            if g % 2 == 0:
                eng.wait_ge(evac_a, it * NA + act_g.index(g) + 1)
            else:
                eng.wait_ge(evac_d, it * NDV + dve_g.index(g) + 1)

        SB, GB = [0, 2], [4, 5]
        YB, YTB = 6, 7
        with nc.Block() as block:
            @block.sync
            def _(sp):
                sp.dma_start(m.wst[:], qkv_packs[0]).then_inc(pack_in, 16)
                with sp.Fori(1, PAIRS) as it:
                    sp.wait_ge(pack_free, it)
                    sp.dma_start(m.wst[:], qkv_packs[ds(it, 1)].rearrange("o p n -> (o p) n")).then_inc(pack_in, 16)

            @block.tensor
            def _(pe):
                with pe.Fori(0, PAIRS) as it:
                    pe.wait_ge(pack_in, it * 16 + 16)
                    for j in range(2):
                        for half in range(2):
                            nc.tensor.matmul(m.ps[:, 2 * j + half, :], m.wst[:, j * P:(j + 1) * P],
                                             m.xnT[:, half * HALF:(half + 1) * HALF], start=True,
                                             stop=True).then_inc(proj_done, 1)
                    for t in range(NT):
                        ins = nc.tensor.matmul(m.ps[:, 4 + t // 4, (t % 4) * P:(t % 4 + 1) * P],
                                               m.xnT[:, t * P:(t + 1) * P], m.wst[:, 2 * P:3 * P], start=True, stop=True)
                        if t % 4 == 3:
                            ins.then_inc(proj_done, 1)
                    pe.wait_ge(proj_ready, it * 4 + 4)
                    pe.wait_ge(vproj_ready, it * 2 + 2)

                    def scores(u):
                        t, h = u // 2, u % 2
                        w = P * (t + 1)
                        if u >= 2:
                            pe.wait_ge(shifted, it * U + u - 1)
                        for a in range(0, w, HALF):
                            b = min(w, a + HALF)
                            ins = nc.tensor.matmul(m.ps[:, SB[h] + a // HALF, 0:b - a],
                                                   m.qT[h * HD0:(h + 1) * HD0, t * P:(t + 1) * P],
                                                   m.kT[h * HD0:(h + 1) * HD0, a:b], start=True, stop=True)
                        ins.then_inc(scores_done, 1)

                    def turn(u):
                        h = u % 2
                        pe.wait_ge(probs_ready, it * U + u + 1)
                        for g in of[u]:
                            copied(pe, g - 2, it)
                            _, k0, k1 = groups[g]
                            for k in range(k0, k1):
                                ins = nc.tensor.transpose(m.ps[:, GB[g % 2], (k - k0) * P:(k - k0 + 1) * P],
                                                          m.prob[:, h, k * P:(k + 1) * P], m.ident[:])
                            ins.then_inc(turned_a if g % 2 == 0 else turned_b, 1)

                    def values(u):
                        t, h = u // 2, u % 2
                        for g in of[u]:
                            copied(pe, g, it)
                        if u >= 1:
                            pe.wait_ge(y_ready, it * U + u)
                        for k in range(t + 1):
                            ins = nc.tensor.matmul(m.ps[:, YB, 0:HD0], m.pT[:, h, k, :],
                                                   m.v[:, k, h * HD0:(h + 1) * HD0], start=(k == 0), stop=(k == t))
                        ins.then_inc(values_done, 1)

                    def turn_y(t):
                        pe.wait_ge(y_ready, it * U + 2 * t + 2)
                        if t >= 1:
                            pe.wait_ge(yt_ready, it * NT + t)
                        nc.tensor.transpose(m.ps[:, YTB, 0:P], m.y[:, t % 2, :], m.ident[:]).then_inc(yt_done, 1)

                    scores(0)
                    for n in range(1, U + 3):
                        if n < U:
                            scores(n)
                        if n - 1 < U:
                            turn(n - 1)
                        if 0 <= n - 2 < U:
                            values(n - 2)
                        if n >= 4 and n % 2 == 0:
                            turn_y((n - 4) // 2)
                    pe.wait_ge(shifted, it * U + U)
                    pe.wait_ge(yt_ready, it * NT + NT)

            @block.vector
            def _(dve):
                with dve.Fori(0, PAIRS) as it:
                    for half in range(2):
                        dve.wait_ge(proj_done, it * 6 + half + 1)
                        nc.vector.tensor_scalar(m.qT[:, half * HALF:(half + 1) * HALF], m.ps[:, half, :],
                                                m.wst[:, 3 * P:3 * P + 1], -1.0 / 8, ALU.add,
                                                ALU.mult).then_inc(proj_ready, 1)
                    for half in range(2):
                        dve.wait_ge(proj_done, it * 6 + half + 3)
                        nc.vector.tensor_scalar(m.kT[:, half * HALF:(half + 1) * HALF], m.ps[:, 2 + half, :],
                                                m.wst[:, 3 * P + 1:3 * P + 2], None, ALU.add).then_inc(proj_ready, 1)
                    c = Chain(dve, chs, it * U)

                    def shift(u):
                        t, h = u // 2, u % 2
                        w = P * (t + 1)
                        if u >= 2:
                            for g in of[u - 2]:
                                dve.wait_ge(turned_a if g % 2 == 0 else turned_b,
                                            it * (NA if g % 2 == 0 else NDV) + (act_g if g % 2 == 0 else dve_g).index(g) + 1)
                        count = dve.to_reg(it * U + u + 1)
                        dve.wait_ge(pack_in, 16)
                        dve.wait_ge(scores_done, count)
                        nc.vector.tensor_tensor_reduce(m.prob[:, h, 0:w], m.psf[:, SB[h] * HALF:SB[h] * HALF + w],
                                                       m.pen[:, t, 0:w], 1.0, 3.0e38, ALU.add, ALU.min,
                                                       m.nmax[:, h:h + 1]).then_inc(shifted, 1)

                    def evac(u):
                        for g in of[u]:
                            if g % 2 == 1:
                                _, k0, k1 = groups[g]
                                dve.wait_ge(turned_b, it * NDV + dve_g.index(g) + 1)
                                if u >= 2:
                                    dve.wait_ge(values_done, it * U + u - 1)
                                nc.vector.tensor_copy(m.pT[:, u % 2, k0:k1, :].rearrange("p k q -> p (k q)"),
                                                      m.ps[:, GB[1], 0:(k1 - k0) * P]).then_inc(evac_d, 1)

                    def finish(u):
                        t, h = u // 2, u % 2
                        dve.wait_ge(values_done, it * U + u + 1)
                        c.link(nc.vector.reciprocal(m.rsum[:, h:h + 1], m.esum[:, u % 4:u % 4 + 1]))
                        if t >= 2:
                            dve.wait_ge(yt_done, it * NT + t - 1)
                        nc.vector.tensor_scalar(m.y[:, t % 2, h * HD0:(h + 1) * HD0], m.ps[:, YB, 0:HD0],
                                                m.rsum[:, h:h + 1], None, ALU.mult).then_inc(y_ready, 1)

                    shift(0)
                    for n in range(1, U + 3):
                        if n < U:
                            shift(n)
                        if n - 1 < U:
                            evac(n - 1)
                        if 0 <= n - 2 < U:
                            finish(n - 2)
                    assert c.n == U

            @block.scalar
            def _(act):
                with act.Fori(0, PAIRS) as it:
                    for half in range(2):
                        act.wait_ge(proj_done, it * 6 + 5 + half)
                        nc.scalar.activation(m.v[:, 4 * half:4 * half + 4, :].rearrange("p t c -> p (t c)"),
                                             m.ps[:, 4 + half, :], ACT.Copy).then_inc(vproj_ready, 1)

                    def exp(u):
                        t, h = u // 2, u % 2
                        w = P * (t + 1)
                        act.wait_ge(shifted, it * U + u + 1)
                        if u >= 4:
                            act.wait_ge(y_ready, it * U + u - 3)
                        nc.scalar.activation(m.prob[:, h, 0:w], m.prob[:, h, 0:w], ACT.Exp, bias=m.nmax[:, h:h + 1],
                                             scale=-1.0, accum_out=m.esum[:, u % 4:u % 4 + 1]).then_inc(probs_ready, 1)

                    def evac(u):
                        for g in of[u]:
                            if g % 2 == 0:
                                _, k0, k1 = groups[g]
                                act.wait_ge(turned_a, it * NA + act_g.index(g) + 1)
                                if u >= 2:
                                    act.wait_ge(values_done, it * U + u - 1)
                                nc.scalar.activation(m.pT[:, u % 2, k0:k1, :].rearrange("p k q -> p (k q)"),
                                                     m.ps[:, GB[0], 0:(k1 - k0) * P], ACT.Copy).then_inc(evac_a, 1)

                    def out_y(t):
                        act.wait_ge(yt_done, it * NT + t + 1)
                        ins = nc.scalar.activation(m.yT[:, ds(it, 1), t * P:(t + 1) * P].rearrange("p o q -> p (o q)"),
                                                   m.ps[:, YTB, 0:P], ACT.Identity,
                                                   bias=m.wst[:, 3 * P + 2:3 * P + 3])
                        ins.then_inc(yt_ready, 1)

                    exp(0)
                    for n in range(1, U + 3):
                        if n < U:
                            exp(n)
                        if n - 1 < U:
                            evac(n - 1)
                        if n >= 4 and n % 2 == 0:
                            out_y((n - 4) // 2)
                    act.wait_ge(yt_ready, it * NT + NT)
                    act.sem_inc(pack_free, 1)


def project_stage(nc, m):
    with signals(nc, "proj_done sum_ready turned added") as (proj_done, sum_ready, turned, added):
        with nc.Block() as block:
            @block.tensor
            def _(pe):
                for half in range(2):
                    for p in range(PAIRS):
                        ins = nc.tensor.matmul(m.ps[:, half, :], m.wprojT[:, p, :],
                                               m.yT[:, p, half * HALF:(half + 1) * HALF],
                                               start=(p == 0), stop=(p == PAIRS - 1))
                    ins.then_inc(proj_done, 1)
                for t in range(NT):
                    pe.wait_ge(sum_ready, t // 4 + 1)
                    nc.tensor.transpose(m.ps[:, 2 + t // 4, (t % 4) * P:(t % 4 + 1) * P],
                                        m.ffnT[:, t * P:(t + 1) * P], m.ident[:]).then_inc(turned, 1)

            @block.vector
            def _(dve):
                for half in range(2):
                    dve.wait_ge(proj_done, half + 1)
                    f = m.ffnT[:, half * HALF:(half + 1) * HALF]
                    nc.vector.scalar_tensor_tensor(out=f, in0=m.ps[:, half, :], scalar=m.bproj[:, 0:1], in1=f,
                                                   op0=ALU.add, op1=ALU.add).then_inc(sum_ready, 1)
                for half in range(2):
                    dve.wait_ge(turned, 4 * half + 4)
                    xs = m.x[:, 4 * half:4 * half + 4, :].rearrange("p t c -> p (t c)")
                    nc.vector.tensor_tensor(xs, m.ps[:, 2 + half, :], xs, ALU.add).then_inc(added, 1)




def delta_prepare_stage(nc, m):
    with signals(nc, "sq_ready ss_ready root_ready xr_ready proj_done xv_ready beta_ready gate_ready xr_turned "
                     "wk_ready abs_ready e_ready decay_ready dec_done decE_done dec_ready decE_ready decT_done "
                     "decT_ready exp_ready conv_ready silu_ready diff_ready rest_ready vb_ready wkbd_ready "
                     "kd_ready rk_ready turned evac_done pad_ready ch") as (
            sq_ready, ss_ready, root_ready, xr_ready, proj_done, xv_ready, beta_ready, gate_ready, xr_turned,
            wk_ready, abs_ready, e_ready, decay_ready, dec_done, decE_done, dec_ready, decE_ready, decT_done,
            decT_ready, exp_ready, conv_ready, silu_ready, diff_ready, rest_ready, vb_ready, wkbd_ready,
            kd_ready, rk_ready, turned, evac_done, pad_ready, chs):
        halves = [(h, slice(h * HALF, (h + 1) * HALF)) for h in range(2)]
        NH = NT * H1
        with nc.Block() as block:
            @block.gpsimd
            def _(pool):
                nc.gpsimd.memset(m.wk[:, 0:1], 0.0).then_inc(pad_ready, 1)
                nc.gpsimd.memset(m.xv[:, 0:3], 0.0).then_inc(pad_ready, 1)
                pool.wait_ge(rk_ready, 1)
                pool.wait_ge(exp_ready, 2)
                nc.gpsimd.tensor_tensor(m.rkd, m.rk, m.grow, ALU.mult).then_inc(rk_ready, 1)
                pool.wait_ge(rest_ready, 1)
                nc.gpsimd.tensor_tensor(m.kdT, m.wk[:, 0:T], m.resto, ALU.mult).then_inc(kd_ready, 1)

            @block.tensor
            def _(pe):
                for h, s in halves:
                    nc.tensor.matmul(m.ps[:, h, :], m.wvT[:], m.xnT[:, s], start=True, stop=True).then_inc(proj_done, 1)
                for h, s in halves:
                    nc.tensor.matmul(m.ps[:, 2 + h, :], m.wbT16[:], m.xnT[:, s], start=True,
                                     stop=True).then_inc(proj_done, 1)
                for t in range(NT):
                    ins = nc.tensor.matmul(m.ps[:, 4, t * H1:(t + 1) * H1], m.xnT[:, t * P:(t + 1) * P], m.waT[:],
                                           start=True, stop=True)
                ins.then_inc(proj_done, 1)
                for t in range(NT):
                    ins = nc.tensor.matmul(m.ps[:, 5 + t // 4, (t % 4) * P:(t % 4 + 1) * P], m.xnT[:, t * P:(t + 1) * P],
                                           m.wgT[:], start=True, stop=True)
                    if t % 4 == 3:
                        ins.then_inc(proj_done, 1)
                for t in range(NT):
                    pe.wait_ge(xr_ready, t // 4 + 1)
                    if t == 4:
                        pe.wait_ge(xv_ready, 1)
                    ins = nc.tensor.transpose(m.ps[:, 7 if t < 4 else 0, (t % 4) * P:(t % 4 + 1) * P], m.xr[:, t, :],
                                              m.ident[:])
                    if t % 4 == 3:
                        ins.then_inc(xr_turned, 1)
                pe.wait_ge(decay_ready, 1)
                nc.tensor.matmul(m.ps[:, 4, 0:NH], m.chunk_upto[:], m.decay[:], start=True, stop=True).then_inc(dec_done, 1)
                pe.wait_ge(gate_ready, 2)
                for t in range(NT):
                    ins = nc.tensor.matmul(m.ps[:, 5 + t // 4, (t % 4) * P:(t % 4 + 1) * P], m.decay16[:, t, :],
                                           m.chunk_upto[:], start=True, stop=True)
                    if t % 4 == 3:
                        ins.then_inc(decE_done, 1)
                pe.wait_ge(dec_ready, 1)
                pe.wait_ge(beta_ready, 2)
                for t in range(NT):
                    ins = nc.tensor.transpose(m.ps[0:H1, 2 + t // 4, (t % 4) * P:(t % 4 + 1) * P],
                                              m.dec[:, t * H1:(t + 1) * H1], m.ident[:])
                ins.then_inc(decT_done, 1)
                pe.wait_ge(wk_ready, 2)
                pe.wait_ge(xv_ready, 2)
                pe.wait_ge(decT_ready, 2)
                pe.wait_ge(exp_ready, 2)
                for src, ready, bank in ((m.vb, vb_ready, 0), (m.wkbd, wkbd_ready, 2), (m.kdT, kd_ready, 5)):
                    pe.wait_ge(ready, 1)
                    for t in range(NT):
                        ins = nc.tensor.transpose(m.ps[:, bank + t // 4, (t % 4) * P:(t % 4 + 1) * P],
                                                  src[:, t * P:(t + 1) * P], m.ident[:])
                        if t % 4 == 3:
                            ins.then_inc(turned, 1)

            @block.scalar
            def _(act):
                nc.scalar.activation(m.sq, m.xn[:].rearrange("p t c -> p (t c)"), ACT.Square).then_inc(sq_ready, 1)
                act.wait_ge(ss_ready, 1)
                nc.scalar.activation(m.rn[:], m.rn[:], ACT.Sqrt).then_inc(root_ready, 1)
                for h, s in halves:
                    act.wait_ge(proj_done, 1 + h)
                    nc.scalar.activation(m.xv[:, 3 + h * HALF:3 + (h + 1) * HALF], m.ps[:, h, :],
                                         ACT.Copy).then_inc(xv_ready, 1)
                for h, s in halves:
                    act.wait_ge(proj_done, 3 + h)
                    nc.scalar.activation(m.beta[:, s], m.ps[:, 2 + h, :], ACT.Sigmoid).then_inc(beta_ready, 1)
                for h, s in halves:
                    act.wait_ge(proj_done, 6 + h)
                    nc.scalar.activation(m.gate[:, 4 * h:4 * h + 4, :].rearrange("p t c -> p (t c)"),
                                         m.ps[:, 5 + h, :], ACT.Silu).then_inc(gate_ready, 1)
                for h, s in halves:
                    act.wait_ge(xr_turned, 1 + h)
                    nc.scalar.activation(m.wk[:, 1 + h * HALF:1 + (h + 1) * HALF] if h == 0 else
                                         m.wk[:, 1 + HALF:1 + T], m.ps[:, 7 if h == 0 else 0, :],
                                         ACT.Copy).then_inc(wk_ready, 1)
                act.wait_ge(conv_ready, 1)
                nc.scalar.activation(m.vb, m.vb, ACT.Silu).then_inc(silu_ready, 1)
                act.wait_ge(abs_ready, 1)
                nc.scalar.activation(m.e64[:], m.e64[:], ACT.Exp, scale=-1.0).then_inc(e_ready, 1)
                for h, s in halves:
                    act.wait_ge(decE_done, 1 + h)
                    nc.scalar.activation(m.decE[:, s], m.ps[:, 5 + h, :], ACT.Copy).then_inc(decE_ready, 1)
                for h, s in halves:
                    nc.scalar.activation(m.grow[:, s], m.ps[:, 5 + h, :], ACT.Exp).then_inc(exp_ready, 1)
                act.wait_ge(decE_ready, 2)
                nc.scalar.activation(m.sdecay[:], m.decE.rearrange("p (n c) -> p n c", c=C1)[:, :, C1 - 1],
                                     ACT.Exp).then_inc(exp_ready, 1)
                act.wait_ge(decT_done, 1)
                for h, s in halves:
                    nc.scalar.activation(m.decT[:, s], m.ps[0:H1, 2 + h, :], ACT.Copy).then_inc(decT_ready, 1)
                act.wait_ge(diff_ready, 1)
                nc.scalar.activation(m.resto, m.resto, ACT.Exp).then_inc(rest_ready, 1)
                for h in range(2):
                    act.wait_ge(turned, 5 + h)
                    nc.scalar.activation(m.kd[:, 4 * h:4 * h + 4, :].rearrange("p t c -> p (t c)"), m.ps[:, 5 + h, :],
                                         ACT.Copy).then_inc(evac_done, 1)

            @block.vector
            def _(dve):
                ch = Chain(dve, chs)
                dve.wait_ge(sq_ready, 1)
                ch.link(nc.vector.tensor_reduce(m.rn[:], m.sq.rearrange("p (n k) -> p n k", k=K1), AX, ALU.add))
                nc.vector.tensor_scalar(m.rn[:], m.rn[:], EPS_L2, None, ALU.add).then_inc(ss_ready, 1)
                dve.wait_ge(root_ready, 1)
                ch.link(nc.vector.reciprocal(m.rn[:], m.rn[:]))
                for h in range(2):
                    v = lambda z: z[:, 4 * h:4 * h + 4, :].rearrange("p t (g k) -> p (t g) k", k=K1)
                    nc.vector.tensor_tensor(v(m.xr), v(m.xn), bcast(m.rn[:, h * NH // 2:(h + 1) * NH // 2].unsqueeze(2),
                                                                   P, NH // 2, K1), ALU.mult).then_inc(xr_ready, 1)
                dve.wait_ge(proj_done, 5)
                ch.link(nc.vector.tensor_tensor(m.z64[:].rearrange("p (t h) -> p t h", h=H1),
                                                m.ps[:, 4, 0:NH].rearrange("p (t h) -> p t h", h=H1),
                                                bcast(m.dtb[:].unsqueeze(1), P, NT, H1), ALU.add))
                nc.vector.scalar_tensor_tensor(out=m.e64[:], in0=m.z64[:], scalar=-1.0, in1=m.z64[:], op0=ALU.mult,
                                               op1=ALU.max).then_inc(abs_ready, 1)
                dve.wait_ge(xv_ready, 2)
                dve.wait_ge(pad_ready, 2)
                ch.link(nc.vector.tensor_scalar(m.vb, m.xv[:, 0:T], m.convw[:, 0:1], m.convw[:, 4:5], ALU.mult, ALU.add))
                for j in range(1, 4):
                    ins = nc.vector.scalar_tensor_tensor(out=m.vb, in0=m.xv[:, j:j + T], scalar=m.convw[:, j:j + 1],
                                                         in1=m.vb, op0=ALU.mult, op1=ALU.add)
                    if j < 3:
                        ch.link(ins)
                    else:
                        ins.then_inc(conv_ready, 1)
                dve.wait_ge(e_ready, 1)
                e, r, r2, q = m.e64[:], m.r64[:], m.rr64[:], m.q64[:]
                ch.link(nc.vector.tensor_scalar(r, e, 2.0, None, ALU.add))
                ch.link(nc.vector.reciprocal(r, r))
                ch.link(nc.vector.tensor_tensor(r, r, e, ALU.mult))
                ch.link(nc.vector.tensor_tensor(r2, r, r, ALU.mult))
                ch.link(nc.vector.tensor_scalar(q, r2, 1.0 / 17, None, ALU.mult))
                for k in range(15, 1, -2):
                    ch.link(nc.vector.scalar_tensor_tensor(out=q, in0=q, scalar=1.0 / k, in1=r2, op0=ALU.add, op1=ALU.mult))
                ch.link(nc.vector.scalar_tensor_tensor(out=q, in0=q, scalar=1.0, in1=r, op0=ALU.add, op1=ALU.mult))
                ch.link(nc.vector.tensor_scalar(m.z64[:], m.z64[:], 0.0, None, ALU.max))
                ch.link(nc.vector.scalar_tensor_tensor(out=q, in0=q, scalar=2.0, in1=m.z64[:], op0=ALU.mult, op1=ALU.add))
                ch.link(nc.vector.tensor_tensor(m.decay[:].rearrange("p (t h) -> p t h", h=H1),
                                                q.rearrange("p (t h) -> p t h", h=H1),
                                                bcast(m.nega[:].unsqueeze(1), P, NT, H1), ALU.mult))
                nc.vector.tensor_copy(m.decay16[:].rearrange("p t (h k) -> p (t h) k", k=K1),
                                      bcast(m.decay[:].unsqueeze(2), P, NH, K1)).then_inc(decay_ready, 1)
                dve.wait_ge(dec_done, 1)
                nc.vector.tensor_copy(m.dec[:], m.ps[:, 4, 0:NH]).then_inc(dec_ready, 1)
                dve.wait_ge(wk_ready, 2)
                nc.vector.tensor_scalar(m.rk, m.wk[:, 1:1 + T], 1.0 / K1 ** 0.5, None, ALU.mult).then_inc(rk_ready, 1)
                dve.wait_ge(beta_ready, 2)
                ch.link(nc.vector.tensor_tensor(m.wkb, m.wk[:, 0:T], m.beta, ALU.mult))
                dve.wait_ge(silu_ready, 1)
                nc.vector.tensor_tensor(m.vb, m.vb, m.beta, ALU.mult).then_inc(vb_ready, 1)
                dve.wait_ge(exp_ready, 2)
                nc.vector.tensor_tensor(m.wkbd, m.wkb, m.grow, ALU.mult).then_inc(wkbd_ready, 1)
                dve.wait_ge(decE_ready, 2)
                dv = m.decE.rearrange("p (n c) -> p n c", c=C1)
                ch.link(nc.vector.tensor_tensor(m.resto.rearrange("p (n c) -> p n c", c=C1),
                                                bcast(dv[:, :, C1 - 1:C1], P, NC1, C1), dv, ALU.subtract))
                nc.vector.tensor_scalar(m.resto, m.resto, 0.0, None, ALU.min).then_inc(diff_ready, 1)
                for i, off in ((0, 0), (1, 0), (2, K1), (3, K1)):
                    dve.wait_ge(turned, i + 1)
                    h = i % 2
                    for t in range(4):
                        nc.vector.tensor_copy(m.rhs[:, 4 * h + t, :, off:off + K1],
                                              m.ps[:, (0 if off == 0 else 2) + h, t * P:(t + 1) * P].rearrange(
                                                  "p (g k) -> p g k", k=K1)).then_inc(evac_done, 1)


def delta_stage(nc, m):
    LV = [2, 4, 8, 16]
    G = 4
    with signals(nc, "staged state_ready dec_done gram_done diff_ready lt_ready lmask_ready nt_ready "
                     "xt_ready x_turned x_ready y_done ym_ready z_done x_next u_done u_ready ntm_ready w_done w_ready "
                     "v2_done solved wt_done wt_ready read_done vnew_ready o_ready upd_done s_ready oi_done out_ready ch"
                 ) as (
            staged, state_ready, dec_done, gram_done, diff_ready, lt_ready, lmask_ready, nt_ready,
            xt_ready, x_turned, x_ready, y_done, ym_ready, z_done, x_next, u_done, u_ready, ntm_ready, w_done, w_ready,
            v2_done, solved, wt_done, wt_ready, read_done, vnew_ready, o_ready, upd_done, s_ready, oi_done, out_ready,
            chs):
        def heads(buf, g):
            return buf[:, g * G:(g + 1) * G, :]

        def bank(k, g):
            return m.ps[:, 2 * k + g, :].rearrange("p (h c) -> p h c", h=G)

        def over_heads(mask):
            return bcast(mask.unsqueeze(1), P, G, P)

        def tile(buf, it):
            return buf[:, ds(it * P, P)]

        with nc.Block() as block:
            @block.gpsimd
            def _(pool):
                nc.gpsimd.memset(m.state[:], 0.0).then_inc(state_ready, 1)
                with pool.Fori(0, NT) as it:
                    nc.gpsimd.tensor_copy(m.wk_t[:], tile(m.wk[:, 0:T], it)).then_inc(staged, 1)
                    nc.gpsimd.tensor_tensor(m.wkb_h[:], bcast(tile(m.wkb, it).unsqueeze(1), P, H1, P),
                                            bcast(m.hmask[:].unsqueeze(2), P, H1, P), ALU.mult).then_inc(staged, 1)
                    nc.gpsimd.tensor_tensor(m.rk_h[:], bcast(tile(m.rk, it).unsqueeze(1), P, H1, P),
                                            bcast(m.hmask[:].unsqueeze(2), P, H1, P), ALU.mult).then_inc(staged, 1)
                    nc.gpsimd.tensor_copy(m.rkd_t[:], tile(m.rkd, it)).then_inc(staged, 1)
                    nc.gpsimd.tensor_copy(m.kd_t[:], m.kd[:, ds(it, 1), :].rearrange("p o c -> p (o c)")).then_inc(staged, 1)
                    nc.gpsimd.tensor_copy(m.sd_t[:], m.sdecay[:, ds(it * 2, 2)]).then_inc(staged, 1)
                    for g in range(2):
                        pool.wait_ge(lt_ready, it * 2 + g + 1)
                        nc.gpsimd.tensor_tensor(heads(m.lts, g), heads(m.lt, g), over_heads(m.strictT[:]),
                                                ALU.mult).then_inc(lmask_ready, 1)
                        nc.gpsimd.tensor_tensor(heads(m.lti, g), heads(m.lt, g), over_heads(m.chunk_upto[:]),
                                                ALU.mult).then_inc(lmask_ready, 1)
                    for g in range(2):
                        pool.wait_ge(nt_ready, it * 2 + g + 1)
                        nc.gpsimd.tensor_tensor(heads(m.ntm, g), heads(m.nt, g), over_heads(m.levT[:, 1, :]),
                                                ALU.mult).then_inc(ntm_ready, 1)
                    pool.wait_ge(out_ready, it + 1)

            @block.tensor
            def _(pe):
                pe.wait_ge(state_ready, 1)
                with pe.Fori(0, NT) as it:
                    def four(k, g, lhs, rhs, n=P, col=P):
                        for h in range(G):
                            ins = nc.tensor.matmul(m.ps[:, 2 * k + g, h * col:h * col + n], lhs(g * G + h), rhs(g * G + h),
                                                   start=True, stop=True)
                        return ins

                    for g in range(2):
                        for h in range(G):
                            ins = nc.tensor.matmul(m.ps[:, g, h * P:(h + 1) * P], m.sel8[:, g * G + h, :],
                                                   m.decT[:, ds(it * P, P)], start=True, stop=True)
                        ins.then_inc(dec_done, 1)
                    pe.wait_ge(staged, it * 6 + 3)
                    for g in range(2):
                        nc.tensor.matmul(m.ps[:, 2 + g, :], m.wk_t[:],
                                         heads(m.wkb_h, g).rearrange("p h c -> p (h c)"), start=True, stop=True)
                        nc.tensor.matmul(m.ps[:, 4 + g, :], m.wk_t[:],
                                         heads(m.rk_h, g).rearrange("p h c -> p (h c)"), start=True,
                                         stop=True).then_inc(gram_done, 1)
                    for g in range(2):
                        pe.wait_ge(xt_ready, it * 2 + g + 1)
                        for h in range(G):
                            ins = nc.tensor.transpose(m.ps[:, g, h * P:(h + 1) * P], m.xt[:, g * G + h, :], m.ident[:])
                        ins.then_inc(x_turned, 1)
                    for l in range(len(LV)):
                        for g in range(2):
                            if l == 0:
                                pe.wait_ge(x_ready, it * 2 + g + 1)
                            else:
                                pe.wait_ge(x_next, it * 8 + (l - 1) * 2 + g + 1)
                            four(1, g, lambda h: m.nt[:, h, :], lambda h: m.xi[:, h, :]).then_inc(y_done, 1)
                        for g in range(2):
                            pe.wait_ge(ym_ready, it * 8 + l * 2 + g + 1)
                            if l < len(LV) - 1:
                                four(2, g, lambda h: m.xt[:, h, :], lambda h: m.ym[:, h, :])
                            four(3, g, lambda h: m.ym[:, h, :], lambda h: m.xt[:, h, :]).then_inc(z_done, 1)
                    for g in range(2):
                        pe.wait_ge(x_next, it * 8 + 6 + g + 1)
                        four(0, g, lambda h: m.xt[:, h, :],
                             lambda h: m.rhs[:, ds(it, 1), h, :].rearrange("p o k -> p (o k)"), 2 * K1,
                             2 * K1).then_inc(u_done, 1)
                    for g in range(2):
                        pe.wait_ge(u_ready, it * 2 + g + 1)
                        pe.wait_ge(ntm_ready, it * 2 + g + 1)
                        four(1, g, lambda h: m.ntm[:, h, :], lambda h: m.u[:, h, :], 2 * K1, 2 * K1).then_inc(w_done, 1)
                    for g in range(2):
                        pe.wait_ge(w_ready, it * 2 + g + 1)
                        four(2, g, lambda h: m.xt[:, h, :], lambda h: m.w[:, h, :], 2 * K1, 2 * K1).then_inc(v2_done, 1)
                    pe.wait_ge(solved, it * 2 + 2)
                    nc.tensor.transpose(m.ps[:, 0, 0:P], m.wsol[:], m.ident[:]).then_inc(wt_done, 1)
                    pe.wait_ge(wt_ready, it + 1)
                    pe.wait_ge(staged, it * 6 + 6)
                    for c in range(2):
                        if c:
                            pe.wait_ge(s_ready, it * 2 + c)
                            pe.wait_ge(o_ready, it * 2 + c)
                        nc.tensor.matmul(m.ps[:, 2, 0:P], m.wcT[:], m.state[:], start=True, stop=True).then_inc(read_done, 1)
                        nc.tensor.matmul(m.ps[:, 4, 0:P], m.rkd_t[:], m.state[:], start=True, stop=True).then_inc(read_done, 1)
                        pe.wait_ge(vnew_ready, it * 2 + c + 1)
                        nc.tensor.matmul(m.ps[:, 6, 0:P], m.kd_t[c * C1:(c + 1) * C1, :],
                                         m.vnew[c * C1:(c + 1) * C1, :], start=True, stop=True).then_inc(upd_done, 1)
                    for h in range(H1):
                        ins = nc.tensor.matmul(m.ps[:, 7, h * K1:(h + 1) * K1], m.at[:, h, :],
                                               m.vnew[:, h * K1:(h + 1) * K1], start=True, stop=True)
                    ins.then_inc(oi_done, 1)
                    pe.wait_ge(s_ready, it * 2 + 2)
                    pe.wait_ge(out_ready, it + 1)

            @block.scalar
            def _(act):
                with act.Fori(0, NT) as it:
                    for g in range(2):
                        act.wait_ge(diff_ready, it * 2 + g + 1)
                        nc.scalar.activation(heads(m.lt, g), heads(m.lt, g), ACT.Exp).then_inc(lt_ready, 1)
                    for g in range(2):
                        act.wait_ge(x_turned, it * 2 + g + 1)
                        nc.scalar.activation(heads(m.xi, g), bank(0, g), ACT.Copy).then_inc(x_ready, 1)
                    for g in range(2):
                        act.wait_ge(u_done, it * 2 + g + 1)
                        nc.scalar.activation(heads(m.u, g).rearrange("p h k -> p (h k)"), m.ps[:, g, 0:G * 2 * K1],
                                             ACT.Copy).then_inc(u_ready, 1)
                    for g in range(2):
                        act.wait_ge(w_done, it * 2 + g + 1)
                        nc.scalar.activation(heads(m.w, g).rearrange("p h k -> p (h k)"), m.ps[:, 2 + g, 0:G * 2 * K1],
                                             ACT.Copy).then_inc(w_ready, 1)
                    act.wait_ge(wt_done, it + 1)
                    nc.scalar.activation(m.wcT[:], m.ps[:, 0, 0:P], ACT.Copy).then_inc(wt_ready, 1)
                    for c in range(2):
                        r = slice(c * C1, (c + 1) * C1)
                        act.wait_ge(read_done, it * 4 + 2 * c + 2)
                        nc.scalar.activation(m.ointer[r, :], m.ps[r, 4, 0:P], ACT.Copy).then_inc(o_ready, 1)

            @block.vector
            def _(dve):
                NCH = 14 + 2 + 2 - 2
                with dve.Fori(0, NT) as it:
                    c_ = Chain(dve, chs, it * 6)
                    for g in range(2):
                        dve.wait_ge(dec_done, it * 2 + g + 1)
                        c_.link(nc.vector.tensor_tensor(heads(m.lt, g), bank(0, g),
                                                        bcast(m.dec[:, ds(it * H1 + g * G, G)].unsqueeze(2), P, G, P),
                                                        ALU.subtract))
                        lt = heads(m.lt, g).rearrange("p h c -> p (h c)")
                        nc.vector.tensor_scalar(lt, lt, 0.0, None, ALU.min).then_inc(diff_ready, 1)
                    for g in range(2):
                        dve.wait_ge(gram_done, it * 2 + g + 1)
                        dve.wait_ge(lmask_ready, it * 4 + 2 * g + 2)
                        c_.add(nc.vector.tensor_tensor(heads(m.at, g), bank(2, g), heads(m.lti, g), ALU.mult))
                        nc.vector.tensor_tensor(heads(m.nt, g), bank(1, g), heads(m.lts, g), ALU.mult).then_inc(nt_ready, 1)
                        dve.wait_ge(nt_ready, it * 2 + g + 1)
                        c_.link(nc.vector.tensor_tensor(heads(m.xt, g), heads(m.nt, g), over_heads(m.levT[:, 0, :]), ALU.mult))
                        nc.vector.tensor_tensor(heads(m.xt, g), over_heads(m.ident[:]), heads(m.xt, g),
                                                ALU.subtract).then_inc(xt_ready, 1)
                    assert c_.n == 6
                    for l in range(len(LV)):
                        for g in range(2):
                            dve.wait_ge(y_done, it * 8 + l * 2 + g + 1)
                            nc.vector.tensor_tensor(heads(m.ym, g), bank(1, g), over_heads(m.lev[:, l, :]),
                                                    ALU.mult).then_inc(ym_ready, 1)
                        for g in range(2):
                            dve.wait_ge(z_done, it * 8 + l * 2 + g + 1)
                            if l < len(LV) - 1:
                                nc.vector.tensor_tensor(heads(m.xi, g), heads(m.xi, g), bank(2, g), ALU.subtract)
                            nc.vector.tensor_tensor(heads(m.xt, g), heads(m.xt, g), bank(3, g),
                                                    ALU.subtract).then_inc(x_next, 1)
                    for g in range(2):
                        dve.wait_ge(v2_done, it * 2 + g + 1)
                        o = m.ps[:, 4 + g, 0:G * 2 * K1].rearrange("p (h k) -> p h k", k=2 * K1)
                        nc.vector.tensor_tensor(m.vsol[:].rearrange("p (h k) -> p h k", k=K1)[:, g * G:(g + 1) * G, :],
                                                heads(m.u, g)[:, :, 0:K1], o[:, :, 0:K1], ALU.subtract)
                        nc.vector.tensor_tensor(m.wsol[:].rearrange("p (h k) -> p h k", k=K1)[:, g * G:(g + 1) * G, :],
                                                heads(m.u, g)[:, :, K1:2 * K1], o[:, :, K1:2 * K1],
                                                ALU.subtract).then_inc(solved, 1)
                    dve.wait_ge(solved, it * 2 + 2)
                    for c in range(2):
                        r = slice(c * C1, (c + 1) * C1)
                        dve.wait_ge(read_done, it * 4 + 2 * c + 1)
                        nc.vector.tensor_tensor(m.vnew[r, :], m.vsol[r, :], m.ps[r, 2, 0:P], ALU.subtract).then_inc(vnew_ready, 1)
                        dve.wait_ge(upd_done, it * 2 + c + 1)
                        nc.vector.tensor_tensor(m.supd[:, c, :], m.ps[:, 6, 0:P], m.bdiag[:], ALU.mult).then_inc(state_ready, 1)
                        dve.wait_ge(state_ready, it * 2 + c + 2)
                        nc.vector.scalar_tensor_tensor(out=m.state[:], in0=m.state[:], scalar=m.sd_t[:, c:c + 1],
                                                       in1=m.supd[:, c, :], op0=ALU.mult, op1=ALU.add).then_inc(s_ready, 1)
                    dve.wait_ge(oi_done, it + 1)
                    dve.wait_ge(o_ready, it * 2 + 2)
                    nc.vector.tensor_tensor(m.o[:, ds(it, 1), :].rearrange("p o c -> p (o c)"), m.ointer[:],
                                            m.ps[:, 7, 0:P], ALU.add).then_inc(out_ready, 1)


def delta_out_stage(nc, m):
    NH = NT * H1
    with signals(nc, "sq_ready ms_ready root_ready o_ready turned oT_ready out_done added ch") as (
            sq_ready, ms_ready, root_ready, o_ready, turned, oT_ready, out_done, added, chs):
        with nc.Block() as block:
            @block.scalar
            def _(act):
                nc.scalar.activation(m.sq, m.o.rearrange("p t c -> p (t c)"), ACT.Square).then_inc(sq_ready, 1)
                act.wait_ge(ms_ready, 1)
                nc.scalar.activation(m.rn[:], m.rn[:], ACT.Sqrt).then_inc(root_ready, 1)
                for h in range(2):
                    act.wait_ge(turned, h + 1)
                    nc.scalar.activation(m.kdT[:, h * HALF:(h + 1) * HALF], m.ps[:, h, :], ACT.Copy).then_inc(oT_ready, 1)

            @block.vector
            def _(dve):
                ch = Chain(dve, chs)
                dve.wait_ge(sq_ready, 1)
                ch.link(nc.vector.tensor_reduce(m.rn[:], m.sq.rearrange("p (n k) -> p n k", k=K1), AX, ALU.add))
                nc.vector.tensor_scalar(m.rn[:], m.rn[:], 1.0 / K1, EPS_RMS, ALU.mult, ALU.add).then_inc(ms_ready, 1)
                dve.wait_ge(root_ready, 1)
                ch.link(nc.vector.reciprocal(m.rn[:], m.rn[:]))
                ov = m.o.rearrange("p t (h k) -> p (t h) k", k=K1)
                ch.link(nc.vector.tensor_tensor(ov, ov, bcast(m.rn[:].unsqueeze(2), P, NH, K1), ALU.mult))
                ch.link(nc.vector.tensor_tensor(ov, ov, bcast(m.normw[:].unsqueeze(1), P, NH, K1), ALU.mult))
                nc.vector.tensor_tensor(m.o, m.o, m.gate, ALU.mult).then_inc(o_ready, 1)
                for h in range(2):
                    dve.wait_ge(out_done, h + 1)
                    xs = m.x[:, 4 * h:4 * h + 4, :].rearrange("p t c -> p (t c)")
                    nc.vector.tensor_tensor(xs, m.ps[:, 2 + h, :], xs, ALU.add).then_inc(added, 1)

            @block.tensor
            def _(pe):
                pe.wait_ge(o_ready, 1)
                for t in range(NT):
                    ins = nc.tensor.transpose(m.ps[:, t // 4, (t % 4) * P:(t % 4 + 1) * P], m.o[:, t, :], m.ident[:])
                    if t % 4 == 3:
                        ins.then_inc(turned, 1)
                for t in range(NT):
                    pe.wait_ge(oT_ready, t // 4 + 1)
                    ins = nc.tensor.matmul(m.ps[:, 2 + t // 4, (t % 4) * P:(t % 4 + 1) * P], m.kdT[:, t * P:(t + 1) * P],
                                           m.woT[:], start=True, stop=True)
                    if t % 4 == 3:
                        ins.then_inc(out_done, 1)




def layer_prepare_stage(nc, m, a, l):
    loads = [("wqkv", "wqkv"), ("wo", "wo"), ("w1", "w1"), ("w2", "w2"), ("lgb", "lgb"), ("b1", "b1"), ("b2", "b2"),
             ("qks", "qks")]
    with signals(nc, "loaded tables_in pad_ready turned hT_ready folded") as (
            loaded, tables_in, pad_ready, turned, hT_ready, folded):
        with nc.Block() as block:
            @block.sync
            def _(sp):
                sp.dma_start(m.rope, a["rope"]).then_inc(tables_in, 16)
                for name, src in loads:
                    ap = a[src][ds(l, 1)]
                    dims = " ".join("abc"[:len(ap.shape) - 2])
                    sp.dma_start(m.named[name][:], ap.rearrange(f"o p {dims} -> (o p) {dims}")).then_inc(loaded, 16)
                sp.wait_ge(loaded, 16 * len(loads))

            @block.gpsimd
            def _(pool):
                nc.gpsimd.memset(m.kwin, 0.0).then_inc(pad_ready, 1)
                nc.gpsimd.memset(m.va[:, 0, :], 0.0).then_inc(pad_ready, 1)
                nc.gpsimd.memset(m.pw[:, :, 0:P - WIN], 0.0).then_inc(pad_ready, 1)
                pool.wait_ge(tables_in, 16)
                pool.wait_ge(loaded, 16 * len(loads))
                for j in range(4):
                    nc.gpsimd.tensor_tensor(m.rope[:, j, :, :], m.rope[:, j, :, :],
                                            bcast(m.qks[:, j, :].unsqueeze(1), P, NT, HD2), ALU.mult).then_inc(folded, 1)
                pool.wait_ge(folded, 4)

            @block.vector
            def _(dve):
                nc.vector.memset(m.hT[P // 2:P, 0:1], 0.0).then_inc(pad_ready, 1)

            @block.tensor
            def _(pe):
                for t in range(NT):
                    ins = nc.tensor.transpose(m.ps[:, t // 4, (t % 4) * P:(t % 4 + 1) * P], m.hc[:, t, :], m.ident[:])
                    if t % 4 == 3:
                        ins.then_inc(turned, 1)

            @block.scalar
            def _(act):
                for h in range(2):
                    act.wait_ge(turned, h + 1)
                    nc.scalar.activation(m.hT[0:P // 2, h * HALF:(h + 1) * HALF], m.ps[0:P // 2, h, :],
                                         ACT.Copy).then_inc(hT_ready, 1)
                    nc.scalar.activation(m.hT[P // 2:P, 1 + h * HALF:1 + (h + 1) * HALF], m.ps[P // 2:P, h, :],
                                         ACT.Copy).then_inc(hT_ready, 1)


def window_stage(nc, m):
    with signals(nc, "staged qkv_done sq_ready ss_ready root_ready prod_ready v_ready rot_ready qk_turned qT_ready "
                     "kT_ready scores_done shifted probs_ready p_turned evac_a evac_d values_done y_ready "
                     "o_turned oT_ready wo_done hc_ready ch rn_ready window_moved band_ready") as (
            staged, qkv_done, sq_ready, ss_ready, root_ready, prod_ready, v_ready, rot_ready, qk_turned, qT_ready,
            kT_ready, scores_done, shifted, probs_ready, p_turned, evac_a, evac_d, values_done, y_ready,
            o_turned, oT_ready, wo_done, hc_ready, chs, rn_ready, window_moved, band_ready):
        HD = HD2 // 2
        with nc.Block() as block:
            @block.gpsimd
            def _(pool):
                nc.gpsimd.tensor_copy(m.band_t[:], m.band[:, 0, :]).then_inc(band_ready, 1)
                with pool.Fori(0, NT) as it:
                    nc.gpsimd.tensor_copy(m.kwin[:, :, 0:WIN], m.kwin[:, :, P:KW]).then_inc(window_moved, 1)
                    nc.gpsimd.tensor_copy(m.hT_t[:], m.hT[:, ds(it * P, P)]).then_inc(staged, 1)
                    for j in range(2):
                        qv = m.rot[:, j, :, :]
                        pool.wait_ge(prod_ready, it * 2 + j + 1)
                        nc.gpsimd.tensor_tensor(qv, qv, m.rot2[:, j, :, :], ALU.add).then_inc(rot_ready, 1)
                        pool.wait_ge(rot_ready, it * 4 + 2 * j + 1)
                        pool.wait_ge(rn_ready, it + 1)
                        nc.gpsimd.tensor_tensor(qv, qv, bcast(m.qkn[:, j * H2:(j + 1) * H2].unsqueeze(2), P, H2, HD2),
                                                ALU.mult).then_inc(rot_ready, 1)
                    pool.wait_ge(band_ready, 1)
                    pool.wait_ge(hc_ready, it + 1)
                    nc.gpsimd.tensor_copy(m.band_t[:], m.band[:, 1, :]).then_inc(band_ready, 1)

            @block.tensor
            def _(pe):
                with pe.Fori(0, NT) as it:
                    pe.wait_ge(staged, it + 1)
                    for j in range(3):
                        nc.tensor.matmul(m.ps[:, j, :], m.hT_t[:], m.wqkv[:, j * INNER:(j + 1) * INNER], start=True,
                                         stop=True).then_inc(qkv_done, 1)
                    for j in range(2):
                        pe.wait_ge(rot_ready, it * 4 + 2 * j + 2)
                        for p in range(4):
                            ins = nc.tensor.transpose(m.ps[:, 3 + j, p * P:(p + 1) * P],
                                                      m.rot[:, j, 2 * p:2 * p + 2, :].rearrange("p h d -> p (h d)"),
                                                      m.ident[:])
                        ins.then_inc(qk_turned, 1)
                    pe.wait_ge(qT_ready, it + 1)
                    pe.wait_ge(kT_ready, it + 1)
                    pe.wait_ge(v_ready, it + 1)

                    def scores(h):
                        if h >= 2:
                            pe.wait_ge(shifted, it * H2 + h - 1)
                        r = slice((h % 2) * HD2, (h % 2 + 1) * HD2)
                        nc.tensor.matmul(m.ps[:, 5 + h % 2, 0:KW], m.qT_t[r, h // 2, :],
                                         m.kwin[r, h // 2, :], start=True,
                                         stop=True).then_inc(scores_done, 1)

                    def copied(h):
                        pe.wait_ge(evac_a if h % 2 else evac_d, it * 4 + h // 2 + 1)

                    def turn(h):
                        pe.wait_ge(probs_ready, it * H2 + h + 1)
                        if h >= 2:
                            copied(h - 2)
                        for k in range(2):
                            ins = nc.tensor.transpose(m.ps[:, 3 + h % 2, k * P:(k + 1) * P], m.pw[:, h % 2, k * P:(k + 1) * P],
                                                      m.ident[:])
                        ins.then_inc(p_turned, 1)

                    def values(h):
                        copied(h)
                        if h >= 2:
                            pe.wait_ge(y_ready, it * H2 + h - 1)
                        for k in range(2):
                            ins = nc.tensor.matmul(m.ps[:, 7 if h % 2 else 2, 0:HD2], m.pwT[:, h % 2, k, :],
                                                   m.va[:, ds(it + k, 1), h * HD2:(h + 1) * HD2].rearrange("p o c -> p (o c)"),
                                                   start=(k == 0), stop=(k == 1))
                        ins.then_inc(values_done, 1)

                    scores(0)
                    for n in range(1, H2 + 2):
                        if n < H2:
                            scores(n)
                        if n - 1 < H2:
                            turn(n - 1)
                        if n >= 2:
                            values(n - 2)
                    pe.wait_ge(y_ready, it * H2 + H2)
                    for p in range(4):
                        ins = nc.tensor.transpose(m.ps[:, 0, p * P:(p + 1) * P], m.ow[:, p * P:(p + 1) * P], m.ident[:])
                    ins.then_inc(o_turned, 1)
                    pe.wait_ge(oT_ready, it + 1)
                    for p in range(4):
                        ins = nc.tensor.matmul(m.ps[:, 1, 0:P], m.oT[:, p * P:(p + 1) * P], m.wo[:, p, :],
                                               start=(p == 0), stop=(p == 3))
                    ins.then_inc(wo_done, 1)
                    pe.wait_ge(hc_ready, it + 1)

            @block.scalar
            def _(act):
                with act.Fori(0, NT) as it:
                    for j in range(2):
                        act.wait_ge(qkv_done, it * 3 + j + 1)
                        nc.scalar.activation(m.sqw[:, j, :], m.ps[:, j, :], ACT.Square).then_inc(sq_ready, 1)
                    act.wait_ge(qkv_done, it * 3 + 3)
                    nc.scalar.activation(m.va[:, ds(it + 1, 1), :].rearrange("p o c -> p (o c)"), m.ps[:, 2, :],
                                         ACT.Copy).then_inc(v_ready, 1)
                    act.wait_ge(ss_ready, it + 1)
                    nc.scalar.activation(m.qkn[:], m.qkn[:], ACT.Sqrt).then_inc(root_ready, 1)
                    act.wait_ge(qk_turned, it * 2 + 1)
                    nc.scalar.activation(m.qT_t.rearrange("p h q -> p (h q)"), m.ps[:, 3, :], ACT.Copy).then_inc(qT_ready, 1)
                    act.wait_ge(qk_turned, it * 2 + 2)
                    act.wait_ge(window_moved, it + 1)
                    nc.scalar.activation(m.kwin[:, :, WIN:KW], m.ps[:, 4, :].rearrange("p (h q) -> p h q", h=4),
                                         ACT.Copy).then_inc(kT_ready, 1)

                    def exp(h):
                        act.wait_ge(shifted, it * H2 + h + 1)
                        nc.scalar.activation(m.pw[:, h % 2, P - WIN:2 * P], m.pw[:, h % 2, P - WIN:2 * P], ACT.Exp,
                                             bias=m.nmaxw[:, h:h + 1], scale=-1.0,
                                             accum_out=m.esumw[:, h:h + 1]).then_inc(probs_ready, 1)

                    exp(0)
                    for n in range(1, H2 + 1):
                        if n < H2:
                            exp(n)
                        h = n - 1
                        if h % 2 == 1:
                            act.wait_ge(p_turned, it * H2 + h + 1)
                            if h >= 2:
                                act.wait_ge(values_done, it * H2 + h - 1)
                            nc.scalar.activation(m.pwT[:, 1, :, :].rearrange("p k q -> p (k q)"), m.ps[:, 4, 0:2 * P],
                                                 ACT.Copy).then_inc(evac_a, 1)
                    act.wait_ge(o_turned, it + 1)
                    nc.scalar.activation(m.oT, m.ps[:, 0, :], ACT.Copy).then_inc(oT_ready, 1)

            @block.vector
            def _(dve):
                PER = 1 + 4 + 1 + H2
                with dve.Fori(0, NT) as it:
                    c_ = Chain(dve, chs, it * PER)
                    for j in range(2):
                        dve.wait_ge(sq_ready, it * 2 + j + 1)
                        ins = nc.vector.tensor_reduce(m.qkn[:, j * H2:(j + 1) * H2],
                                                      m.sqw[:, j, :].rearrange("p (h d) -> p h d", h=H2), AX, ALU.add)
                        if j == 0:
                            c_.add(ins)
                        else:
                            ins.then_inc(ss_ready, 1)
                    for j in range(2):
                        src = m.ps[:, j, :].rearrange("p (h d) -> p h d", h=H2)

                        def table(i, a, b):
                            return bcast(m.rope[:, 2 * j + i, ds(it, 1), a:b], P, H2, b - a)

                        if j == 0:
                            dve.wait_ge(sq_ready, it * 2 + 2)
                        c_.add(nc.vector.tensor_tensor(m.rot[:, j, :, :], src, table(0, 0, HD2), ALU.mult))
                        c_.add(nc.vector.tensor_tensor(m.rot2[:, j, :, 0:HD], src[:, :, HD:HD2], table(1, 0, HD), ALU.mult))
                        nc.vector.tensor_tensor(m.rot2[:, j, :, HD:HD2], src[:, :, 0:HD], table(1, HD, HD2),
                                                ALU.mult).then_inc(prod_ready, 1)
                        if j == 0:
                            dve.wait_ge(root_ready, it + 1)
                            c_.link(nc.vector.tensor_scalar(m.qkn[:], m.qkn[:], 1e-12, None, ALU.max))
                            nc.vector.reciprocal(m.qkn[:], m.qkn[:]).then_inc(rn_ready, 1)

                    def shift(h):
                        if h >= 2:
                            dve.wait_ge(p_turned, it * H2 + h - 1)
                        if h == 0:
                            dve.wait_ge(band_ready, it + 1)
                        count = dve.to_reg(it * H2 + h + 1)
                        dve.wait_ge(band_ready, 1)
                        dve.wait_ge(scores_done, count)
                        nc.vector.tensor_tensor_reduce(m.pw[:, h % 2, P - WIN:2 * P], m.ps[:, 5 + h % 2, 0:KW],
                                                       m.band_t[:], 1.0, 3.0e38,
                                                       ALU.add, ALU.min, m.nmaxw[:, h:h + 1]).then_inc(shifted, 1)

                    def finish(h):
                        dve.wait_ge(values_done, it * H2 + h + 1)
                        c_.link(nc.vector.reciprocal(m.rsumw[:, h:h + 1], m.esumw[:, h:h + 1]))
                        nc.vector.tensor_scalar(m.ow[:, h * HD2:(h + 1) * HD2], m.ps[:, 7 if h % 2 else 2, 0:HD2],
                                                m.rsumw[:, h:h + 1], None, ALU.mult).then_inc(y_ready, 1)

                    shift(0)
                    for n in range(1, H2 + 2):
                        if n < H2:
                            shift(n)
                        h = n - 1
                        if h < H2 and h % 2 == 0:
                            dve.wait_ge(p_turned, it * H2 + h + 1)
                            if h >= 2:
                                dve.wait_ge(values_done, it * H2 + h - 1)
                            nc.vector.tensor_copy(m.pwT[:, 0, :, :].rearrange("p k q -> p (k q)"),
                                                  m.ps[:, 3, 0:2 * P]).then_inc(evac_d, 1)
                        if n >= 2:
                            finish(n - 2)
                    dve.wait_ge(wo_done, it + 1)
                    hv = m.hc[:, ds(it, 1), :].rearrange("p o c -> p (o c)")
                    nc.vector.tensor_tensor(hv, m.ps[:, 1, 0:P], hv, ALU.add).then_inc(hc_ready, 1)
                    assert c_.n == PER


def shift_stage(nc, m):
    U = P // 2
    with signals(nc, "shifted low_ready high_ready") as (shifted, low_ready, high_ready):
        with nc.Block() as block:
            @block.tensor
            def _(pe):
                for t in range(NT):
                    ins = nc.tensor.matmul(m.ps[:, 0, t * U:(t + 1) * U], m.late[:], m.hc[:, t, U:P], start=True,
                                           stop=(t == 0))
                    if t:
                        ins = nc.tensor.matmul(m.ps[:, 0, t * U:(t + 1) * U], m.carry[:], m.hc[:, t - 1, U:P],
                                               start=False, stop=True)
                ins.then_inc(shifted, 1)

            @block.vector
            def _(dve):
                nc.vector.tensor_copy(m.hs[:, :, 0:U], m.hc[:, :, 0:U]).then_inc(low_ready, 1)
                dve.wait_ge(shifted, 1)
                nc.vector.tensor_copy(m.hs[:, :, U:P], m.ps[:, 0, :].rearrange("p (t c) -> p t c", t=NT)).then_inc(
                    high_ready, 1)


def mlp_stage(nc, m):
    NCH = len(HCH)
    with signals(nc, "up_done gelu_ready hid_ready down_done biased added") as (
            up_done, gelu_ready, hid_ready, down_done, biased, added):
        with nc.Block() as block:
            @block.tensor
            def _(pe):
                def up(half):
                    for i, (c0, n) in enumerate(HCH):
                        if half:
                            pe.wait_ge(hid_ready, i + 1)
                        for j in range(2):
                            ins = nc.tensor.matmul(m.ps[0:n, 3 * j + i, :], m.w1[:, j * HID + c0:j * HID + c0 + n],
                                                   m.hnT[:, half * HALF:(half + 1) * HALF], start=True, stop=True)
                        ins.then_inc(up_done, 1)

                def down(half):
                    pe.wait_ge(hid_ready, NCH * (half + 1))
                    for t in range(4):
                        for i, (c0, n) in enumerate(HCH):
                            ins = nc.tensor.matmul(m.ps[:, 6 + half, t * P:(t + 1) * P], m.hidm[0:n, half, i, t * P:(t + 1) * P],
                                                   m.w2[0:n, i, :], start=(i == 0), stop=(i == NCH - 1))
                    ins.then_inc(down_done, 1)

                up(0)
                up(1)
                down(0)
                down(1)

            @block.scalar
            def _(act):
                for half in range(2):
                    for i, (c0, n) in enumerate(HCH):
                        act.wait_ge(up_done, half * NCH + i + 1)
                        nc.scalar.activation(m.gel[0:n, half, i, :], m.ps[0:n, 3 + i, :], ACT.Gelu,
                                             bias=m.b1[0:n, i, 1:2]).then_inc(gelu_ready, 1)

            @block.vector
            def _(dve):
                nc.vector.tensor_tensor(m.hc, m.hc, bcast(m.b2[:].unsqueeze(1), P, NT, D), ALU.add).then_inc(biased, 1)
                for half in range(2):
                    for i, (c0, n) in enumerate(HCH):
                        dve.wait_ge(gelu_ready, half * NCH + i + 1)
                        nc.vector.scalar_tensor_tensor(out=m.hidm[0:n, half, i, :], in0=m.ps[0:n, i, :],
                                                       scalar=m.b1[0:n, i, 0:1], in1=m.gel[0:n, half, i, :],
                                                       op0=ALU.add, op1=ALU.mult).then_inc(hid_ready, 1)
                dve.wait_ge(biased, 1)
                for half in range(2):
                    dve.wait_ge(down_done, half + 1)
                    hv = m.hc[:, 4 * half:4 * half + 4, :].rearrange("p t c -> p (t c)")
                    nc.vector.tensor_tensor(hv, m.ps[:, 6 + half, :], hv, ALU.add).then_inc(added, 1)




SBUF = {
    "ident": [P, P], "ones": [P, P], "zeros": [P, P],
    "before": [P, P],
    "below": [P, P],
    "later": [P, P],
    "want": [P, 2, NSEL],
    "gateT": [P, E0], "wprojT": [P, PAIRS, P], "bproj": [P, 1],
    "pack": [P, 2, 4 * P], "wst": [P, 3 * P + 3],
    "x": [P, NT, D], "xn": [P, NT, D], "xnT": [P, T], "ffnT": [P, T],
    "bn": [P, NT, 6], "mv": [P, NT, 2], "rstd": [P, NT],
    "rs8": [P, NT], "rs8b": [P, NT], 
    "score": [P, NT, E0 + 1], "rest": [P, NT, E0], "top8": [P, NT, 8],
    "combT": [E0 + 1, T], "silu": [P, 2, HALF], "hid": [P, 2, HALF],
    "qT": [P, T], "kT": [P, T], "v": [P, NT, P], "srelu": [P, 2, T], "past": [P, T],
    "pen": [P, NT, T], "bitf": [P, NSEL], "few": [P, NSEL], "count": [P, NSEL], "need": [P, NSEL],
    "prob": [P, 2, T], "nmax": [P, 2], "esum": [P, 4], "rsum": [P, 4], "pT": [P, 2, NT, P],
    "y": [P, 2, P], "yT": [P, PAIRS, T],
    "chunk_upto": [P, P],
    "strictT": [P, P],
    "bdiag": [P, P],
    "hmask": [P, H1],
    "lev": [P, 4, P],
    "levT": [P, 2, P],
    "sel8": [H1, H1, P], "wvT": [P, D], "wbT16": [P, D], "waT": [P, H1], "wgT": [P, D], "woT": [P, D],
    "dtb": [P, H1], "nega": [P, H1], "convw": [P, 5], "normw": [P, K1],
    "wk": [P, 1 + T], "xv": [P, 3 + T], "rn": [P, NT * H1], "z64": [P, NT * H1], "e64": [P, NT * H1],
    "r64": [P, NT * H1], "rr64": [P, NT * H1], "q64": [P, NT * H1], "decay": [P, NT * H1], "dec": [P, NT * H1],
    "sdecay": [P, NC1], "sd_t": [P, 2],
    "wk_t": [P, P], "rkd_t": [P, P], "kd_t": [P, P], "wcT": [P, P], "ointer": [P, P], "vnew": [P, P],
    "vsol": [P, P], "wsol": [P, P], "state": [P, P], "supd": [P, 2, P], "u": [P, H1, 2 * K1], "w": [P, H1, 2 * K1],
    "late": [P, P],
    "carry": [P, P],
    "band": [P, 2, KW],
    "band_t": [P, KW],
    "wqkv": [P, 3 * INNER], "wo": [P, 4, D], "w1": [P, 2 * HID], "w2": [P, len(HCH), D],
    "lgb": [P, 2], "b1": [P, len(HCH), 2], "b2": [P, D], "qks": [P, 4, HD2],
    "hT_t": [P, P], "qkn": [P, 2 * H2],
    "nmaxw": [P, H2], "esumw": [P, H2], "rsumw": [P, H2],
}
SBUF_INT = {"biti": [P, NSEL], "thr": [P, NSEL], "cand": [P, NSEL]}


class Memory:

    def __init__(self, named):
        self.named = named
        self.ident, self.ones, self.zeros, self.before, self.below, self.later = (
            named[n] for n in "ident ones zeros before below later".split())
        self.want, self.gateT, self.wprojT, self.bproj, self.pack, self.wst = (
            named[n] for n in "want gateT wprojT bproj pack wst".split())
        self.x, self.xn, self.xnT, self.ffnT, self.bn, self.mv = (
            named[n] for n in "x xn xnT ffnT bn mv".split())
        self.rstd, self.rs8, self.rs8b, self.score, self.rest, self.top8 = (
            named[n] for n in "rstd rs8 rs8b score rest top8".split())
        self.combT, self.silu, self.hid, self.qT, self.kT, self.v = (
            named[n] for n in "combT silu hid qT kT v".split())
        self.srelu, self.past, self.pen, self.bitf, self.few, self.count = (
            named[n] for n in "srelu past pen bitf few count".split())
        self.need, self.prob, self.nmax, self.esum, self.rsum, self.pT = (
            named[n] for n in "need prob nmax esum rsum pT".split())
        self.y, self.yT, self.chunk_upto, self.strictT, self.bdiag, self.hmask = (
            named[n] for n in "y yT chunk_upto strictT bdiag hmask".split())
        self.lev, self.levT, self.sel8, self.wvT, self.wbT16, self.waT = (
            named[n] for n in "lev levT sel8 wvT wbT16 waT".split())
        self.wgT, self.woT, self.dtb, self.nega, self.convw, self.normw = (
            named[n] for n in "wgT woT dtb nega convw normw".split())
        self.wk, self.xv, self.rn, self.z64, self.e64, self.r64 = (
            named[n] for n in "wk xv rn z64 e64 r64".split())
        self.rr64, self.q64, self.decay, self.dec, self.sdecay, self.sd_t = (
            named[n] for n in "rr64 q64 decay dec sdecay sd_t".split())
        self.wk_t, self.rkd_t, self.kd_t, self.wcT, self.ointer, self.vnew = (
            named[n] for n in "wk_t rkd_t kd_t wcT ointer vnew".split())
        self.vsol, self.wsol, self.state, self.supd, self.u, self.w = (
            named[n] for n in "vsol wsol state supd u w".split())
        self.late, self.carry, self.band, self.band_t, self.wqkv, self.wo = (
            named[n] for n in "late carry band band_t wqkv wo".split())
        self.w1, self.w2, self.lgb, self.b1, self.b2, self.qks = (
            named[n] for n in "w1 w2 lgb b1 b2 qks".split())
        self.hT_t, self.qkn, self.nmaxw, self.esumw, self.rsumw, self.biti = (
            named[n] for n in "hT_t qkn nmaxw esumw rsumw biti".split())
        self.thr, self.cand = (
            named[n] for n in "thr cand".split())


def share_buffers(m):
    flat = {n: m.named[n][:].rearrange("p a b -> p (a b)") for n in ("pen", "yT", "srelu", "prob", "pack", "silu", "hid")}
    flat["pT"] = m.pT[:].rearrange("p a b c -> p (a b c)")

    def part(name, at, *shape):
        n = int(np.prod(shape))
        ap = flat[name][:, at:at + n]
        if len(shape) == 2:
            return ap.rearrange("p (a b) -> p a b", a=shape[0])
        if len(shape) == 4:
            return ap.rearrange("p (a b c d) -> p a b c d", a=shape[0], b=shape[1], c=shape[2])
        if len(shape) == 3:
            return ap.rearrange("p (a b c) -> p a b c", a=shape[0], b=shape[1])
        return ap

    m.junk = flat["yT"].bitcast(BF16)
    m.sq, m.vb, m.beta, m.decE, m.grow, m.wkb, m.wkbd, m.resto = (part("pen", i * T, T) for i in range(8))
    m.rk, m.rkd, m.kdT = (part("yT", i * T, T) for i in range(3))
    m.xr, m.gate, m.o = (part("yT", (3 + i) * T, NT, D) for i in range(3))
    m.rhs = part("yT", 6 * T, NT, H1, 2 * K1)
    m.kd, m.decT, m.decay16 = m.v, m.combT[0:H1, :], m.kT[:].rearrange("p (t c) -> p t c", t=NT)
    m.lt, m.lts = part("pT", 0, H1, P), part("pT", T, H1, P)
    m.lti, m.nt = part("prob", 0, H1, P), part("prob", T, H1, P)
    m.at, m.xt = part("srelu", 0, H1, P), part("srelu", T, H1, P)
    m.xi, m.ym, m.wkb_h = part("silu", 0, H1, P), part("hid", 0, H1, P), part("pack", 0, H1, P)
    m.rk_h, m.ntm = (z[:].rearrange("p (t c) -> p t c", t=NT) for z in (m.qT, m.past))
    m.hc = m.ffnT[:].rearrange("p (t c) -> p t c", t=NT)
    m.hT = m.xv
    m.rope = flat["srelu"].rearrange("p (j t d) -> p j t d", j=4, t=NT)
    KE = 4 * (P + T)
    m.kwin = part("pen", 0, 4, KW)
    m.va = part("yT", 0, NT + 1, INNER)
    m.rot, m.rot2, m.sqw = part("pen", KE, 2, H2, HD2), part("pen", KE + 2 * INNER, 2, H2, HD2), part("pen", KE + 4 * INNER, 2, INNER)
    m.qT_t, m.ow, m.oT = part("yT", KE, 4, P), part("yT", KE + INNER, INNER), part("yT", KE + 2 * INNER, INNER)
    m.pw, m.pwT = part("yT", KE + 3 * INNER, 2, 2 * P), part("yT", KE + 4 * INNER, 2, 2, P)
    m.hs, m.hn, m.hnT = part("pT", 0, NT, D), part("pT", T, NT, D), m.past[:]
    m.gel, m.hidm = part("pen", 0, 2, len(HCH), HALF), part("yT", 0, 2, len(HCH), HALF)


def build(nc, a, out):
    with ExitStack() as ctx:
        named = {n: ctx.enter_context(nc.sbuf_tensor(n, shape, F32)) for n, shape in SBUF.items()}
        named.update({n: ctx.enter_context(nc.sbuf_tensor(n, shape, I32)) for n, shape in SBUF_INT.items()})
        m = Memory(named)
        m.ps = ctx.enter_context(nc.psum_tensor("ps", [P, 8, HALF], F32))
        m.psf = m.ps[:].rearrange("p b c -> p (b c)")
        share_buffers(m)
        m.candf, m.thrf = m.cand[:].bitcast(F32), m.thr[:].bitcast(F32)
        setup_stage(nc, m, a)
        with nc.Fori(0, B) as b:
            batch_row(nc, m, a, out, b)


def setup_stage(nc, m, a):
    loads = ["ident", "ones", "before", "below", "later", "want", "wprojT", "bproj", "chunk_upto", "strictT", "bdiag",
             "hmask", "lev", "levT", "sel8", "wvT", "wbT16", "waT", "wgT", "woT", "dtb", "nega", "convw", "normw",
             "late", "carry", "band"]
    with signals(nc, "loaded cleared gate_in sq_ready root_ready ch turned") as (
            loaded, cleared, gate_in, sq_ready, root_ready, chs, turned):
        with nc.Block() as block:
            @block.sync
            def _(sp):
                for name in loads:
                    sp.dma_start(m.named[name][:], a[name]).then_inc(loaded, 16)
                sp.dma_start(m.y[0:E0, 0, :], a["gate_w"]).then_inc(gate_in, 16)
                sp.wait_ge(loaded, 16 * len(loads))

            @block.gpsimd
            def _(pool):
                nc.gpsimd.memset(m.zeros[:], 0.0)
                nc.gpsimd.memset(m.score[:], 1.0)

            @block.scalar
            def _(act):
                act.wait_ge(loaded, 16 * len(loads))
                nc.scalar.activation(m.nega[:], m.nega[:], ACT.Exp).then_inc(cleared, 1)
                act.wait_ge(gate_in, 16)
                nc.scalar.activation(m.y[0:E0, 1, :], m.y[0:E0, 0, :], ACT.Square,
                                     accum_out=m.rs8[0:E0, 0:1]).then_inc(sq_ready, 1)
                act.wait_ge(sq_ready, 1)
                nc.scalar.activation(m.rs8b[0:E0, 0:1], m.rs8[0:E0, 0:1], ACT.Sqrt).then_inc(root_ready, 1)

            @block.vector
            def _(dve):
                ch = Chain(dve, chs)
                dve.wait_ge(root_ready, 1)
                r = m.rs8b[0:E0, 0:1]
                ch.link(nc.vector.tensor_scalar(r, r, 1e-12, None, ALU.max))
                ch.link(nc.vector.reciprocal(r, r))
                ch.link(nc.vector.tensor_scalar(m.y[0:E0, 0, :], m.y[0:E0, 0, :], r, None, ALU.mult))
                dve.wait_ge(cleared, 1)
                ch.add(nc.vector.tensor_scalar(m.nega[:], m.nega[:], -1.0, None, ALU.mult))
                dve.wait_ge(turned, 1)
                nc.vector.tensor_copy(m.gateT[:], m.ps[:, 0, 0:E0])

            @block.tensor
            def _(pe):
                pe.wait_ge(chs, 3)
                pe.wait_ge(loaded, 16 * len(loads))
                nc.tensor.transpose(m.ps[:, 0, 0:E0], m.y[0:E0, 0, :], m.ident[0:E0, 0:E0]).then_inc(turned, 1)


def copy_stage(nc, m, b):
    with nc.Block() as block:
        @block.gpsimd
        def _(pool):
            nc.gpsimd.tensor_copy(m.hc, m.xn[:])


def add_stage(nc, m):
    with nc.Block() as block:
        @block.vector
        def _(dve):
            nc.vector.tensor_tensor(m.x[:], m.x[:], m.hc, ALU.add)


def batch_row(nc, m, a, out, b):
    with signals(nc, "x_in") as (x_in,):
        with nc.Block() as block:
            @block.sync
            def _(sp):
                sp.dma_start(m.x[:], a["x"][ds(b, 1)].rearrange("o (t p) d -> p (o t) d", p=P)).then_inc(x_in, 16)
                sp.wait_ge(x_in, 16)
    norm_stage(nc, m, m.x, m.xn, m.xnT)
    experts_stage(nc, m, a["packs"])
    penalty_stage(nc, m, a["qkv_packs"])
    select_stage(nc, m)
    attention_stage(nc, m, a["qkv_packs"])
    project_stage(nc, m)
    norm_stage(nc, m, m.x, m.xn, m.xnT)
    delta_prepare_stage(nc, m)
    delta_stage(nc, m)
    delta_out_stage(nc, m)
    copy_stage(nc, m, b)
    with nc.Fori(0, DEPTH) as l:
        layer_prepare_stage(nc, m, a, l)
        window_stage(nc, m)
        shift_stage(nc, m)
        norm_stage(nc, m, m.hs, m.hn, m.hnT, m.lgb[:, 0:1], m.lgb[:, 1:2])
        mlp_stage(nc, m)
    add_stage(nc, m)
    with signals(nc, "x_out") as (x_out,):
        with nc.Block() as block:
            @block.sync
            def _(sp):
                sp.dma_start(out[ds(b, 1)].rearrange("o (t p) d -> p (o t) d", p=P), m.x[:]).then_inc(x_out, 16)
                sp.wait_ge(x_out, 16)




def shape_constants():
    i = np.arange(P)
    r, c = i[:, None], i[None, :]
    f = lambda z: np.ascontiguousarray(z, dtype=np.float32)
    row = np.arange(TSEL, NT)[None, :] * P + r
    k = np.minimum(KEEP, row + 1)
    width = (np.arange(TSEL, NT) + 1)[None, :] * P
    act = np.zeros(NSEL, bool)
    act[::-2] = True
    want = np.stack([np.where(act[None, :], 2 * k - width, k), k], axis=1)
    same = r // C1 == c // C1

    def joins(rows, cols, s):
        return same & ((rows // s) % 2 == 1) & (cols // s == rows // s - 1)

    half = np.arange(0, HD2, 2, dtype=np.float32)
    inv = (1.0 / np.float32(10000.0) ** (half / np.float32(HD2))).astype(np.float32)
    tt = np.arange(T, dtype=np.float32)
    ang = (tt[:, None] * inv[None, :]).astype(np.float32).astype(np.float64)
    grown = ((half + 0.4 * HD2) / (1.4 * HD2)).astype(np.float64)[None, :] ** ((tt.astype(np.float64) - T // 2) / (WIN // 2))[:, None]
    two = lambda z: np.concatenate([z, z], -1)
    signed = lambda z: np.concatenate([-z, z], -1)
    rope = np.stack([-8 * two(np.cos(ang) * grown), -8 * signed(np.sin(ang) * grown), two(np.cos(ang) / grown),
                     signed(np.sin(ang) / grown)])
    key = np.arange(KW)[None, None, :] - WIN
    tile = np.arange(2)[None, :, None]
    off = r[:, :, None] - key
    seen = (off >= 0) & (off <= WIN) & (tile * P + key >= 0)
    return {
        "chunk_upto": f(same & (r <= c)), "strictT": f(same & (r < c)), "bdiag": f(r // K1 == c // K1),
        "hmask": f(r // K1 == np.arange(H1)[None, :]),
        "lev": f(np.stack([joins(r, c, s) for s in (2, 4, 8, 16)], 1)),
        "levT": f(np.stack([joins(c, r, s) for s in (1, 32)], 1)),
        "sel8": f(np.broadcast_to(np.eye(H1)[:, :, None], (H1, H1, P))),
        "late": f(r == c - 1), "carry": f((r == P - 1) & (c == 0)), "band": f(np.where(seen, 0.0, BIG)),
        "rope": f(rope.reshape(4, NT, P, HD2).transpose(2, 0, 1, 3)),
        "ident": f(r == c), "ones": f(np.ones((P, P))), "before": f(r < c), "below": f(c < r),
        "later": f((c > r) * BIG), "want": f(want),
    }


def layouts(i):
    f32 = np.float32
    w = np.asarray(i["L0_attn_W_attn"]).reshape(3, PAIRS, P, D)
    bias = np.asarray(i["L0_attn_b_attn"]).reshape(3, PAIRS, P)
    qkv = np.zeros((PAIRS, P, 3 * P + 3), f32)
    for j in range(3):
        qkv[:, :, j * P:(j + 1) * P] = w[j].transpose(0, 2, 1)
        qkv[:, :, 3 * P + j] = bias[j]
    packs = np.zeros((PACKS, P, 4 * P), f32)
    for p in range(PACKS - 1):
        for e in range(2):
            packs[p, :, e * HE0:(e + 1) * HE0] = i["L0_ffn_w_gate"][2 * p + e]
            packs[p, :, P + e * HE0:P + (e + 1) * HE0] = i["L0_ffn_w_up"][2 * p + e]
            packs[p, e * HE0:(e + 1) * HE0, 2 * P:3 * P] = i["L0_ffn_w_down"][2 * p + e]
            packs[p, 2 * p + e, 3 * P + e * HE0:3 * P + (e + 1) * HE0] = 1.0
    packs[-1, :, 0:HE0] = i["L0_ffn_sw_gate"]
    packs[-1, :, P:P + HE0] = i["L0_ffn_sw_up"]
    packs[-1, 0:HE0, 2 * P:3 * P] = i["L0_ffn_sw_down"]
    packs[-1, E0, 3 * P:4 * P] = 1.0
    c = np.ascontiguousarray
    wproj = np.asarray(i["L0_attn_W_proj"]).reshape(D, PAIRS, P).transpose(2, 1, 0)
    g = {n: np.asarray(v) for n, v in i.items()}
    rows = lambda z: c(np.broadcast_to(z[..., None, :], (*z.shape[:-1], P, z.shape[-1])))
    qs, ks = g["L1_ffn_q_scale"], g["L1_ffn_k_scale"]
    qks = np.stack([qs, np.roll(qs, HD2 // 2, -1), ks, np.roll(ks, HD2 // 2, -1)], 1)
    w2, b1 = np.zeros((DEPTH, P, len(HCH), D), f32), np.zeros((DEPTH, P, len(HCH), 2), f32)
    for j, (c0, n) in enumerate(HCH):
        w2[:, 0:n, j, :] = g["L1_ffn_w2"][:, c0:c0 + n, :]
        for k in range(2):
            b1[:, 0:n, j, k] = g["L1_ffn_b1"][:, k * HID + c0:k * HID + c0 + n]
    return {
        "wvT": c(g["L1_attn_Wv"].T), "wgT": c(g["L1_attn_Wg"].T), "woT": c(g["L1_attn_Wo"].T),
        "waT": c(g["L1_attn_Wa"].T), "wbT16": c(np.repeat(g["L1_attn_Wb"].T, K1, axis=1)),
        "dtb": rows(g["L1_attn_dt_bias"]), "nega": rows(g["L1_attn_A_log"]), "normw": rows(g["L1_attn_norm_w"]),
        "convw": c(np.concatenate([g["L1_attn_conv_w"], g["L1_attn_conv_b"][:, None]], 1)),
        "wqkv": c(g["L1_ffn_wqkv"]), "w1": c(g["L1_ffn_w1"]), "w2": w2, "b1": b1, "b2": rows(g["L1_ffn_b2"]),
        "wo": c(g["L1_ffn_wo"].reshape(DEPTH, 4, P, D).transpose(0, 2, 1, 3)),
        "lgb": c(np.stack([g["L1_ffn_ln_g"], g["L1_ffn_ln_b"]], -1)),
        "qks": c(np.broadcast_to(qks[:, None], (DEPTH, P, 4, HD2))),
        "x": c(i["L0_attn_x"]), "gate_w": c(i["L0_ffn_gate_w"]), "qkv_packs": qkv, "packs": packs,
        "wprojT": c(wproj), "bproj": c(np.asarray(i["L0_attn_b_proj"]).reshape(D, 1)),
    }


def kernel(**inputs):
    import concourse.bacc as bacc
    from concourse.bass_utils import run_bass_kernel_spmd

    nc = bacc.Bacc("TRN2", target_bir_lowering=False, num_devices=1)
    arrays = {n: np.asarray(v) for n, v in {**shape_constants(), **layouts(inputs)}.items()}
    a = {n: nc.dram_tensor(f"in_{n}", v.shape, mybir.dt.from_np(v.dtype), kind="ExternalInput").ap()
         for n, v in arrays.items()}
    out = nc.dram_tensor("out", (B, T, D), F32, kind="ExternalOutput").ap()
    build(nc, a, out)
    r = run_bass_kernel_spmd(nc, [{f"in_{n}": v for n, v in arrays.items()}], core_ids=[0])
    return r.results[0]["out"]
```

```python
from contextlib import ExitStack, contextmanager

import numpy as np

import concourse.bass as bass
from concourse import mybir

F32 = mybir.dt.float32
I32 = mybir.dt.int32
BF16 = mybir.dt.bfloat16
ALU = mybir.AluOpType
ACT = mybir.ActivationFunctionType
AX = mybir.AxisListType.X
ds = bass.ds

P = 128
B, T, D = 2, 1024, 128
NT = T // P
HALF = 512
BIG = 1.5e38
LN_EPS = 1e-5

H0, HD0 = 16, 64
PAIRS = H0 // 2
BUDGET = max(1, int(T * 0.2))
KEEP = min(BUDGET - 1, T)
TSEL = KEEP // P
NSEL = NT - TSEL
E0, HE0, TOPK = 16, 64, 8
PACKS = E0 // 2 + 1
H1, K1, C1 = 8, 16, 64
NC1 = T // C1
EPS_L2, EPS_RMS = 1e-6, 1e-5
DEPTH, H2, HD2, WIN = 2, 8, 64, 64
INNER = H2 * HD2
HID = int(D * 4 * 2 / 3)
HCH = [(0, 128), (128, 128), (256, HID - 256)]
KW = WIN + P


@contextmanager
def signals(nc, names):
    with ExitStack() as ctx:
        got = [ctx.enter_context(nc.semaphore(n)) for n in names.split()]
        yield got
        nums = sorted(s.num for s in got)
        while nums:
            run = next(k for k in range(1, len(nums) + 1) if k == len(nums) or nums[k] != nums[0] + k)
            nc.gpsimd.sem_clear(range(nums[0], nums[0] + run))
            nums = nums[run:]
        nc.all_engine_barrier()


class Chain:

    def __init__(self, eng, sem, base=0):
        self.eng, self.sem, self.base, self.n = eng, sem, base, 0

    def add(self, ins):
        self.n += 1
        ins.then_inc(self.sem, 1)

    def hold(self):
        self.eng.wait_ge(self.sem, self.base + self.n)

    def link(self, ins):
        self.add(ins)
        self.hold()


def bcast(ap, *shape):
    return ap.to_broadcast(list(shape))




def norm_stage(nc, m, src, out, outT, gain=None, shift=None):
    with signals(nc, "stats_step var_ready rstd_root normed turned outT_step") as (
            stats_step, var_ready, rstd_root, normed, turned, outT_step):
        with nc.Block() as block:
            @block.vector
            def _(dve):
                ch = Chain(dve, stats_step)
                for t in range(NT):
                    ch.add(nc.vector.bn_stats(m.bn[:, t, :], src[:, t, :]))
                ch.hold()
                for t in range(NT):
                    ch.add(nc.vector.bn_aggr(m.mv[:, t, :], m.bn[:, t, :]))
                ch.hold()
                nc.vector.tensor_scalar(m.rstd[:], m.mv[:, :, 1], LN_EPS, None, ALU.add).then_inc(var_ready, 1)
                dve.wait_ge(rstd_root, 1)
                ch.link(nc.vector.reciprocal(m.rstd[:], m.rstd[:]))
                for t in range(NT):
                    nc.vector.tensor_scalar(out[:, t, :], src[:, t, :], m.mv[:, t, 0:1], m.rstd[:, t:t + 1],
                                            ALU.subtract, ALU.mult).then_inc(normed, 1)

            @block.tensor
            def _(pe):
                for t in range(NT):
                    pe.wait_ge(normed, t + 1)
                    nc.tensor.transpose(m.ps[:, t // 4, (t % 4) * P:(t % 4 + 1) * P], out[:, t, :],
                                        m.ident[:]).then_inc(turned, 1)

            @block.scalar
            def _(act):
                act.wait_ge(var_ready, 1)
                nc.scalar.activation(m.rstd[:], m.rstd[:], ACT.Sqrt).then_inc(rstd_root, 1)
                for half in range(2):
                    act.wait_ge(turned, 4 * half + 4)
                    o = outT[:, half * HALF:(half + 1) * HALF]
                    if gain is None:
                        nc.scalar.activation(o, m.ps[:, half, :], ACT.Copy).then_inc(outT_step, 1)
                    else:
                        nc.scalar.activation(o, m.ps[:, half, :], ACT.Identity, bias=shift,
                                             scale=gain).then_inc(outT_step, 1)




def experts_stage(nc, m, packs):
    with signals(nc, "pack0 pack1 sq_ready root_ready dv logits_ready scores_ready topk_step combT_turned "
                     "combT_ready gates_ready silu_ready hidden_ready used_pack out_done out_ready") as (
            pack0, pack1, sq_ready, root_ready, dv, logits_ready, scores_ready, topk_step, combT_turned,
            combT_ready, gates_ready, silu_ready, hidden_ready, used_pack, out_done, out_ready):
        pack_sem = [pack0, pack1]
        nloop = PACKS // 2
        with nc.Block() as block:
            @block.sync
            def _(sp):
                for s in range(2):
                    sp.dma_start(m.pack[:, s, :], packs[s]).then_inc(pack_sem[s], 16)
                with sp.Fori(1, nloop) as it:
                    for s in range(2):
                        sp.wait_ge(used_pack, it * 2 - 1 + s)
                        sp.dma_start(m.pack[:, s, :], packs[ds(it * 2 + s, 1)].rearrange("o p n -> (o p) n")
                                     ).then_inc(pack_sem[s], 16)
                sp.wait_ge(used_pack, PACKS - 2)
                sp.dma_start(m.pack[:, 0, :], packs[PACKS - 1]).then_inc(pack_sem[0], 16)

            def elementwise(dve, k, it2, s, half, first):
                base = it2 * 4 + k
                dve.wait_ge(silu_ready, base + 1)
                c = dv_chain[0]
                c.link(nc.vector.tensor_tensor(m.hid[:, half, :], m.ps[:, 2 + half, :], m.silu[:, half, :], ALU.mult))
                nc.vector.tensor_tensor(m.hid[:, half, :], m.ps[:, 4 + half, :], m.hid[:, half, :],
                                        ALU.mult).then_inc(hidden_ready, 1)

            dv_chain = [None]
            TOPK_STEPS = [0]

            @block.vector
            def _(dve):
                ch = Chain(dve, dv)
                dve.wait_ge(root_ready, 1)
                ch.link(nc.vector.tensor_scalar(m.rs8[:], m.rs8[:], 1e-12, None, ALU.max))
                ch.link(nc.vector.reciprocal(m.rs8[:], m.rs8[:]))
                dve.wait_ge(logits_ready, NT)
                nc.vector.tensor_tensor(m.score[:, :, 0:E0], m.ps[:, 0, 0:NT * E0].rearrange("p (t e) -> p t e", e=E0),
                                        bcast(m.rs8[:].unsqueeze(2), P, NT, E0), ALU.mult).then_inc(topk_step, 1)
                dve.wait_ge(scores_ready, 1)
                for t in range(NT):
                    ch.add(nc.vector.max(m.top8[:, t, :], m.score[:, t, 0:E0]))
                ch.hold()
                for t in range(NT):
                    ch.add(nc.vector.match_replace(m.rest[:, t, :], m.top8[:, t, :], m.score[:, t, 0:E0], -1.0))
                ch.hold()
                ch.link(nc.vector.scalar_tensor_tensor(out=m.rest[:], in0=m.rest[:], scalar=0.0,
                                                       in1=m.score[:, :, 0:E0], op0=ALU.is_lt, op1=ALU.mult))
                ch.link(nc.vector.tensor_reduce(m.rs8b[:], m.rest[:], AX, ALU.add))
                ch.link(nc.vector.reciprocal(m.rs8b[:], m.rs8b[:]))
                nc.vector.tensor_tensor(m.score[:, :, 0:E0], m.rest[:], bcast(m.rs8b[:].unsqueeze(2), P, NT, E0),
                                        ALU.mult).then_inc(topk_step, 1)
                base = ch.n
                with dve.Fori(0, nloop) as it:
                    c = dv_chain[0] = Chain(dve, dv, base + it * 4)
                    for k in range(4):
                        elementwise(dve, k, it, k // 2, k % 2, False)
                    assert c.n == 4
                dv_chain[0] = Chain(dve, dv, base + 4 * nloop)
                for k in range(2):
                    elementwise(dve, k, nloop, 0, k, False)

            @block.scalar
            def _(act):
                for t in range(NT):
                    nc.scalar.activation(m.silu[:, t // 4, (t % 4) * P:(t % 4 + 1) * P], m.xn[:, t, :], ACT.Square,
                                         accum_out=m.rs8[:, t:t + 1]).then_inc(sq_ready, 1)
                act.wait_ge(sq_ready, NT)
                nc.scalar.activation(m.rs8[:], m.rs8[:], ACT.Sqrt).then_inc(root_ready, 1)
                act.wait_ge(topk_step, 1)
                nc.scalar.activation(m.score[:, :, 0:E0], m.score[:, :, 0:E0], ACT.Sigmoid).then_inc(scores_ready, 1)
                for half in range(2):
                    act.wait_ge(combT_turned, 4 * (half + 1))
                    nc.scalar.activation(m.combT[0:E0 + 1, half * HALF:(half + 1) * HALF],
                                         m.ps[0:E0 + 1, half, :], ACT.Copy).then_inc(combT_ready, 1)

                def silu(n, half):
                    act.wait_ge(gates_ready, n + 1)
                    nc.scalar.activation(m.silu[:, half, :], m.ps[:, half, :], ACT.Silu).then_inc(silu_ready, 1)

                with act.Fori(0, nloop) as it:
                    for k in range(4):
                        silu(it * 4 + k, k % 2)
                for k in range(2):
                    silu(nloop * 4 + k, k)
                for half in range(2):
                    act.wait_ge(out_done, 1)
                    nc.scalar.activation(m.ffnT[:, half * HALF:(half + 1) * HALF], m.ps[:, 6 + half, :],
                                         ACT.Copy).then_inc(out_ready, 1)

            @block.tensor
            def _(pe):
                for t in range(NT):
                    nc.tensor.matmul(m.ps[:, 0, t * E0:(t + 1) * E0], m.xnT[:, t * P:(t + 1) * P],
                                     m.gateT[:, 0:E0], start=True, stop=True).then_inc(logits_ready, 1)
                pe.wait_ge(topk_step, 2)
                for t in range(NT):
                    nc.tensor.transpose(m.ps[0:E0 + 1, t // 4, (t % 4) * P:(t % 4 + 1) * P], m.score[:, t, :],
                                        m.ident[:]).then_inc(combT_turned, 1)
                for half in range(2):
                    nc.tensor.matmul(m.ps[:, 6 + half, :], m.zeros[:, 0:P], m.xnT[:, half * HALF:(half + 1) * HALF],
                                     start=True, stop=False, skip_group_check=True)

                def up(n, s, half, wait_hidden):
                    if wait_hidden is not None:
                        pe.wait_ge(hidden_ready, wait_hidden)
                    x = m.xnT[:, half * HALF:(half + 1) * HALF]
                    nc.tensor.matmul(m.ps[:, 2 + half, :], m.pack[:, s, P:2 * P], x, start=True, stop=True)
                    nc.tensor.matmul(m.ps[:, 4 + half, :], m.pack[0:E0 + 1, s, 3 * P:4 * P],
                                     m.combT[0:E0 + 1, half * HALF:(half + 1) * HALF], start=True, stop=True)
                    nc.tensor.matmul(m.ps[:, half, :], m.pack[:, s, 0:P], x, start=True,
                                     stop=True).then_inc(gates_ready, 1)

                def down(n, s, half):
                    pe.wait_ge(hidden_ready, n + 1)
                    ins = nc.tensor.matmul(m.ps[:, 6 + half, :], m.pack[:, s, 2 * P:3 * P], m.hid[:, half, :],
                                           start=False, stop=False, skip_group_check=True)
                    if half == 1:
                        ins.then_inc(used_pack, 1)

                pe.wait_ge(combT_ready, 2)
                pe.wait_ge(pack0, 16)
                up(0, 0, 0, None)
                up(1, 0, 1, None)
                with pe.Fori(0, nloop) as it:
                    for k in range(4):
                        down(it * 4 + k, k // 2, k % 2)
                        s = (k // 2 + 1) % 2
                        if k % 2 == 0:
                            pe.wait_ge(pack_sem[s], (it + 1) * 16 if s == 1 else (it + 2) * 16)
                        up(it * 4 + k + 2, s, k % 2, it * 4 + k + 1)
                for k in range(2):
                    down(nloop * 4 + k, 0, k)
                nc.tensor.matmul(m.ps[:, 7, :], m.zeros[:, 0:P], m.xnT[:, 0:HALF], start=False, stop=True,
                                 skip_group_check=True).then_inc(out_done, 1)




def penalty_stage(nc, m, qkv_packs):
    with signals(nc, "pack_in qk_done qk_ready att_done relu_ready summed past_ready pen_ready ch padded") as (
            pack_in, qk_done, qk_ready, att_done, relu_ready, summed, past_ready, pen_ready, chs, padded):
        with nc.Block() as block:
            @block.sync
            def _(sp):
                sp.dma_start(m.wst[:], qkv_packs[0]).then_inc(pack_in, 16)

            @block.gpsimd
            def _(pool):
                nc.gpsimd.memset(m.past[:], 0.0).then_inc(past_ready, 1)
                for t in range(NT - 1):
                    w = P * (t + 1)
                    pool.wait_ge(summed, t + 1)
                    pool.wait_ge(past_ready, t + 1)
                    nc.gpsimd.tensor_tensor(m.past[:, 0:w], m.past[:, 0:w], m.srelu[:, t % 2, 0:w],
                                            ALU.add).then_inc(past_ready, 1)

            @block.tensor
            def _(pe):
                pe.wait_ge(pack_in, 16)
                for j in range(2):
                    for half in range(2):
                        nc.tensor.matmul(m.ps[:, 2 * j + half, :], m.wst[:, j * P:(j + 1) * P],
                                         m.xnT[:, half * HALF:(half + 1) * HALF], start=True,
                                         stop=True).then_inc(qk_done, 1)
                pe.wait_ge(qk_ready, 4)
                pe.wait_ge(padded, 1)

                def att(t):
                    w = P * (t + 1)
                    if t >= 2:
                        pe.wait_ge(relu_ready, t - 1)
                    for a in range(0, w, HALF):
                        b = min(w, a + HALF)
                        ins = nc.tensor.matmul(m.ps[:, 2 * (t % 2) + a // HALF, 0:b - a], m.qT[:, 0, t * P:(t + 1) * P],
                                               m.kT[:, a:b], start=True, stop=True)
                    ins.then_inc(att_done, 1)

                att(0)
                for t in range(NT):
                    w = P * (t + 1)
                    if t + 1 < NT:
                        att(t + 1)
                    pe.wait_ge(relu_ready, t + 1)
                    pe.wait_ge(past_ready, t + 1)
                    if t >= 2:
                        pe.wait_ge(pen_ready, t - 1)
                    for a in range(0, w, HALF):
                        b = min(w, a + HALF)
                        bank = 4 + 2 * (t % 2) + a // HALF
                        nc.tensor.matmul(m.ps[:, bank, 0:b - a], m.before[:], m.srelu[:, t % 2, a:b],
                                         start=True, stop=False)
                        ins = nc.tensor.matmul(m.ps[:, bank, 0:b - a], m.ones[:], m.past[:, a:b],
                                               start=False, stop=True)
                    ins.then_inc(summed, 1)

            @block.vector
            def _(dve):
                nc.vector.memset(m.qT[HD0:P, 0, :], 0.0).then_inc(padded, 1)
                for half in range(2):
                    dve.wait_ge(qk_done, half + 1)
                    nc.vector.tensor_scalar(m.qT[0:HD0, 0, half * HALF:(half + 1) * HALF], m.ps[0:HD0, half, :],
                                            m.qkvb[0:HD0, 0:1], -1.0 / 8, ALU.add, ALU.mult).then_inc(qk_ready, 1)
                for half in range(2):
                    dve.wait_ge(qk_done, half + 3)
                    nc.vector.tensor_scalar(m.kT[:, half * HALF:(half + 1) * HALF], m.ps[:, 2 + half, :],
                                            m.qkvb[:, 1:2], None, ALU.add).then_inc(qk_ready, 1)
                ch = Chain(dve, chs)

                def relu(t):
                    w = P * (t + 1)
                    dve.wait_ge(att_done, t + 1)
                    if t >= 2:
                        dve.wait_ge(summed, t - 1)
                        dve.wait_ge(past_ready, t)
                    ch.link(nc.vector.tensor_scalar(m.srelu[:, t % 2, 0:w], m.psf[:, 2 * (t % 2) * HALF:2 * (t % 2) * HALF + w],
                                                    -1.0, 0.0, ALU.mult, ALU.max))
                    ch.link(nc.vector.tensor_tensor(m.srelu[:, t % 2, t * P:w], m.srelu[:, t % 2, t * P:w],
                                                    m.below[:], ALU.mult))
                    nc.vector.memset(m.srelu[:, t % 2, 0:1], 0.0).then_inc(relu_ready, 1)

                relu(0)
                for t in range(NT):
                    w = P * (t + 1)
                    if t + 1 < NT:
                        relu(t + 1)
                    dve.wait_ge(summed, t + 1)
                    o = (4 + 2 * (t % 2)) * HALF
                    if t:
                        ch.add(nc.vector.tensor_copy(m.pen[:, t, 0:t * P], m.psf[:, o:o + t * P]))
                    nc.vector.tensor_tensor(m.pen[:, t, t * P:w], m.psf[:, o + t * P:o + w], m.later[:],
                                            ALU.add).then_inc(pen_ready, 1)


def select_stage(nc, m):
    NB = 31

    def joff(t):
        return P * t * (t + 1) // 2

    tiles = list(range(TSEL, NT))
    by_act = tiles[::-2]
    by_dve = [t for t in tiles if t not in by_act]
    with signals(nc, "ch start_ready cand_ready act_counted") as (chs, start_ready, cand_ready, act_counted):
        with nc.Block() as block:
            @block.scalar
            def _(act):
                with act.Fori(0, NB) as it:
                    act.wait_ge(cand_ready, it + 1)
                    for t in by_act:
                        i = t - TSEL
                        nc.scalar.activation(m.junk[:, joff(t):joff(t) + P * (t + 1)], m.pen[:, t, 0:P * (t + 1)], ACT.Sign,
                                             bias=m.candf[:, i:i + 1], scale=-1.0,
                                             accum_out=m.count[:, i:i + 1]).then_inc(act_counted, 1)

            @block.vector
            def _(dve):
                ch = Chain(dve, chs)
                ch.add(nc.vector.memset(m.bitf[:], float(2 ** (NB - 1))))
                ch.add(nc.vector.memset(m.thr[:], 0))
                ch.hold()
                ch.link(nc.vector.tensor_copy(m.biti[:], m.bitf[:]))
                nc.vector.tensor_tensor(m.cand[:], m.thr[:], m.biti[:], ALU.bitwise_or).then_inc(cand_ready, 1)
                base, per = ch.n, len(by_dve) + 4
                with dve.Fori(0, NB) as it:
                    c = Chain(dve, chs, base + it * per)
                    dve.wait_ge(cand_ready, it + 1)
                    for t in by_dve:
                        i = t - TSEL
                        c.add(nc.vector.tensor_scalar(m.junk[:, joff(t):joff(t) + P * (t + 1)], m.pen[:, t, 0:P * (t + 1)],
                                                      m.candf[:, i:i + 1], 0.0, ALU.is_lt, ALU.add,
                                                      accum_out=m.count[:, i:i + 1]))
                    dve.wait_ge(act_counted, (it + 1) * len(by_act))
                    c.hold()
                    c.link(nc.vector.tensor_tensor(m.few[:], m.count[:], m.want[:, 0, :], ALU.is_lt))
                    c.link(nc.vector.tensor_tensor(m.biti[:], m.few[:], m.bitf[:], ALU.mult))
                    c.add(nc.vector.tensor_tensor(m.thr[:], m.thr[:], m.biti[:], ALU.bitwise_or))
                    c.link(nc.vector.tensor_scalar(m.bitf[:], m.bitf[:], 0.5, None, ALU.mult))
                    c2 = Chain(dve, start_ready, it)
                    c2.link(nc.vector.tensor_copy(m.biti[:], m.bitf[:]))
                    nc.vector.tensor_tensor(m.cand[:], m.thr[:], m.biti[:], ALU.bitwise_or).then_inc(cand_ready, 1)
                    assert c.n == per
                ch = Chain(dve, chs, base + NB * per)
                for t in tiles:
                    i = t - TSEL
                    ch.add(nc.vector.tensor_scalar(m.junk[:, joff(t):joff(t) + P * (t + 1)], m.pen[:, t, 0:P * (t + 1)],
                                                   m.thrf[:, i:i + 1], 0.0, ALU.is_le, ALU.add,
                                                   accum_out=m.count[:, i:i + 1]))
                ch.hold()
                ch.link(nc.vector.tensor_tensor(m.biti[:], m.count[:], m.want[:, 1, :], ALU.is_lt))
                ch.link(nc.vector.tensor_tensor(m.thr[:], m.thr[:], m.biti[:], ALU.add))
                for t in tiles:
                    i = t - TSEL
                    w = P * (t + 1)
                    pen, thr = m.pen[:, t, 0:w], m.thrf[:, i:i + 1]
                    same, keep = m.past[:, 0:w], m.srelu[:, 0, 0:w]
                    ch.add(nc.vector.tensor_scalar(keep, pen, thr, 0.0, ALU.is_lt, ALU.add,
                                                   accum_out=m.count[:, i:i + 1]))
                    ch.link(nc.vector.tensor_scalar(same, pen, thr, None, ALU.is_equal))
                    ch.add(nc.vector.tensor_tensor_scan(m.srelu[:, 1, 0:w], bcast(m.ones[:, 0:1], P, w), same, 0.0,
                                                        ALU.mult, ALU.add))
                    ch.link(nc.vector.tensor_tensor(m.need[:, i:i + 1], m.want[:, 1, i:i + 1], m.count[:, i:i + 1],
                                                    ALU.subtract))
                    ch.link(nc.vector.scalar_tensor_tensor(out=same, in0=m.srelu[:, 1, 0:w], scalar=m.need[:, i:i + 1],
                                                           in1=same, op0=ALU.is_le, op1=ALU.mult))
                    ch.link(nc.vector.tensor_tensor(keep, keep, same, ALU.add))
                    ch.link(nc.vector.tensor_tensor(keep[:, t * P:w], keep[:, t * P:w], m.ident[:], ALU.max))
                    ch.link(nc.vector.tensor_scalar(keep, keep, -BIG, BIG, ALU.mult, ALU.add))
                    ch.link(nc.vector.tensor_tensor(pen, pen, keep, ALU.max))




def attention_stage(nc, m, qkv_packs):
    U = 2 * NT
    with signals(nc, "pack_in proj_done proj_ready scores_done shifted probs_ready turned_a turned_b "
                     "evac_a evac_d values_done y_ready yt_done yt_ready ch vproj_ready keys_ready padded") as (
            pack_in, proj_done, proj_ready, scores_done, shifted, probs_ready, turned_a, turned_b,
            evac_a, evac_d, values_done, y_ready, yt_done, yt_ready, chs, vproj_ready, keys_ready, padded):
        groups = []
        for u in range(U):
            t = u // 2
            for g0 in range(0, t + 1, 4):
                groups.append((u, g0, min(t + 1, g0 + 4)))
        NG = len(groups)
        of = {u: [g for g in range(NG) if groups[g][0] == u] for u in range(U)}
        act_g = [g for g in range(NG) if g % 2 == 0]
        dve_g = [g for g in range(NG) if g % 2 == 1]
        NA, NDV = len(act_g), len(dve_g)

        def copied(eng, g, it, prev=False):
            if g < 0:
                return
            if g % 2 == 0:
                eng.wait_ge(evac_a, it * NA + act_g.index(g) + 1)
            else:
                eng.wait_ge(evac_d, it * NDV + dve_g.index(g) + 1)

        SB, GB = [0, 2], [4, 5]
        YB, YTB = 6, 7
        with nc.Block() as block:
            @block.sync
            def _(sp):
                sp.dma_start(m.wst[:], qkv_packs[0]).then_inc(pack_in, 16)
                with sp.Fori(1, PAIRS) as it:
                    sp.wait_ge(proj_done, it * 6)
                    sp.dma_start(m.wst[:], qkv_packs[ds(it, 1)].rearrange("o p n -> (o p) n")).then_inc(pack_in, 16)

            @block.tensor
            def _(pe):
                pe.wait_ge(padded, 2)
                def queries_keys(pair):
                    pe.wait_ge(pack_in, pair * 16 + 16)
                    for j in range(2):
                        for half in range(2):
                            nc.tensor.matmul(m.ps[:, 2 * j + half, :], m.wst[:, j * P:(j + 1) * P],
                                             m.xnT[:, half * HALF:(half + 1) * HALF], start=True,
                                             stop=True).then_inc(proj_done, 1)

                def values_in():
                    for t in range(NT):
                        ins = nc.tensor.matmul(m.ps[:, 4 + t // 4, (t % 4) * P:(t % 4 + 1) * P],
                                               m.xnT[:, t * P:(t + 1) * P], m.wst[:, 2 * P:3 * P], start=True, stop=True)
                        if t % 4 == 3:
                            ins.then_inc(proj_done, 1)

                def scores(it, u):
                    t, h = u // 2, u % 2
                    w = P * (t + 1)
                    if u >= 2:
                        pe.wait_ge(shifted, it * U + u - 1)
                    for a in range(0, w, HALF):
                        b = min(w, a + HALF)
                        ins = nc.tensor.matmul(m.ps[:, SB[h] + a // HALF, 0:b - a],
                                               m.qT[:, h, t * P:(t + 1) * P], m.kT[:, a:b], start=True, stop=True)
                    ins.then_inc(scores_done, 1)

                def first_scores(it):
                    pe.wait_ge(proj_ready, it * 2 + 2)
                    pe.wait_ge(keys_ready, it * 2 + 2)
                    scores(it, 0)
                    scores(it, 1)

                def pair_turn(it, more):
                    def turn(u):
                        h = u % 2
                        pe.wait_ge(probs_ready, it * U + u + 1)
                        if u == 0:
                            pe.wait_ge(vproj_ready, it * 2 + 2)
                        for g in of[u]:
                            copied(pe, g - 2, it)
                            _, k0, k1 = groups[g]
                            for k in range(k0, k1):
                                ins = nc.tensor.transpose(m.ps[:, GB[g % 2], (k - k0) * P:(k - k0 + 1) * P],
                                                          m.prob[:, u % 4, k * P:(k + 1) * P], m.ident[:])
                            ins.then_inc(turned_a if g % 2 == 0 else turned_b, 1)

                    def values(u):
                        t, h = u // 2, u % 2
                        for g in of[u]:
                            copied(pe, g, it)
                        if u >= 1:
                            pe.wait_ge(y_ready, it * U + u)
                        for k in range(t + 1):
                            ins = nc.tensor.matmul(m.ps[:, YB, 0:HD0], m.pT[:, h, k, :],
                                                   m.v[:, k, h * HD0:(h + 1) * HD0], start=(k == 0), stop=(k == t))
                        ins.then_inc(values_done, 1)

                    def turn_y(t):
                        pe.wait_ge(y_ready, it * U + 2 * t + 2)
                        pe.wait_ge(yt_ready, it * NT + t + 1)
                        nc.tensor.transpose(m.ps[:, YTB, 0:P], m.y[:, t % 2, :], m.ident[:]).then_inc(yt_done, 1)

                    for n in range(2, U + 4):
                        if n < U:
                            scores(it, n)
                        if 0 <= n - 2 < U:
                            turn(n - 2)
                        if 0 <= n - 3 < U:
                            values(n - 3)
                        if n == U and more:
                            pe.wait_ge(shifted, it * U + U)
                            queries_keys(it + 1)
                        if n == U + 2 and more:
                            values_in()
                        if n >= 5 and n % 2 == 1:
                            turn_y((n - 5) // 2)
                    if more:
                        first_scores(it + 1)

                queries_keys(0)
                values_in()
                first_scores(0)
                with pe.Fori(0, PAIRS - 1) as it:
                    pair_turn(it, True)
                pair_turn(PAIRS - 1, False)

            @block.vector
            def _(dve):
                nc.vector.memset(m.qT[HD0:P, 0, :], 0.0).then_inc(padded, 1)
                nc.vector.memset(m.qT[0:HD0, 1, :], 0.0).then_inc(padded, 1)
                def queries(pair):
                    for half in range(2):
                        dve.wait_ge(proj_done, pair * 6 + half + 1)
                        for h in range(2):
                            r = slice(h * HD0, (h + 1) * HD0)
                            ins = nc.vector.tensor_scalar(m.qT[r, h, half * HALF:(half + 1) * HALF], m.ps[r, half, :],
                                                          m.qkvb[r, ds(pair * 3, 1)], -1.0 / 8, ALU.add, ALU.mult)
                        ins.then_inc(proj_ready, 1)

                def shift(it, u):
                    t, h = u // 2, u % 2
                    w = P * (t + 1)
                    if u >= 4:
                        for g in of[u - 4]:
                            dve.wait_ge(turned_a if g % 2 == 0 else turned_b,
                                        it * (NA if g % 2 == 0 else NDV) + (act_g if g % 2 == 0 else dve_g).index(g) + 1)
                    count = dve.to_reg(it * U + u + 1)
                    dve.wait_ge(keys_ready, 2)
                    dve.wait_ge(scores_done, count)
                    nc.vector.tensor_tensor_reduce(m.prob[:, u % 4, 0:w], m.psf[:, SB[h] * HALF:SB[h] * HALF + w],
                                                   m.pen[:, t, 0:w], 1.0, 3.0e38, ALU.add, ALU.min,
                                                   m.nmax[:, u % 4:u % 4 + 1]).then_inc(shifted, 1)

                def pair_turn(it, more):
                    c = Chain(dve, chs, it * U)

                    def evac(u):
                        for g in of[u]:
                            if g % 2 == 1:
                                _, k0, k1 = groups[g]
                                dve.wait_ge(turned_b, it * NDV + dve_g.index(g) + 1)
                                if u >= 2:
                                    dve.wait_ge(values_done, it * U + u - 1)
                                nc.vector.tensor_copy(m.pT[:, u % 2, k0:k1, :].rearrange("p k q -> p (k q)"),
                                                      m.ps[:, GB[1], 0:(k1 - k0) * P]).then_inc(evac_d, 1)

                    def finish(u):
                        t, h = u // 2, u % 2
                        dve.wait_ge(values_done, it * U + u + 1)
                        c.link(nc.vector.reciprocal(m.rsum[:, h:h + 1], m.esum[:, u % 8:u % 8 + 1]))
                        if t >= 2:
                            dve.wait_ge(yt_done, it * NT + t - 1)
                        nc.vector.tensor_scalar(m.y[:, t % 2, h * HD0:(h + 1) * HD0], m.ps[:, YB, 0:HD0],
                                                m.rsum[:, h:h + 1], None, ALU.mult).then_inc(y_ready, 1)

                    for n in range(2, U + 3):
                        if n < U:
                            shift(it, n)
                        if 0 <= n - 2 < U:
                            evac(n - 2)
                        if 0 <= n - 3 < U:
                            finish(n - 3)
                        if n == U and more:
                            queries(it + 1)
                    assert c.n == U
                    if more:
                        shift(it + 1, 0)
                        shift(it + 1, 1)

                queries(0)
                shift(0, 0)
                shift(0, 1)
                with dve.Fori(0, PAIRS - 1) as it:
                    pair_turn(it, True)
                pair_turn(PAIRS - 1, False)

            @block.scalar
            def _(act):
                act.sem_inc(yt_ready, 1)

                def keys(pair):
                    for half in range(2):
                        count = act.to_reg(pair * 6 + half + 3)
                        act.wait_ge(pack_in, 16)
                        act.wait_ge(proj_done, count)
                        nc.scalar.activation(m.kT[:, half * HALF:(half + 1) * HALF], m.ps[:, 2 + half, :], ACT.Identity,
                                             bias=m.qkvb[:, ds(pair * 3 + 1, 1)]).then_inc(keys_ready, 1)

                def values_out(pair):
                    for half in range(2):
                        act.wait_ge(proj_done, pair * 6 + 5 + half)
                        nc.scalar.activation(m.v[:, 4 * half:4 * half + 4, :].rearrange("p t c -> p (t c)"),
                                             m.ps[:, 4 + half, :], ACT.Copy).then_inc(vproj_ready, 1)

                def exp(it, u):
                    t, h = u // 2, u % 2
                    w = P * (t + 1)
                    act.wait_ge(shifted, it * U + u + 1)
                    if u >= 8:
                        act.wait_ge(y_ready, it * U + u - 7)
                    nc.scalar.activation(m.prob[:, u % 4, 0:w], m.prob[:, u % 4, 0:w], ACT.Exp,
                                         bias=m.nmax[:, u % 4:u % 4 + 1],
                                         scale=-1.0, accum_out=m.esum[:, u % 8:u % 8 + 1]).then_inc(probs_ready, 1)

                def pair_turn(it, more):
                    def evac(u):
                        for g in of[u]:
                            if g % 2 == 0:
                                _, k0, k1 = groups[g]
                                act.wait_ge(turned_a, it * NA + act_g.index(g) + 1)
                                if u >= 2:
                                    act.wait_ge(values_done, it * U + u - 1)
                                nc.scalar.activation(m.pT[:, u % 2, k0:k1, :].rearrange("p k q -> p (k q)"),
                                                     m.ps[:, GB[0], 0:(k1 - k0) * P], ACT.Copy).then_inc(evac_a, 1)

                    def out_y(t):
                        act.wait_ge(yt_done, it * NT + t + 1)
                        ins = nc.scalar.activation(m.yT[:, ds(it, 1), t * P:(t + 1) * P].rearrange("p o q -> p (o q)"),
                                                   m.ps[:, YTB, 0:P], ACT.Identity,
                                                   bias=m.qkvb[:, ds(it * 3 + 2, 1)])
                        ins.then_inc(yt_ready, 1)

                    for n in range(2, U + 4):
                        if 0 <= n - 2 < U:
                            evac(n - 2)
                        if n < U:
                            exp(it, n)
                        if n == U and more:
                            keys(it + 1)
                        if n == U + 2 and more:
                            act.wait_ge(values_done, it * U + U)
                            values_out(it + 1)
                        if n >= 5 and n % 2 == 1:
                            out_y((n - 5) // 2)
                    if more:
                        exp(it + 1, 0)
                        exp(it + 1, 1)

                keys(0)
                values_out(0)
                exp(0, 0)
                exp(0, 1)
                with act.Fori(0, PAIRS - 1) as it:
                    pair_turn(it, True)
                pair_turn(PAIRS - 1, False)


def project_stage(nc, m):
    with signals(nc, "proj_done sum_ready turned added") as (proj_done, sum_ready, turned, added):
        with nc.Block() as block:
            @block.tensor
            def _(pe):
                for half in range(2):
                    for p in range(PAIRS):
                        ins = nc.tensor.matmul(m.ps[:, half, :], m.wprojT[:, p, :],
                                               m.yT[:, p, half * HALF:(half + 1) * HALF],
                                               start=(p == 0), stop=(p == PAIRS - 1))
                    ins.then_inc(proj_done, 1)
                for t in range(NT):
                    pe.wait_ge(sum_ready, t // 4 + 1)
                    nc.tensor.transpose(m.ps[:, 2 + t // 4, (t % 4) * P:(t % 4 + 1) * P],
                                        m.ffnT[:, t * P:(t + 1) * P], m.ident[:]).then_inc(turned, 1)

            @block.vector
            def _(dve):
                for half in range(2):
                    dve.wait_ge(proj_done, half + 1)
                    f = m.ffnT[:, half * HALF:(half + 1) * HALF]
                    nc.vector.scalar_tensor_tensor(out=f, in0=m.ps[:, half, :], scalar=m.bproj[:, 0:1], in1=f,
                                                   op0=ALU.add, op1=ALU.add).then_inc(sum_ready, 1)
                for half in range(2):
                    dve.wait_ge(turned, 4 * half + 4)
                    xs = m.x[:, 4 * half:4 * half + 4, :].rearrange("p t c -> p (t c)")
                    nc.vector.tensor_tensor(xs, m.ps[:, 2 + half, :], xs, ALU.add).then_inc(added, 1)




def delta_prepare_stage(nc, m):
    with signals(nc, "sq_ready ss_ready root_ready xr_ready proj_done xv_ready beta_ready gate_ready xr_turned "
                     "wk_ready abs_ready e_ready decay_ready dec_done decE_done dec_ready decE_ready decT_done "
                     "decT_ready exp_ready conv_ready silu_ready diff_ready rest_ready vb_ready wkbd_ready "
                     "kd_ready rk_ready turned evac_done pad_ready ch") as (
            sq_ready, ss_ready, root_ready, xr_ready, proj_done, xv_ready, beta_ready, gate_ready, xr_turned,
            wk_ready, abs_ready, e_ready, decay_ready, dec_done, decE_done, dec_ready, decE_ready, decT_done,
            decT_ready, exp_ready, conv_ready, silu_ready, diff_ready, rest_ready, vb_ready, wkbd_ready,
            kd_ready, rk_ready, turned, evac_done, pad_ready, chs):
        halves = [(h, slice(h * HALF, (h + 1) * HALF)) for h in range(2)]
        NH = NT * H1
        with nc.Block() as block:
            @block.gpsimd
            def _(pool):
                nc.gpsimd.memset(m.wk[:, 0:1], 0.0).then_inc(pad_ready, 1)
                nc.gpsimd.memset(m.xv[:, 0:3], 0.0).then_inc(pad_ready, 1)
                pool.wait_ge(rk_ready, 1)
                pool.wait_ge(exp_ready, 2)
                nc.gpsimd.tensor_tensor(m.rkd, m.rk, m.grow, ALU.mult).then_inc(rk_ready, 1)
                pool.wait_ge(rest_ready, 1)
                nc.gpsimd.tensor_tensor(m.kdT, m.wk[:, 0:T], m.resto, ALU.mult).then_inc(kd_ready, 1)

            @block.tensor
            def _(pe):
                for h, s in halves:
                    nc.tensor.matmul(m.ps[:, h, :], m.wvT[:], m.xnT[:, s], start=True, stop=True).then_inc(proj_done, 1)
                for h, s in halves:
                    nc.tensor.matmul(m.ps[:, 2 + h, :], m.wbT16[:], m.xnT[:, s], start=True,
                                     stop=True).then_inc(proj_done, 1)
                for t in range(NT):
                    ins = nc.tensor.matmul(m.ps[:, 4, t * H1:(t + 1) * H1], m.xnT[:, t * P:(t + 1) * P], m.waT[:],
                                           start=True, stop=True)
                ins.then_inc(proj_done, 1)
                for t in range(NT):
                    ins = nc.tensor.matmul(m.ps[:, 5 + t // 4, (t % 4) * P:(t % 4 + 1) * P], m.xnT[:, t * P:(t + 1) * P],
                                           m.wgT[:], start=True, stop=True)
                    if t % 4 == 3:
                        ins.then_inc(proj_done, 1)
                for t in range(NT):
                    pe.wait_ge(xr_ready, t // 4 + 1)
                    if t == 4:
                        pe.wait_ge(xv_ready, 1)
                    ins = nc.tensor.transpose(m.ps[:, 7 if t < 4 else 0, (t % 4) * P:(t % 4 + 1) * P], m.xr[:, t, :],
                                              m.ident[:])
                    if t % 4 == 3:
                        ins.then_inc(xr_turned, 1)
                pe.wait_ge(decay_ready, 1)
                nc.tensor.matmul(m.ps[:, 4, 0:NH], m.chunk_upto[:], m.decay[:], start=True, stop=True).then_inc(dec_done, 1)
                pe.wait_ge(gate_ready, 2)
                for t in range(NT):
                    ins = nc.tensor.matmul(m.ps[:, 5 + t // 4, (t % 4) * P:(t % 4 + 1) * P], m.decay16[:, t, :],
                                           m.chunk_upto[:], start=True, stop=True)
                    if t % 4 == 3:
                        ins.then_inc(decE_done, 1)
                pe.wait_ge(dec_ready, 1)
                pe.wait_ge(beta_ready, 2)
                for t in range(NT):
                    ins = nc.tensor.transpose(m.ps[0:H1, 2 + t // 4, (t % 4) * P:(t % 4 + 1) * P],
                                              m.dec[:, t * H1:(t + 1) * H1], m.ident[:])
                ins.then_inc(decT_done, 1)
                pe.wait_ge(wk_ready, 2)
                pe.wait_ge(xv_ready, 2)
                pe.wait_ge(decT_ready, 2)
                pe.wait_ge(exp_ready, 2)
                for src, ready, bank in ((m.vb, vb_ready, 0), (m.wkbd, wkbd_ready, 2), (m.kdT, kd_ready, 5)):
                    pe.wait_ge(ready, 1)
                    for t in range(NT):
                        ins = nc.tensor.transpose(m.ps[:, bank + t // 4, (t % 4) * P:(t % 4 + 1) * P],
                                                  src[:, t * P:(t + 1) * P], m.ident[:])
                        if t % 4 == 3:
                            ins.then_inc(turned, 1)

            @block.scalar
            def _(act):
                nc.scalar.activation(m.sq, m.xn[:].rearrange("p t c -> p (t c)"), ACT.Square).then_inc(sq_ready, 1)
                act.wait_ge(ss_ready, 1)
                nc.scalar.activation(m.rn[:], m.rn[:], ACT.Sqrt).then_inc(root_ready, 1)
                for h, s in halves:
                    act.wait_ge(proj_done, 1 + h)
                    nc.scalar.activation(m.xv[:, 3 + h * HALF:3 + (h + 1) * HALF], m.ps[:, h, :],
                                         ACT.Copy).then_inc(xv_ready, 1)
                for h, s in halves:
                    act.wait_ge(proj_done, 3 + h)
                    nc.scalar.activation(m.beta[:, s], m.ps[:, 2 + h, :], ACT.Sigmoid).then_inc(beta_ready, 1)
                for h, s in halves:
                    act.wait_ge(proj_done, 6 + h)
                    nc.scalar.activation(m.gate[:, 4 * h:4 * h + 4, :].rearrange("p t c -> p (t c)"),
                                         m.ps[:, 5 + h, :], ACT.Silu).then_inc(gate_ready, 1)
                for h, s in halves:
                    act.wait_ge(xr_turned, 1 + h)
                    nc.scalar.activation(m.wk[:, 1 + h * HALF:1 + (h + 1) * HALF] if h == 0 else
                                         m.wk[:, 1 + HALF:1 + T], m.ps[:, 7 if h == 0 else 0, :],
                                         ACT.Copy).then_inc(wk_ready, 1)
                act.wait_ge(conv_ready, 1)
                nc.scalar.activation(m.vb, m.vb, ACT.Silu).then_inc(silu_ready, 1)
                act.wait_ge(abs_ready, 1)
                nc.scalar.activation(m.e64[:], m.e64[:], ACT.Exp, scale=-1.0).then_inc(e_ready, 1)
                for h, s in halves:
                    act.wait_ge(decE_done, 1 + h)
                    nc.scalar.activation(m.decE[:, s], m.ps[:, 5 + h, :], ACT.Copy).then_inc(decE_ready, 1)
                for h, s in halves:
                    nc.scalar.activation(m.grow[:, s], m.ps[:, 5 + h, :], ACT.Exp).then_inc(exp_ready, 1)
                act.wait_ge(decE_ready, 2)
                nc.scalar.activation(m.sdecay[:], m.decE.rearrange("p (n c) -> p n c", c=C1)[:, :, C1 - 1],
                                     ACT.Exp).then_inc(exp_ready, 1)
                act.wait_ge(decT_done, 1)
                for h, s in halves:
                    nc.scalar.activation(m.decT[:, s], m.ps[0:H1, 2 + h, :], ACT.Copy).then_inc(decT_ready, 1)
                act.wait_ge(diff_ready, 1)
                nc.scalar.activation(m.resto, m.resto, ACT.Exp).then_inc(rest_ready, 1)
                for h in range(2):
                    act.wait_ge(turned, 5 + h)
                    nc.scalar.activation(m.kd[:, 4 * h:4 * h + 4, :].rearrange("p t c -> p (t c)"), m.ps[:, 5 + h, :],
                                         ACT.Copy).then_inc(evac_done, 1)

            @block.vector
            def _(dve):
                ch = Chain(dve, chs)
                dve.wait_ge(sq_ready, 1)
                ch.link(nc.vector.tensor_reduce(m.rn[:], m.sq.rearrange("p (n k) -> p n k", k=K1), AX, ALU.add))
                nc.vector.tensor_scalar(m.rn[:], m.rn[:], EPS_L2, None, ALU.add).then_inc(ss_ready, 1)
                dve.wait_ge(root_ready, 1)
                ch.link(nc.vector.reciprocal(m.rn[:], m.rn[:]))
                for h in range(2):
                    v = lambda z: z[:, 4 * h:4 * h + 4, :].rearrange("p t (g k) -> p (t g) k", k=K1)
                    nc.vector.tensor_tensor(v(m.xr), v(m.xn), bcast(m.rn[:, h * NH // 2:(h + 1) * NH // 2].unsqueeze(2),
                                                                   P, NH // 2, K1), ALU.mult).then_inc(xr_ready, 1)
                dve.wait_ge(proj_done, 5)
                ch.link(nc.vector.tensor_tensor(m.z64[:].rearrange("p (t h) -> p t h", h=H1),
                                                m.ps[:, 4, 0:NH].rearrange("p (t h) -> p t h", h=H1),
                                                bcast(m.dtb[:].unsqueeze(1), P, NT, H1), ALU.add))
                nc.vector.scalar_tensor_tensor(out=m.e64[:], in0=m.z64[:], scalar=-1.0, in1=m.z64[:], op0=ALU.mult,
                                               op1=ALU.max).then_inc(abs_ready, 1)
                dve.wait_ge(xv_ready, 2)
                dve.wait_ge(pad_ready, 2)
                ch.link(nc.vector.tensor_scalar(m.vb, m.xv[:, 0:T], m.convw[:, 0:1], m.convw[:, 4:5], ALU.mult, ALU.add))
                for j in range(1, 4):
                    ins = nc.vector.scalar_tensor_tensor(out=m.vb, in0=m.xv[:, j:j + T], scalar=m.convw[:, j:j + 1],
                                                         in1=m.vb, op0=ALU.mult, op1=ALU.add)
                    if j < 3:
                        ch.link(ins)
                    else:
                        ins.then_inc(conv_ready, 1)
                dve.wait_ge(e_ready, 1)
                e, r, r2, q = m.e64[:], m.r64[:], m.rr64[:], m.q64[:]
                ch.link(nc.vector.tensor_scalar(r, e, 2.0, None, ALU.add))
                ch.link(nc.vector.reciprocal(r, r))
                ch.link(nc.vector.tensor_tensor(r, r, e, ALU.mult))
                ch.link(nc.vector.tensor_tensor(r2, r, r, ALU.mult))
                ch.link(nc.vector.tensor_scalar(q, r2, 1.0 / 17, None, ALU.mult))
                for k in range(15, 1, -2):
                    ch.link(nc.vector.scalar_tensor_tensor(out=q, in0=q, scalar=1.0 / k, in1=r2, op0=ALU.add, op1=ALU.mult))
                ch.link(nc.vector.scalar_tensor_tensor(out=q, in0=q, scalar=1.0, in1=r, op0=ALU.add, op1=ALU.mult))
                ch.link(nc.vector.tensor_scalar(m.z64[:], m.z64[:], 0.0, None, ALU.max))
                ch.link(nc.vector.scalar_tensor_tensor(out=q, in0=q, scalar=2.0, in1=m.z64[:], op0=ALU.mult, op1=ALU.add))
                ch.link(nc.vector.tensor_tensor(m.decay[:].rearrange("p (t h) -> p t h", h=H1),
                                                q.rearrange("p (t h) -> p t h", h=H1),
                                                bcast(m.nega[:].unsqueeze(1), P, NT, H1), ALU.mult))
                nc.vector.tensor_copy(m.decay16[:].rearrange("p t (h k) -> p (t h) k", k=K1),
                                      bcast(m.decay[:].unsqueeze(2), P, NH, K1)).then_inc(decay_ready, 1)
                dve.wait_ge(dec_done, 1)
                nc.vector.tensor_copy(m.dec[:], m.ps[:, 4, 0:NH]).then_inc(dec_ready, 1)
                dve.wait_ge(wk_ready, 2)
                nc.vector.tensor_scalar(m.rk, m.wk[:, 1:1 + T], 1.0 / K1 ** 0.5, None, ALU.mult).then_inc(rk_ready, 1)
                dve.wait_ge(beta_ready, 2)
                ch.link(nc.vector.tensor_tensor(m.wkb, m.wk[:, 0:T], m.beta, ALU.mult))
                dve.wait_ge(silu_ready, 1)
                nc.vector.tensor_tensor(m.vb, m.vb, m.beta, ALU.mult).then_inc(vb_ready, 1)
                dve.wait_ge(exp_ready, 2)
                nc.vector.tensor_tensor(m.wkbd, m.wkb, m.grow, ALU.mult).then_inc(wkbd_ready, 1)
                dve.wait_ge(decE_ready, 2)
                dv = m.decE.rearrange("p (n c) -> p n c", c=C1)
                ch.link(nc.vector.tensor_tensor(m.resto.rearrange("p (n c) -> p n c", c=C1),
                                                bcast(dv[:, :, C1 - 1:C1], P, NC1, C1), dv, ALU.subtract))
                nc.vector.tensor_scalar(m.resto, m.resto, 0.0, None, ALU.min).then_inc(diff_ready, 1)
                for i, off in ((0, 0), (1, 0), (2, K1), (3, K1)):
                    dve.wait_ge(turned, i + 1)
                    h = i % 2
                    for t in range(4):
                        nc.vector.tensor_copy(m.rhs[:, 4 * h + t, :, off:off + K1],
                                              m.ps[:, (0 if off == 0 else 2) + h, t * P:(t + 1) * P].rearrange(
                                                  "p (g k) -> p g k", k=K1)).then_inc(evac_done, 1)


def delta_stage(nc, m):
    LV = [2, 4, 8, 16]
    G = 4
    with signals(nc, "staged padded walk_staged state_ready dec_done gram_done diff_ready lt_ready lmask_ready nt_ready "
                     "xt_ready x_turned x_ready y_done ym_ready z_done x_next u_done u_ready ntm_ready w_done w_ready "
                     "v2_done solved wt_done wt_ready read_done vnew_ready o_ready upd_done s_ready oi_done out_ready ch"
                 ) as (
            staged, padded, walk_staged, state_ready, dec_done, gram_done, diff_ready, lt_ready, lmask_ready, nt_ready,
            xt_ready, x_turned, x_ready, y_done, ym_ready, z_done, x_next, u_done, u_ready, ntm_ready, w_done, w_ready,
            v2_done, solved, wt_done, wt_ready, read_done, vnew_ready, o_ready, upd_done, s_ready, oi_done, out_ready,
            chs):
        def heads(buf, g):
            return buf[:, g * G:(g + 1) * G, :]

        def bank(k, g):
            return m.ps[:, 2 * k + g, :].rearrange("p (h c) -> p h c", h=G)

        def over_heads(mask):
            return bcast(mask.unsqueeze(1), P, G, P)

        def tile(buf, it):
            return buf[:, ds(it * P, P)]

        def four(k, g, lhs, rhs, n=P):
            for h in range(G):
                ins = nc.tensor.matmul(m.ps[:, 2 * k + g, h * n:(h + 1) * n], lhs(g * G + h), rhs(g * G + h),
                                       start=True, stop=True)
            return ins

        def side(ap, l, odd):
            return ap.rearrange("p (a two s) -> p a two s", two=2, s=LV[l])[:, :, odd, :]

        WT, READ, UPD = (m.ps[:, 6, k * P:(k + 1) * P] for k in range(3))
        READO, INTRA = (m.ps[:, 7, k * P:(k + 1) * P] for k in range(2))
        with nc.Block() as block:
            @block.gpsimd
            def _(pool):
                nc.gpsimd.memset(m.state[:], 0.0).then_inc(state_ready, 1)
                pool.wait_ge(state_ready, 1)

                def stage_gram(t):
                    nc.gpsimd.tensor_copy(m.wk_t[:], tile(m.wk[:, 0:T], t)).then_inc(staged, 1)
                    nc.gpsimd.tensor_tensor(m.wkb_h[:], bcast(tile(m.wkb, t).unsqueeze(1), P, H1, P),
                                            bcast(m.hmask[:].unsqueeze(2), P, H1, P), ALU.mult).then_inc(staged, 1)
                    nc.gpsimd.tensor_tensor(m.rk_h[:], bcast(tile(m.rk, t).unsqueeze(1), P, H1, P),
                                            bcast(m.hmask[:].unsqueeze(2), P, H1, P), ALU.mult).then_inc(staged, 1)

                def stage_walk(t):
                    nc.gpsimd.tensor_copy(m.rkd_t[:], tile(m.rkd, t)).then_inc(walk_staged, 1)
                    nc.gpsimd.tensor_copy(m.kd_t[:], m.kd[:, ds(t, 1), :].rearrange("p o c -> p (o c)")
                                          ).then_inc(walk_staged, 1)
                    nc.gpsimd.tensor_copy(m.sd_t[:], m.sdecay[:, ds(t * 2, 2)]).then_inc(walk_staged, 1)

                def masks(t):
                    for buf, mask in ((m.lts, m.strictT[:]), (m.lti, m.chunk_upto[:])):
                        for g in range(2):
                            pool.wait_ge(lt_ready, t * 2 + g + 1)
                            nc.gpsimd.tensor_tensor(heads(buf, g), heads(m.lt, g), over_heads(mask),
                                                    ALU.mult).then_inc(lmask_ready, 1)

                def far_blocks(t):
                    for g in range(2):
                        pool.wait_ge(nt_ready, t * 2 + g + 1)
                        nc.gpsimd.tensor_tensor(heads(m.ntm, g), heads(m.nt, g), over_heads(m.levT[:, 1, :]),
                                                ALU.mult).then_inc(ntm_ready, 1)

                def turn(t, more):
                    far_blocks(t)
                    if more:
                        pool.wait_ge(gram_done, t * 2 + 2)
                        stage_gram(t + 1)
                        masks(t + 1)
                        pool.wait_ge(state_ready, 1)
                        pool.wait_ge(out_ready, t + 2)
                        stage_walk(t + 1)

                stage_gram(0)
                stage_walk(0)
                masks(0)
                with pool.Fori(0, NT - 1) as it:
                    turn(it, True)
                turn(NT - 1, False)

            @block.tensor
            def _(pe):
                pe.wait_ge(state_ready, 1)

                def decays(t, g):
                    for h in range(G):
                        ins = nc.tensor.matmul(m.ps[:, g, h * P:(h + 1) * P], m.sel8[:, g * G + h, :],
                                               m.decT[:, ds(t * P, P)], start=True, stop=True)
                    ins.then_inc(dec_done, 1)

                def gram(t, g):
                    pe.wait_ge(staged, t * 3 + 3)
                    nc.tensor.matmul(m.ps[:, 2 + g, :], m.wk_t[:],
                                     heads(m.wkb_h, g).rearrange("p h c -> p (h c)"), start=True, stop=True)
                    nc.tensor.matmul(m.ps[:, 4 + g, :], m.wk_t[:],
                                     heads(m.rk_h, g).rearrange("p h c -> p (h c)"), start=True,
                                     stop=True).then_inc(gram_done, 1)

                def turn_x(t, g):
                    pe.wait_ge(xt_ready, t * 2 + g + 1)
                    for h in range(G):
                        ins = nc.tensor.transpose(m.ps[:, g, h * P:(h + 1) * P], m.xt[:, g * G + h, :], m.ident[:])
                    ins.then_inc(x_turned, 1)

                def solve(t, more):
                    for l in range(len(LV)):
                        for g in range(2):
                            if l == 0:
                                pe.wait_ge(x_ready, t * 2 + g + 1)
                            else:
                                pe.wait_ge(x_next, t * 8 + (l - 1) * 2 + g + 1)
                            four(1, g, lambda h: m.nt[:, h, :], lambda h: m.xi[:, h, :]).then_inc(y_done, 1)
                        for g in range(2):
                            pe.wait_ge(ym_ready, t * 8 + l * 2 + g + 1)
                            if l < len(LV) - 1:
                                four(2, g, lambda h: m.xt[:, h, :], lambda h: m.ym[l][:, h, :])
                            if l == 0 and g == 0:
                                pe.wait_ge(out_ready, t + 1)
                            four(3, g, lambda h: m.ym[l][:, h, :], lambda h: m.xt[:, h, :]).then_inc(z_done, 1)
                        if more and l < 2:
                            decays(t + 1, l)
                    for g in range(2):
                        pe.wait_ge(x_next, t * 8 + 6 + g + 1)
                        four(0, g, lambda h: m.xt[:, h, :],
                             lambda h: m.rhs[:, ds(t, 1), h, :].rearrange("p o k -> p (o k)"), 2 * K1).then_inc(u_done, 1)
                    for g in range(2):
                        pe.wait_ge(u_ready, t * 2 + g + 1)
                        pe.wait_ge(ntm_ready, t * 2 + g + 1)
                        four(1, g, lambda h: m.ntm[:, h, :], lambda h: m.u[:, h, :], 2 * K1).then_inc(w_done, 1)
                    for g in range(2):
                        pe.wait_ge(w_ready, t * 2 + g + 1)
                        four(2, g, lambda h: m.xt[:, h, :], lambda h: m.w[:, h, :], 2 * K1).then_inc(v2_done, 1)

                def read_state(t, c):
                    if c:
                        pe.wait_ge(s_ready, t * 2 + c)
                        pe.wait_ge(o_ready, t * 2 + c)
                    nc.tensor.matmul(READ, m.wcT[:], m.state[:], start=True, stop=True).then_inc(read_done, 1)
                    nc.tensor.matmul(READO, m.rkd_t[:], m.state[:], start=True, stop=True).then_inc(read_done, 1)

                def update(t, c):
                    pe.wait_ge(vnew_ready, t * 2 + c + 1)
                    nc.tensor.matmul(UPD, m.kd_t[c * C1:(c + 1) * C1, :],
                                     m.vnew[c * C1:(c + 1) * C1, :], start=True, stop=True).then_inc(upd_done, 1)

                def turn(t, more):
                    solve(t, more)
                    pe.wait_ge(solved, t * 2 + 2)
                    nc.tensor.transpose(WT, m.wsol[:], m.ident[:]).then_inc(wt_done, 1)
                    if more:
                        gram(t + 1, 0)
                    pe.wait_ge(wt_ready, t + 1)
                    pe.wait_ge(walk_staged, t * 3 + 3)
                    read_state(t, 0)
                    if more:
                        gram(t + 1, 1)
                    update(t, 0)
                    if more:
                        turn_x(t + 1, 0)
                    read_state(t, 1)
                    update(t, 1)
                    if more:
                        turn_x(t + 1, 1)
                    pe.wait_ge(o_ready, t * 2 + 2)
                    for h in range(H1):
                        ins = nc.tensor.matmul(INTRA[:, h * K1:(h + 1) * K1], m.at[:, h, :],
                                               m.vnew[:, h * K1:(h + 1) * K1], start=True, stop=True)
                    ins.then_inc(oi_done, 1)

                for g in range(2):
                    decays(0, g)
                for g in range(2):
                    gram(0, g)
                for g in range(2):
                    turn_x(0, g)
                with pe.Fori(0, NT - 1) as it:
                    turn(it, True)
                turn(NT - 1, False)

            @block.scalar
            def _(act):
                def decay(t, g):
                    act.wait_ge(diff_ready, t * 2 + g + 1)
                    nc.scalar.activation(heads(m.lt, g), heads(m.lt, g), ACT.Exp).then_inc(lt_ready, 1)

                def take_x(t, g):
                    act.wait_ge(x_turned, t * 2 + g + 1)
                    nc.scalar.activation(heads(m.xi, g), bank(0, g), ACT.Copy).then_inc(x_ready, 1)

                def turn(t, more):
                    if more:
                        for g in range(2):
                            decay(t + 1, g)
                    for g in range(2):
                        act.wait_ge(u_done, t * 2 + g + 1)
                        nc.scalar.activation(heads(m.u, g).rearrange("p h k -> p (h k)"), m.ps[:, g, 0:G * 2 * K1],
                                             ACT.Copy).then_inc(u_ready, 1)
                    for g in range(2):
                        act.wait_ge(w_done, t * 2 + g + 1)
                        nc.scalar.activation(heads(m.w, g).rearrange("p h k -> p (h k)"), m.ps[:, 2 + g, 0:G * 2 * K1],
                                             ACT.Copy).then_inc(w_ready, 1)
                    act.wait_ge(wt_done, t + 1)
                    nc.scalar.activation(m.wcT[:], WT, ACT.Copy).then_inc(wt_ready, 1)
                    for c in range(2):
                        r = slice(c * C1, (c + 1) * C1)
                        act.wait_ge(read_done, t * 4 + 2 * c + 2)
                        nc.scalar.activation(m.ointer[r, :], READO[r, :], ACT.Copy).then_inc(o_ready, 1)
                        if more:
                            take_x(t + 1, c)

                for g in range(2):
                    decay(0, g)
                for g in range(2):
                    take_x(0, g)
                with act.Fori(0, NT - 1) as it:
                    turn(it, True)
                turn(NT - 1, False)

            @block.vector
            def _(dve):
                def decay(t, g, c_):
                    dve.wait_ge(dec_done, t * 2 + g + 1)
                    c_.link(nc.vector.tensor_tensor(heads(m.lt, g), bank(0, g),
                                                    bcast(m.dec[:, ds(t * H1 + g * G, G)].unsqueeze(2), P, G, P),
                                                    ALU.subtract))
                    lt = heads(m.lt, g).rearrange("p h c -> p (h c)")
                    nc.vector.tensor_scalar(lt, lt, 0.0, None, ALU.min).then_inc(diff_ready, 1)

                def systems(t, g, c_):
                    dve.wait_ge(gram_done, t * 2 + g + 1)
                    dve.wait_ge(lmask_ready, t * 4 + g + 1)
                    nc.vector.tensor_tensor(heads(m.nt, g), bank(1, g), heads(m.lts, g), ALU.mult).then_inc(nt_ready, 1)
                    dve.wait_ge(nt_ready, t * 2 + g + 1)
                    c_.link(nc.vector.tensor_tensor(heads(m.xt, g), heads(m.nt, g), over_heads(m.levT[:, 0, :]), ALU.mult))
                    nc.vector.tensor_tensor(heads(m.xt, g), over_heads(m.ident[:]), heads(m.xt, g),
                                            ALU.subtract).then_inc(xt_ready, 1)

                def intra(t, c_):
                    for g in range(2):
                        dve.wait_ge(lmask_ready, t * 4 + g + 3)
                        c_.add(nc.vector.tensor_tensor(heads(m.at, g), bank(2, g), heads(m.lti, g), ALU.mult))
                    assert c_.n == 6

                def turn(t, more):
                    c_ = Chain(dve, chs, (t + 1) * 6)
                    for l in range(len(LV)):
                        for g in range(2):
                            dve.wait_ge(y_done, t * 8 + l * 2 + g + 1)
                            s, a = LV[l], P // 2 // LV[l]
                            nc.vector.tensor_tensor(
                                heads(m.ym[l], g).rearrange("p h (a two s) -> p h a two s", two=2, s=s)[:, :, :, 0, :],
                                bank(1, g).rearrange("p h (a two s) -> p h a two s", two=2, s=s)[:, :, :, 0, :],
                                bcast(side(m.lev[:, l, :], l, 0).unsqueeze(1), P, G, a, s), ALU.mult).then_inc(ym_ready, 1)
                        for g in range(2):
                            dve.wait_ge(z_done, t * 8 + l * 2 + g + 1)
                            if l < len(LV) - 1:
                                joined = side(heads(m.xi, g).rearrange("p h c -> p (h c)"), l, 0)
                                nc.vector.tensor_tensor(joined, joined, side(m.ps[:, 4 + g, :], l, 0), ALU.subtract)
                            joined = side(heads(m.xt, g).rearrange("p h c -> p (h c)"), l, 1)
                            nc.vector.tensor_tensor(joined, joined, side(m.ps[:, 6 + g, :], l, 1), ALU.subtract).then_inc(x_next, 1)
                        if more and l < 2:
                            decay(t + 1, l, c_)
                    for g in range(2):
                        dve.wait_ge(v2_done, t * 2 + g + 1)
                        o = m.ps[:, 4 + g, 0:G * 2 * K1].rearrange("p (h k) -> p h k", k=2 * K1)
                        nc.vector.tensor_tensor(m.vsol[:].rearrange("p (h k) -> p h k", k=K1)[:, g * G:(g + 1) * G, :],
                                                heads(m.u, g)[:, :, 0:K1], o[:, :, 0:K1], ALU.subtract)
                        nc.vector.tensor_tensor(m.wsol[:].rearrange("p (h k) -> p h k", k=K1)[:, g * G:(g + 1) * G, :],
                                                heads(m.u, g)[:, :, K1:2 * K1], o[:, :, K1:2 * K1],
                                                ALU.subtract).then_inc(solved, 1)
                    dve.wait_ge(solved, t * 2 + 2)
                    for c in range(2):
                        r = slice(c * C1, (c + 1) * C1)
                        dve.wait_ge(read_done, t * 4 + 2 * c + 1)
                        nc.vector.tensor_tensor(m.vnew[r, :], m.vsol[r, :], READ[r, :], ALU.subtract).then_inc(vnew_ready, 1)
                        if more:
                            systems(t + 1, c, c_)
                        dve.wait_ge(upd_done, t * 2 + c + 1)
                        nc.vector.tensor_tensor(m.supd[:, c, :], UPD, m.bdiag[:], ALU.mult).then_inc(state_ready, 1)
                        dve.wait_ge(state_ready, t * 2 + c + 2)
                        nc.vector.scalar_tensor_tensor(out=m.state[:], in0=m.state[:], scalar=m.sd_t[:, c:c + 1],
                                                       in1=m.supd[:, c, :], op0=ALU.mult, op1=ALU.add).then_inc(s_ready, 1)
                    dve.wait_ge(oi_done, t + 1)
                    dve.wait_ge(o_ready, t * 2 + 2)
                    nc.vector.tensor_tensor(m.o[:, ds(t, 1), :].rearrange("p o c -> p (o c)"), m.ointer[:],
                                            INTRA, ALU.add).then_inc(out_ready, 1)
                    if more:
                        intra(t + 1, c_)

                for z in m.ym:
                    nc.vector.memset(z, 0.0).then_inc(padded, 1)
                dve.wait_ge(padded, 4)
                dve.sem_inc(out_ready, 1)
                first = Chain(dve, chs)
                for g in range(2):
                    decay(0, g, first)
                for g in range(2):
                    systems(0, g, first)
                intra(0, first)
                with dve.Fori(0, NT - 1) as it:
                    turn(it, True)
                turn(NT - 1, False)


def delta_out_stage(nc, m):
    NH = NT * H1
    with signals(nc, "sq_ready ms_ready root_ready o_ready turned oT_ready out_done added ch") as (
            sq_ready, ms_ready, root_ready, o_ready, turned, oT_ready, out_done, added, chs):
        with nc.Block() as block:
            @block.scalar
            def _(act):
                nc.scalar.activation(m.sq, m.o.rearrange("p t c -> p (t c)"), ACT.Square).then_inc(sq_ready, 1)
                act.wait_ge(ms_ready, 1)
                nc.scalar.activation(m.rn[:], m.rn[:], ACT.Sqrt).then_inc(root_ready, 1)
                for h in range(2):
                    act.wait_ge(turned, h + 1)
                    nc.scalar.activation(m.kdT[:, h * HALF:(h + 1) * HALF], m.ps[:, h, :], ACT.Copy).then_inc(oT_ready, 1)

            @block.vector
            def _(dve):
                ch = Chain(dve, chs)
                dve.wait_ge(sq_ready, 1)
                ch.link(nc.vector.tensor_reduce(m.rn[:], m.sq.rearrange("p (n k) -> p n k", k=K1), AX, ALU.add))
                nc.vector.tensor_scalar(m.rn[:], m.rn[:], 1.0 / K1, EPS_RMS, ALU.mult, ALU.add).then_inc(ms_ready, 1)
                dve.wait_ge(root_ready, 1)
                ch.link(nc.vector.reciprocal(m.rn[:], m.rn[:]))
                ov = m.o.rearrange("p t (h k) -> p (t h) k", k=K1)
                ch.link(nc.vector.tensor_tensor(ov, ov, bcast(m.rn[:].unsqueeze(2), P, NH, K1), ALU.mult))
                ch.link(nc.vector.tensor_tensor(ov, ov, bcast(m.normw[:].unsqueeze(1), P, NH, K1), ALU.mult))
                nc.vector.tensor_tensor(m.o, m.o, m.gate, ALU.mult).then_inc(o_ready, 1)
                for h in range(2):
                    dve.wait_ge(out_done, h + 1)
                    xs = m.x[:, 4 * h:4 * h + 4, :].rearrange("p t c -> p (t c)")
                    nc.vector.tensor_tensor(xs, m.ps[:, 2 + h, :], xs, ALU.add).then_inc(added, 1)

            @block.tensor
            def _(pe):
                pe.wait_ge(o_ready, 1)
                for t in range(NT):
                    ins = nc.tensor.transpose(m.ps[:, t // 4, (t % 4) * P:(t % 4 + 1) * P], m.o[:, t, :], m.ident[:])
                    if t % 4 == 3:
                        ins.then_inc(turned, 1)
                for t in range(NT):
                    pe.wait_ge(oT_ready, t // 4 + 1)
                    ins = nc.tensor.matmul(m.ps[:, 2 + t // 4, (t % 4) * P:(t % 4 + 1) * P], m.kdT[:, t * P:(t + 1) * P],
                                           m.woT[:], start=True, stop=True)
                    if t % 4 == 3:
                        ins.then_inc(out_done, 1)




def layer_prepare_stage(nc, m, a, l):
    loads = [("wqkv", "wqkv"), ("wo", "wo"), ("w1", "w1"), ("w2", "w2"), ("lgb", "lgb"), ("b1", "b1"), ("b2", "b2"),
             ("qks", "qks")]
    with signals(nc, "loaded tables_in pad_ready turned hT_ready folded") as (
            loaded, tables_in, pad_ready, turned, hT_ready, folded):
        with nc.Block() as block:
            @block.sync
            def _(sp):
                sp.dma_start(m.rope, a["rope"]).then_inc(tables_in, 16)
                for name, src in loads:
                    ap = a[src][ds(l, 1)]
                    dims = " ".join("abc"[:len(ap.shape) - 2])
                    sp.dma_start(m.named[name][:], ap.rearrange(f"o p {dims} -> (o p) {dims}")).then_inc(loaded, 16)
                sp.wait_ge(loaded, 16 * len(loads))

            @block.gpsimd
            def _(pool):
                nc.gpsimd.memset(m.kwin, 0.0).then_inc(pad_ready, 1)
                nc.gpsimd.memset(m.va[:, 0, :], 0.0).then_inc(pad_ready, 1)
                nc.gpsimd.memset(m.pw[:, :, 0:P - WIN], 0.0).then_inc(pad_ready, 1)
                pool.wait_ge(tables_in, 16)
                pool.wait_ge(loaded, 16 * len(loads))
                for j in range(4):
                    nc.gpsimd.tensor_tensor(m.rope[:, j, :, :], m.rope[:, j, :, :],
                                            bcast(m.qks[:, j, :].unsqueeze(1), P, NT, HD2), ALU.mult).then_inc(folded, 1)
                pool.wait_ge(folded, 4)

            @block.vector
            def _(dve):
                nc.vector.memset(m.hT[P // 2:P, 0:1], 0.0).then_inc(pad_ready, 1)

            @block.tensor
            def _(pe):
                for t in range(NT):
                    ins = nc.tensor.transpose(m.ps[:, t // 4, (t % 4) * P:(t % 4 + 1) * P], m.hc[:, t, :], m.ident[:])
                    if t % 4 == 3:
                        ins.then_inc(turned, 1)

            @block.scalar
            def _(act):
                for h in range(2):
                    act.wait_ge(turned, h + 1)
                    nc.scalar.activation(m.hT[0:P // 2, h * HALF:(h + 1) * HALF], m.ps[0:P // 2, h, :],
                                         ACT.Copy).then_inc(hT_ready, 1)
                    nc.scalar.activation(m.hT[P // 2:P, 1 + h * HALF:1 + (h + 1) * HALF], m.ps[P // 2:P, h, :],
                                         ACT.Copy).then_inc(hT_ready, 1)


def window_stage(nc, m):
    with signals(nc, "staged qkv_done sq_ready ss_ready root_ready prod_ready v_ready rot_ready qk_turned qT_ready "
                     "kT_ready scores_done shifted probs_ready p_turned evac_a evac_d values_done y_ready "
                     "o_turned oT_ready wo_done hc_ready ch rn_ready window_moved band_ready padded") as (
            staged, qkv_done, sq_ready, ss_ready, root_ready, prod_ready, v_ready, rot_ready, qk_turned, qT_ready,
            kT_ready, scores_done, shifted, probs_ready, p_turned, evac_a, evac_d, values_done, y_ready,
            o_turned, oT_ready, wo_done, hc_ready, chs, rn_ready, window_moved, band_ready, padded):
        HD = HD2 // 2
        with nc.Block() as block:
            @block.gpsimd
            def _(pool):
                nc.gpsimd.tensor_copy(m.band_t[:], m.band[:, 0, :]).then_inc(band_ready, 1)
                pairs = m.qT_t.rearrange("p (a b) q -> p a b q", b=2)
                pool.wait_ge(band_ready, 1)
                nc.gpsimd.memset(pairs[HD2:P, :, 0, :], 0.0).then_inc(padded, 1)
                pool.wait_ge(padded, 1)
                nc.gpsimd.memset(pairs[0:HD2, :, 1, :], 0.0).then_inc(padded, 1)
                with pool.Fori(0, NT) as it:
                    nc.gpsimd.tensor_copy(m.kwin[:, :, 0:WIN], m.kwin[:, :, P:KW]).then_inc(window_moved, 1)
                    nc.gpsimd.tensor_copy(m.hT_t[:], m.hT[:, ds(it * P, P)]).then_inc(staged, 1)
                    for j in range(2):
                        qv = m.rot[:, j, :, :]
                        pool.wait_ge(prod_ready, it * 2 + j + 1)
                        nc.gpsimd.tensor_tensor(qv, qv, m.rot2[:, j, :, :], ALU.add).then_inc(rot_ready, 1)
                        pool.wait_ge(rot_ready, it * 4 + 2 * j + 1)
                        pool.wait_ge(rn_ready, it + 1)
                        nc.gpsimd.tensor_tensor(qv, qv, bcast(m.qkn[:, j * H2:(j + 1) * H2].unsqueeze(2), P, H2, HD2),
                                                ALU.mult).then_inc(rot_ready, 1)
                    pool.wait_ge(band_ready, 1)
                    pool.wait_ge(hc_ready, it + 1)
                    nc.gpsimd.tensor_copy(m.band_t[:], m.band[:, 1, :]).then_inc(band_ready, 1)

            @block.tensor
            def _(pe):
                pe.wait_ge(padded, 2)
                with pe.Fori(0, NT) as it:
                    pe.wait_ge(staged, it + 1)
                    for j in range(3):
                        nc.tensor.matmul(m.ps[:, j, :], m.hT_t[:], m.wqkv[:, j * INNER:(j + 1) * INNER], start=True,
                                         stop=True).then_inc(qkv_done, 1)
                    for j in range(2):
                        pe.wait_ge(rot_ready, it * 4 + 2 * j + 2)
                        for p in range(4):
                            ins = nc.tensor.transpose(m.ps[:, 3 + j, p * P:(p + 1) * P],
                                                      m.rot[:, j, 2 * p:2 * p + 2, :].rearrange("p h d -> p (h d)"),
                                                      m.ident[:])
                        ins.then_inc(qk_turned, 1)
                    pe.wait_ge(qT_ready, it * 2 + 2)
                    pe.wait_ge(kT_ready, it + 1)
                    pe.wait_ge(v_ready, it + 1)

                    def scores(h):
                        if h >= 2:
                            pe.wait_ge(shifted, it * H2 + h - 1)
                        nc.tensor.matmul(m.ps[:, 5 + h % 2, 0:KW], m.qT_t[:, h, :], m.kwin[:, h // 2, :], start=True,
                                         stop=True).then_inc(scores_done, 1)

                    def copied(h):
                        pe.wait_ge(evac_a if h % 2 else evac_d, it * 4 + h // 2 + 1)

                    def turn(h):
                        pe.wait_ge(probs_ready, it * H2 + h + 1)
                        if h >= 2:
                            copied(h - 2)
                        for k in range(2):
                            ins = nc.tensor.transpose(m.ps[:, 3 + h % 2, k * P:(k + 1) * P], m.pw[:, h % 2, k * P:(k + 1) * P],
                                                      m.ident[:])
                        ins.then_inc(p_turned, 1)

                    def values(h):
                        copied(h)
                        if h >= 2:
                            pe.wait_ge(y_ready, it * H2 + h - 1)
                        for k in range(2):
                            ins = nc.tensor.matmul(m.ps[:, 7 if h % 2 else 2, 0:HD2], m.pwT[:, h % 2, k, :],
                                                   m.va[:, ds(it + k, 1), h * HD2:(h + 1) * HD2].rearrange("p o c -> p (o c)"),
                                                   start=(k == 0), stop=(k == 1))
                        ins.then_inc(values_done, 1)

                    scores(0)
                    for n in range(1, H2 + 2):
                        if n < H2:
                            scores(n)
                        if n - 1 < H2:
                            turn(n - 1)
                        if n >= 2:
                            values(n - 2)
                    pe.wait_ge(y_ready, it * H2 + H2)
                    for p in range(4):
                        ins = nc.tensor.transpose(m.ps[:, 0, p * P:(p + 1) * P], m.ow[:, p * P:(p + 1) * P], m.ident[:])
                    ins.then_inc(o_turned, 1)
                    pe.wait_ge(oT_ready, it + 1)
                    for p in range(4):
                        ins = nc.tensor.matmul(m.ps[:, 1, 0:P], m.oT[:, p * P:(p + 1) * P], m.wo[:, p, :],
                                               start=(p == 0), stop=(p == 3))
                    ins.then_inc(wo_done, 1)
                    pe.wait_ge(hc_ready, it + 1)

            @block.scalar
            def _(act):
                with act.Fori(0, NT) as it:
                    for j in range(2):
                        act.wait_ge(qkv_done, it * 3 + j + 1)
                        nc.scalar.activation(m.sqw[:, j, :], m.ps[:, j, :], ACT.Square).then_inc(sq_ready, 1)
                    act.wait_ge(qkv_done, it * 3 + 3)
                    nc.scalar.activation(m.va[:, ds(it + 1, 1), :].rearrange("p o c -> p (o c)"), m.ps[:, 2, :],
                                         ACT.Copy).then_inc(v_ready, 1)
                    act.wait_ge(ss_ready, it + 1)
                    nc.scalar.activation(m.qkn[:], m.qkn[:], ACT.Sqrt).then_inc(root_ready, 1)
                    act.wait_ge(qk_turned, it * 2 + 1)
                    for j in range(2):
                        r = slice(j * HD2, (j + 1) * HD2)
                        nc.scalar.activation(m.qT_t.rearrange("p (a b) q -> p a b q", b=2)[r, :, j, :],
                                             m.ps[r, 3, :].rearrange("p (a q) -> p a q", a=4), ACT.Copy
                                             ).then_inc(qT_ready, 1)
                    act.wait_ge(qk_turned, it * 2 + 2)
                    act.wait_ge(window_moved, it + 1)
                    nc.scalar.activation(m.kwin[:, :, WIN:KW], m.ps[:, 4, :].rearrange("p (h q) -> p h q", h=4),
                                         ACT.Copy).then_inc(kT_ready, 1)

                    def exp(h):
                        act.wait_ge(shifted, it * H2 + h + 1)
                        nc.scalar.activation(m.pw[:, h % 2, P - WIN:2 * P], m.pw[:, h % 2, P - WIN:2 * P], ACT.Exp,
                                             bias=m.nmaxw[:, h:h + 1], scale=-1.0,
                                             accum_out=m.esumw[:, h:h + 1]).then_inc(probs_ready, 1)

                    exp(0)
                    for n in range(1, H2 + 1):
                        if n < H2:
                            exp(n)
                        h = n - 1
                        if h % 2 == 1:
                            act.wait_ge(p_turned, it * H2 + h + 1)
                            if h >= 2:
                                act.wait_ge(values_done, it * H2 + h - 1)
                            nc.scalar.activation(m.pwT[:, 1, :, :].rearrange("p k q -> p (k q)"), m.ps[:, 4, 0:2 * P],
                                                 ACT.Copy).then_inc(evac_a, 1)
                    act.wait_ge(o_turned, it + 1)
                    nc.scalar.activation(m.oT, m.ps[:, 0, :], ACT.Copy).then_inc(oT_ready, 1)

            @block.vector
            def _(dve):
                PER = 1 + 4 + 1 + H2
                with dve.Fori(0, NT) as it:
                    c_ = Chain(dve, chs, it * PER)
                    for j in range(2):
                        dve.wait_ge(sq_ready, it * 2 + j + 1)
                        ins = nc.vector.tensor_reduce(m.qkn[:, j * H2:(j + 1) * H2],
                                                      m.sqw[:, j, :].rearrange("p (h d) -> p h d", h=H2), AX, ALU.add)
                        if j == 0:
                            c_.add(ins)
                        else:
                            ins.then_inc(ss_ready, 1)
                    for j in range(2):
                        src = m.ps[:, j, :].rearrange("p (h d) -> p h d", h=H2)

                        def table(i, a, b):
                            return bcast(m.rope[:, 2 * j + i, ds(it, 1), a:b], P, H2, b - a)

                        if j == 0:
                            dve.wait_ge(sq_ready, it * 2 + 2)
                        c_.add(nc.vector.tensor_tensor(m.rot[:, j, :, :], src, table(0, 0, HD2), ALU.mult))
                        c_.add(nc.vector.tensor_tensor(m.rot2[:, j, :, 0:HD], src[:, :, HD:HD2], table(1, 0, HD), ALU.mult))
                        nc.vector.tensor_tensor(m.rot2[:, j, :, HD:HD2], src[:, :, 0:HD], table(1, HD, HD2),
                                                ALU.mult).then_inc(prod_ready, 1)
                        if j == 0:
                            dve.wait_ge(root_ready, it + 1)
                            c_.link(nc.vector.tensor_scalar(m.qkn[:], m.qkn[:], 1e-12, None, ALU.max))
                            nc.vector.reciprocal(m.qkn[:], m.qkn[:]).then_inc(rn_ready, 1)

                    def shift(h):
                        if h >= 2:
                            dve.wait_ge(p_turned, it * H2 + h - 1)
                        if h == 0:
                            dve.wait_ge(band_ready, it + 1)
                        count = dve.to_reg(it * H2 + h + 1)
                        dve.wait_ge(band_ready, 1)
                        dve.wait_ge(scores_done, count)
                        nc.vector.tensor_tensor_reduce(m.pw[:, h % 2, P - WIN:2 * P], m.ps[:, 5 + h % 2, 0:KW],
                                                       m.band_t[:], 1.0, 3.0e38,
                                                       ALU.add, ALU.min, m.nmaxw[:, h:h + 1]).then_inc(shifted, 1)

                    def finish(h):
                        dve.wait_ge(values_done, it * H2 + h + 1)
                        c_.link(nc.vector.reciprocal(m.rsumw[:, h:h + 1], m.esumw[:, h:h + 1]))
                        nc.vector.tensor_scalar(m.ow[:, h * HD2:(h + 1) * HD2], m.ps[:, 7 if h % 2 else 2, 0:HD2],
                                                m.rsumw[:, h:h + 1], None, ALU.mult).then_inc(y_ready, 1)

                    shift(0)
                    for n in range(1, H2 + 2):
                        if n < H2:
                            shift(n)
                        h = n - 1
                        if h < H2 and h % 2 == 0:
                            dve.wait_ge(p_turned, it * H2 + h + 1)
                            if h >= 2:
                                dve.wait_ge(values_done, it * H2 + h - 1)
                            nc.vector.tensor_copy(m.pwT[:, 0, :, :].rearrange("p k q -> p (k q)"),
                                                  m.ps[:, 3, 0:2 * P]).then_inc(evac_d, 1)
                        if n >= 2:
                            finish(n - 2)
                    dve.wait_ge(wo_done, it + 1)
                    hv = m.hc[:, ds(it, 1), :].rearrange("p o c -> p (o c)")
                    nc.vector.tensor_tensor(hv, m.ps[:, 1, 0:P], hv, ALU.add).then_inc(hc_ready, 1)
                    assert c_.n == PER


def shift_stage(nc, m):
    U = P // 2
    with signals(nc, "shifted low_ready high_ready") as (shifted, low_ready, high_ready):
        with nc.Block() as block:
            @block.tensor
            def _(pe):
                for t in range(NT):
                    ins = nc.tensor.matmul(m.ps[:, 0, t * U:(t + 1) * U], m.late[:], m.hc[:, t, U:P], start=True,
                                           stop=(t == 0))
                    if t:
                        ins = nc.tensor.matmul(m.ps[:, 0, t * U:(t + 1) * U], m.carry[:], m.hc[:, t - 1, U:P],
                                               start=False, stop=True)
                ins.then_inc(shifted, 1)

            @block.vector
            def _(dve):
                nc.vector.tensor_copy(m.hs[:, :, 0:U], m.hc[:, :, 0:U]).then_inc(low_ready, 1)
                dve.wait_ge(shifted, 1)
                nc.vector.tensor_copy(m.hs[:, :, U:P], m.ps[:, 0, :].rearrange("p (t c) -> p t c", t=NT)).then_inc(
                    high_ready, 1)


def mlp_stage(nc, m):
    NCH = len(HCH)
    with signals(nc, "up_done gelu_ready hid_ready down_done biased added") as (
            up_done, gelu_ready, hid_ready, down_done, biased, added):
        with nc.Block() as block:
            @block.tensor
            def _(pe):
                def up(half):
                    for i, (c0, n) in enumerate(HCH):
                        if half:
                            pe.wait_ge(hid_ready, i + 1)
                        for j in range(2):
                            ins = nc.tensor.matmul(m.ps[0:n, 3 * j + i, :], m.w1[:, j * HID + c0:j * HID + c0 + n],
                                                   m.hnT[:, half * HALF:(half + 1) * HALF], start=True, stop=True)
                        ins.then_inc(up_done, 1)

                def down(half):
                    pe.wait_ge(hid_ready, NCH * (half + 1))
                    for t in range(4):
                        for i, (c0, n) in enumerate(HCH):
                            ins = nc.tensor.matmul(m.ps[:, 6 + half, t * P:(t + 1) * P], m.hidm[0:n, half, i, t * P:(t + 1) * P],
                                                   m.w2[0:n, i, :], start=(i == 0), stop=(i == NCH - 1))
                    ins.then_inc(down_done, 1)

                up(0)
                up(1)
                down(0)
                down(1)

            @block.scalar
            def _(act):
                for half in range(2):
                    for i, (c0, n) in enumerate(HCH):
                        act.wait_ge(up_done, half * NCH + i + 1)
                        nc.scalar.activation(m.gel[0:n, half, i, :], m.ps[0:n, 3 + i, :], ACT.Gelu,
                                             bias=m.b1[0:n, i, 1:2]).then_inc(gelu_ready, 1)

            @block.vector
            def _(dve):
                nc.vector.tensor_tensor(m.hc, m.hc, bcast(m.b2[:].unsqueeze(1), P, NT, D), ALU.add).then_inc(biased, 1)
                for half in range(2):
                    for i, (c0, n) in enumerate(HCH):
                        dve.wait_ge(gelu_ready, half * NCH + i + 1)
                        nc.vector.scalar_tensor_tensor(out=m.hidm[0:n, half, i, :], in0=m.ps[0:n, i, :],
                                                       scalar=m.b1[0:n, i, 0:1], in1=m.gel[0:n, half, i, :],
                                                       op0=ALU.add, op1=ALU.mult).then_inc(hid_ready, 1)
                dve.wait_ge(biased, 1)
                for half in range(2):
                    dve.wait_ge(down_done, half + 1)
                    hv = m.hc[:, 4 * half:4 * half + 4, :].rearrange("p t c -> p (t c)")
                    nc.vector.tensor_tensor(hv, m.ps[:, 6 + half, :], hv, ALU.add).then_inc(added, 1)




SBUF = {
    "ident": [P, P], "ones": [P, P], "zeros": [P, P],
    "before": [P, P],
    "below": [P, P],
    "later": [P, P],
    "want": [P, 2, NSEL],
    "gateT": [P, E0], "wprojT": [P, PAIRS, P], "bproj": [P, 1],
    "pack": [P, 2, 4 * P], "wst": [P, 3 * P], "qkvb": [P, PAIRS * 3],
    "x": [P, NT, D], "xn": [P, NT, D], "xnT": [P, T], "ffnT": [P, T],
    "bn": [P, NT, 6], "mv": [P, NT, 2], "rstd": [P, NT],
    "rs8": [P, NT], "rs8b": [P, NT], 
    "score": [P, NT, E0 + 1], "rest": [P, NT, E0], "top8": [P, NT, 8],
    "combT": [E0 + 1, T], "silu": [P, 2, HALF], "hid": [P, 2, HALF],
    "qT": [P, 2, T], "kT": [P, T], "v": [P, NT, P], "srelu": [P, 2, T], "past": [P, T],
    "pen": [P, NT, T], "bitf": [P, NSEL], "few": [P, NSEL], "count": [P, NSEL], "need": [P, NSEL],
    "prob": [P, 4, T], "nmax": [P, 4], "esum": [P, 8], "rsum": [P, 4], "pT": [P, 2, NT, P],
    "y": [P, 2, P], "yT": [P, PAIRS, T],
    "chunk_upto": [P, P],
    "strictT": [P, P],
    "bdiag": [P, P],
    "hmask": [P, H1],
    "lev": [P, 4, P],
    "levT": [P, 2, P],
    "sel8": [H1, H1, P], "wvT": [P, D], "wbT16": [P, D], "waT": [P, H1], "wgT": [P, D], "woT": [P, D],
    "dtb": [P, H1], "nega": [P, H1], "convw": [P, 5], "normw": [P, K1],
    "wk": [P, 1 + T], "xv": [P, 3 + T], "rn": [P, NT * H1], "z64": [P, NT * H1], "e64": [P, NT * H1],
    "r64": [P, NT * H1], "rr64": [P, NT * H1], "q64": [P, NT * H1], "decay": [P, NT * H1], "dec": [P, NT * H1],
    "sdecay": [P, NC1], "sd_t": [P, 2],
    "wk_t": [P, P], "rkd_t": [P, P], "kd_t": [P, P], "wcT": [P, P], "ointer": [P, P], "vnew": [P, P],
    "vsol": [P, P], "wsol": [P, P], "state": [P, P], "supd": [P, 2, P], "u": [P, H1, 2 * K1], "w": [P, H1, 2 * K1],
    "late": [P, P],
    "carry": [P, P],
    "band": [P, 2, KW],
    "band_t": [P, KW],
    "wqkv": [P, 3 * INNER], "wo": [P, 4, D], "w1": [P, 2 * HID], "w2": [P, len(HCH), D],
    "lgb": [P, 2], "b1": [P, len(HCH), 2], "b2": [P, D], "qks": [P, 4, HD2],
    "hT_t": [P, P], "qkn": [P, 2 * H2],
    "nmaxw": [P, H2], "esumw": [P, H2], "rsumw": [P, H2],
}
SBUF_INT = {"biti": [P, NSEL], "thr": [P, NSEL], "cand": [P, NSEL]}


class Memory:

    def __init__(self, named):
        self.named = named
        self.ident, self.ones, self.zeros, self.before, self.below, self.later = (
            named[n] for n in "ident ones zeros before below later".split())
        self.qkvb = named["qkvb"]
        self.want, self.gateT, self.wprojT, self.bproj, self.pack, self.wst = (
            named[n] for n in "want gateT wprojT bproj pack wst".split())
        self.x, self.xn, self.xnT, self.ffnT, self.bn, self.mv = (
            named[n] for n in "x xn xnT ffnT bn mv".split())
        self.rstd, self.rs8, self.rs8b, self.score, self.rest, self.top8 = (
            named[n] for n in "rstd rs8 rs8b score rest top8".split())
        self.combT, self.silu, self.hid, self.qT, self.kT, self.v = (
            named[n] for n in "combT silu hid qT kT v".split())
        self.srelu, self.past, self.pen, self.bitf, self.few, self.count = (
            named[n] for n in "srelu past pen bitf few count".split())
        self.need, self.prob, self.nmax, self.esum, self.rsum, self.pT = (
            named[n] for n in "need prob nmax esum rsum pT".split())
        self.y, self.yT, self.chunk_upto, self.strictT, self.bdiag, self.hmask = (
            named[n] for n in "y yT chunk_upto strictT bdiag hmask".split())
        self.lev, self.levT, self.sel8, self.wvT, self.wbT16, self.waT = (
            named[n] for n in "lev levT sel8 wvT wbT16 waT".split())
        self.wgT, self.woT, self.dtb, self.nega, self.convw, self.normw = (
            named[n] for n in "wgT woT dtb nega convw normw".split())
        self.wk, self.xv, self.rn, self.z64, self.e64, self.r64 = (
            named[n] for n in "wk xv rn z64 e64 r64".split())
        self.rr64, self.q64, self.decay, self.dec, self.sdecay, self.sd_t = (
            named[n] for n in "rr64 q64 decay dec sdecay sd_t".split())
        self.wk_t, self.rkd_t, self.kd_t, self.wcT, self.ointer, self.vnew = (
            named[n] for n in "wk_t rkd_t kd_t wcT ointer vnew".split())
        self.vsol, self.wsol, self.state, self.supd, self.u, self.w = (
            named[n] for n in "vsol wsol state supd u w".split())
        self.late, self.carry, self.band, self.band_t, self.wqkv, self.wo = (
            named[n] for n in "late carry band band_t wqkv wo".split())
        self.w1, self.w2, self.lgb, self.b1, self.b2, self.qks = (
            named[n] for n in "w1 w2 lgb b1 b2 qks".split())
        self.hT_t, self.qkn, self.nmaxw, self.esumw, self.rsumw, self.biti = (
            named[n] for n in "hT_t qkn nmaxw esumw rsumw biti".split())
        self.thr, self.cand = (
            named[n] for n in "thr cand".split())


def share_buffers(m):
    flat = {n: m.named[n][:].rearrange("p a b -> p (a b)") for n in ("pen", "yT", "srelu", "prob", "pack", "silu", "hid")}
    flat["pT"] = m.pT[:].rearrange("p a b c -> p (a b c)")

    def part(name, at, *shape):
        n = int(np.prod(shape))
        ap = flat[name][:, at:at + n]
        if len(shape) == 2:
            return ap.rearrange("p (a b) -> p a b", a=shape[0])
        if len(shape) == 4:
            return ap.rearrange("p (a b c d) -> p a b c d", a=shape[0], b=shape[1], c=shape[2])
        if len(shape) == 3:
            return ap.rearrange("p (a b c) -> p a b c", a=shape[0], b=shape[1])
        return ap

    m.junk = flat["yT"].bitcast(BF16)
    m.sq, m.vb, m.beta, m.decE, m.grow, m.wkb, m.wkbd, m.resto = (part("pen", i * T, T) for i in range(8))
    m.rk, m.rkd, m.kdT = (part("yT", i * T, T) for i in range(3))
    m.xr, m.gate, m.o = (part("yT", (3 + i) * T, NT, D) for i in range(3))
    m.rhs = part("yT", 6 * T, NT, H1, 2 * K1)
    m.kd, m.decT, m.decay16 = m.v, m.combT[0:H1, :], m.kT[:].rearrange("p (t c) -> p t c", t=NT)
    m.lt, m.lts = part("pT", 0, H1, P), part("pT", T, H1, P)
    m.lti, m.nt = part("prob", 0, H1, P), part("prob", T, H1, P)
    m.at, m.xt = part("srelu", 0, H1, P), part("srelu", T, H1, P)
    m.xi, m.wkb_h = part("silu", 0, H1, P), part("pack", 0, H1, P)
    m.ym = [part("hid", 0, H1, P), part("prob", 2 * T, H1, P), part("prob", 3 * T, H1, P),
            m.qT[:, 1, :].rearrange("p (h c) -> p h c", h=H1)]
    m.rk_h, m.ntm = (z.rearrange("p (t c) -> p t c", t=NT) for z in (m.qT[:, 0, :], m.past[:]))
    m.hc = m.ffnT[:].rearrange("p (t c) -> p t c", t=NT)
    m.hT = m.xv
    m.rope = flat["srelu"].rearrange("p (j t d) -> p j t d", j=4, t=NT)
    KE = 4 * (P + T)
    m.kwin = part("pen", 0, 4, KW)
    m.va = part("yT", 0, NT + 1, INNER)
    m.rot, m.rot2, m.sqw = part("pen", KE, 2, H2, HD2), part("pen", KE + 2 * INNER, 2, H2, HD2), part("pen", KE + 4 * INNER, 2, INNER)
    m.qT_t, m.ow, m.oT = part("yT", KE + 5 * INNER, H2, P), part("yT", KE + INNER, INNER), part("yT", KE + 2 * INNER, INNER)
    m.pw, m.pwT = part("yT", KE + 3 * INNER, 2, 2 * P), part("yT", KE + 4 * INNER, 2, 2, P)
    m.hs, m.hn, m.hnT = part("pT", 0, NT, D), part("pT", T, NT, D), m.past[:]
    m.gel, m.hidm = part("pen", 0, 2, len(HCH), HALF), part("yT", 0, 2, len(HCH), HALF)


def build(nc, a, out):
    with ExitStack() as ctx:
        named = {n: ctx.enter_context(nc.sbuf_tensor(n, shape, F32)) for n, shape in SBUF.items()}
        named.update({n: ctx.enter_context(nc.sbuf_tensor(n, shape, I32)) for n, shape in SBUF_INT.items()})
        m = Memory(named)
        m.ps = ctx.enter_context(nc.psum_tensor("ps", [P, 8, HALF], F32))
        m.psf = m.ps[:].rearrange("p b c -> p (b c)")
        share_buffers(m)
        m.candf, m.thrf = m.cand[:].bitcast(F32), m.thr[:].bitcast(F32)
        setup_stage(nc, m, a)
        with nc.Fori(0, B) as b:
            batch_row(nc, m, a, out, b)


def setup_stage(nc, m, a):
    loads = ["ident", "ones", "before", "below", "later", "want", "wprojT", "bproj", "qkvb", "chunk_upto", "strictT", "bdiag",
             "hmask", "lev", "levT", "sel8", "wvT", "wbT16", "waT", "wgT", "woT", "dtb", "nega", "convw", "normw",
             "late", "carry", "band"]
    with signals(nc, "loaded cleared gate_in sq_ready root_ready ch turned") as (
            loaded, cleared, gate_in, sq_ready, root_ready, chs, turned):
        with nc.Block() as block:
            @block.sync
            def _(sp):
                for name in loads:
                    sp.dma_start(m.named[name][:], a[name]).then_inc(loaded, 16)
                sp.dma_start(m.y[0:E0, 0, :], a["gate_w"]).then_inc(gate_in, 16)
                sp.wait_ge(loaded, 16 * len(loads))

            @block.gpsimd
            def _(pool):
                nc.gpsimd.memset(m.zeros[:], 0.0)
                nc.gpsimd.memset(m.score[:], 1.0)

            @block.scalar
            def _(act):
                act.wait_ge(loaded, 16 * len(loads))
                nc.scalar.activation(m.nega[:], m.nega[:], ACT.Exp).then_inc(cleared, 1)
                act.wait_ge(gate_in, 16)
                nc.scalar.activation(m.y[0:E0, 1, :], m.y[0:E0, 0, :], ACT.Square,
                                     accum_out=m.rs8[0:E0, 0:1]).then_inc(sq_ready, 1)
                act.wait_ge(sq_ready, 1)
                nc.scalar.activation(m.rs8b[0:E0, 0:1], m.rs8[0:E0, 0:1], ACT.Sqrt).then_inc(root_ready, 1)

            @block.vector
            def _(dve):
                ch = Chain(dve, chs)
                dve.wait_ge(root_ready, 1)
                r = m.rs8b[0:E0, 0:1]
                ch.link(nc.vector.tensor_scalar(r, r, 1e-12, None, ALU.max))
                ch.link(nc.vector.reciprocal(r, r))
                ch.link(nc.vector.tensor_scalar(m.y[0:E0, 0, :], m.y[0:E0, 0, :], r, None, ALU.mult))
                dve.wait_ge(cleared, 1)
                ch.add(nc.vector.tensor_scalar(m.nega[:], m.nega[:], -1.0, None, ALU.mult))
                dve.wait_ge(turned, 1)
                nc.vector.tensor_copy(m.gateT[:], m.ps[:, 0, 0:E0])

            @block.tensor
            def _(pe):
                pe.wait_ge(chs, 3)
                pe.wait_ge(loaded, 16 * len(loads))
                nc.tensor.transpose(m.ps[:, 0, 0:E0], m.y[0:E0, 0, :], m.ident[0:E0, 0:E0]).then_inc(turned, 1)


def copy_stage(nc, m, b):
    with nc.Block() as block:
        @block.gpsimd
        def _(pool):
            nc.gpsimd.tensor_copy(m.hc, m.xn[:])


def add_stage(nc, m):
    with nc.Block() as block:
        @block.vector
        def _(dve):
            nc.vector.tensor_tensor(m.x[:], m.x[:], m.hc, ALU.add)


def batch_row(nc, m, a, out, b):
    with signals(nc, "x_in") as (x_in,):
        with nc.Block() as block:
            @block.sync
            def _(sp):
                sp.dma_start(m.x[:], a["x"][ds(b, 1)].rearrange("o (t p) d -> p (o t) d", p=P)).then_inc(x_in, 16)
                sp.wait_ge(x_in, 16)
    norm_stage(nc, m, m.x, m.xn, m.xnT)
    experts_stage(nc, m, a["packs"])
    penalty_stage(nc, m, a["qkv_packs"])
    select_stage(nc, m)
    attention_stage(nc, m, a["qkv_packs"])
    project_stage(nc, m)
    norm_stage(nc, m, m.x, m.xn, m.xnT)
    delta_prepare_stage(nc, m)
    delta_stage(nc, m)
    delta_out_stage(nc, m)
    copy_stage(nc, m, b)
    with nc.Fori(0, DEPTH) as l:
        layer_prepare_stage(nc, m, a, l)
        window_stage(nc, m)
        shift_stage(nc, m)
        norm_stage(nc, m, m.hs, m.hn, m.hnT, m.lgb[:, 0:1], m.lgb[:, 1:2])
        mlp_stage(nc, m)
    add_stage(nc, m)
    with signals(nc, "x_out") as (x_out,):
        with nc.Block() as block:
            @block.sync
            def _(sp):
                sp.dma_start(out[ds(b, 1)].rearrange("o (t p) d -> p (o t) d", p=P), m.x[:]).then_inc(x_out, 16)
                sp.wait_ge(x_out, 16)




def shape_constants():
    i = np.arange(P)
    r, c = i[:, None], i[None, :]
    f = lambda z: np.ascontiguousarray(z, dtype=np.float32)
    row = np.arange(TSEL, NT)[None, :] * P + r
    k = np.minimum(KEEP, row + 1)
    width = (np.arange(TSEL, NT) + 1)[None, :] * P
    act = np.zeros(NSEL, bool)
    act[::-2] = True
    want = np.stack([np.where(act[None, :], 2 * k - width, k), k], axis=1)
    same = r // C1 == c // C1

    def joins(rows, cols, s):
        return same & ((rows // s) % 2 == 1) & (cols // s == rows // s - 1)

    half = np.arange(0, HD2, 2, dtype=np.float32)
    inv = (1.0 / np.float32(10000.0) ** (half / np.float32(HD2))).astype(np.float32)
    tt = np.arange(T, dtype=np.float32)
    ang = (tt[:, None] * inv[None, :]).astype(np.float32).astype(np.float64)
    grown = ((half + 0.4 * HD2) / (1.4 * HD2)).astype(np.float64)[None, :] ** ((tt.astype(np.float64) - T // 2) / (WIN // 2))[:, None]
    two = lambda z: np.concatenate([z, z], -1)
    signed = lambda z: np.concatenate([-z, z], -1)
    rope = np.stack([-8 * two(np.cos(ang) * grown), -8 * signed(np.sin(ang) * grown), two(np.cos(ang) / grown),
                     signed(np.sin(ang) / grown)])
    key = np.arange(KW)[None, None, :] - WIN
    tile = np.arange(2)[None, :, None]
    off = r[:, :, None] - key
    seen = (off >= 0) & (off <= WIN) & (tile * P + key >= 0)
    return {
        "chunk_upto": f(same & (r <= c)), "strictT": f(same & (r < c)), "bdiag": f(r // K1 == c // K1),
        "hmask": f(r // K1 == np.arange(H1)[None, :]),
        "lev": f(np.stack([joins(r, c, s) for s in (2, 4, 8, 16)], 1)),
        "levT": f(np.stack([joins(c, r, s) for s in (1, 32)], 1)),
        "sel8": f(np.broadcast_to(np.eye(H1)[:, :, None], (H1, H1, P))),
        "late": f(r == c - 1), "carry": f((r == P - 1) & (c == 0)), "band": f(np.where(seen, 0.0, BIG)),
        "rope": f(rope.reshape(4, NT, P, HD2).transpose(2, 0, 1, 3)),
        "ident": f(r == c), "ones": f(np.ones((P, P))), "before": f(r < c), "below": f(c < r),
        "later": f((c > r) * BIG), "want": f(want),
    }


def layouts(i):
    f32 = np.float32
    w = np.asarray(i["L0_attn_W_attn"]).reshape(3, PAIRS, P, D)
    bias = np.asarray(i["L0_attn_b_attn"]).reshape(3, PAIRS, P)
    qkv, qkvb = np.zeros((PAIRS, P, 3 * P), f32), np.zeros((P, PAIRS, 3), f32)
    for j in range(3):
        qkv[:, :, j * P:(j + 1) * P] = w[j].transpose(0, 2, 1)
        qkvb[:, :, j] = bias[j].T
    packs = np.zeros((PACKS, P, 4 * P), f32)
    for p in range(PACKS - 1):
        for e in range(2):
            packs[p, :, e * HE0:(e + 1) * HE0] = i["L0_ffn_w_gate"][2 * p + e]
            packs[p, :, P + e * HE0:P + (e + 1) * HE0] = i["L0_ffn_w_up"][2 * p + e]
            packs[p, e * HE0:(e + 1) * HE0, 2 * P:3 * P] = i["L0_ffn_w_down"][2 * p + e]
            packs[p, 2 * p + e, 3 * P + e * HE0:3 * P + (e + 1) * HE0] = 1.0
    packs[-1, :, 0:HE0] = i["L0_ffn_sw_gate"]
    packs[-1, :, P:P + HE0] = i["L0_ffn_sw_up"]
    packs[-1, 0:HE0, 2 * P:3 * P] = i["L0_ffn_sw_down"]
    packs[-1, E0, 3 * P:4 * P] = 1.0
    c = np.ascontiguousarray
    wproj = np.asarray(i["L0_attn_W_proj"]).reshape(D, PAIRS, P).transpose(2, 1, 0)
    g = {n: np.asarray(v) for n, v in i.items()}
    rows = lambda z: c(np.broadcast_to(z[..., None, :], (*z.shape[:-1], P, z.shape[-1])))
    qs, ks = g["L1_ffn_q_scale"], g["L1_ffn_k_scale"]
    qks = np.stack([qs, np.roll(qs, HD2 // 2, -1), ks, np.roll(ks, HD2 // 2, -1)], 1)
    w2, b1 = np.zeros((DEPTH, P, len(HCH), D), f32), np.zeros((DEPTH, P, len(HCH), 2), f32)
    for j, (c0, n) in enumerate(HCH):
        w2[:, 0:n, j, :] = g["L1_ffn_w2"][:, c0:c0 + n, :]
        for k in range(2):
            b1[:, 0:n, j, k] = g["L1_ffn_b1"][:, k * HID + c0:k * HID + c0 + n]
    return {
        "wvT": c(g["L1_attn_Wv"].T), "wgT": c(g["L1_attn_Wg"].T), "woT": c(g["L1_attn_Wo"].T),
        "waT": c(g["L1_attn_Wa"].T), "wbT16": c(np.repeat(g["L1_attn_Wb"].T, K1, axis=1)),
        "dtb": rows(g["L1_attn_dt_bias"]), "nega": rows(g["L1_attn_A_log"]), "normw": rows(g["L1_attn_norm_w"]),
        "convw": c(np.concatenate([g["L1_attn_conv_w"], g["L1_attn_conv_b"][:, None]], 1)),
        "wqkv": c(g["L1_ffn_wqkv"]), "w1": c(g["L1_ffn_w1"]), "w2": w2, "b1": b1, "b2": rows(g["L1_ffn_b2"]),
        "wo": c(g["L1_ffn_wo"].reshape(DEPTH, 4, P, D).transpose(0, 2, 1, 3)),
        "lgb": c(np.stack([g["L1_ffn_ln_g"], g["L1_ffn_ln_b"]], -1)),
        "qks": c(np.broadcast_to(qks[:, None], (DEPTH, P, 4, HD2))),
        "x": c(i["L0_attn_x"]), "gate_w": c(i["L0_ffn_gate_w"]), "qkv_packs": qkv, "qkvb": qkvb.reshape(P, PAIRS * 3), "packs": packs,
        "wprojT": c(wproj), "bproj": c(np.asarray(i["L0_attn_b_proj"]).reshape(D, 1)),
    }


def kernel(**inputs):
    import concourse.bacc as bacc
    from concourse.bass_utils import run_bass_kernel_spmd

    nc = bacc.Bacc("TRN2", target_bir_lowering=False, num_devices=1)
    arrays = {n: np.asarray(v) for n, v in {**shape_constants(), **layouts(inputs)}.items()}
    a = {n: nc.dram_tensor(f"in_{n}", v.shape, mybir.dt.from_np(v.dtype), kind="ExternalInput").ap()
         for n, v in arrays.items()}
    out = nc.dram_tensor("out", (B, T, D), F32, kind="ExternalOutput").ap()
    build(nc, a, out)
    r = run_bass_kernel_spmd(nc, [{f"in_{n}": v for n, v in arrays.items()}], core_ids=[0])
    return r.results[0]["out"]
```

```python
from contextlib import ExitStack, contextmanager

import numpy as np

import concourse.bass as bass
from concourse import mybir

F32 = mybir.dt.float32
I32 = mybir.dt.int32
BF16 = mybir.dt.bfloat16
ALU = mybir.AluOpType
ACT = mybir.ActivationFunctionType
AX = mybir.AxisListType.X
ds = bass.ds

P = 128
B, T, D = 2, 1024, 128
NT = T // P
HALF = 512
BIG = 1.5e38
LN_EPS = 1e-5

H0, HD0 = 16, 64
PAIRS = H0 // 2
BUDGET = max(1, int(T * 0.2))
KEEP = min(BUDGET - 1, T)
TSEL = KEEP // P
NSEL = NT - TSEL
E0, HE0 = 16, 64
PACKS = E0 // 2 + 1
H1, K1, C1 = 8, 16, 64
NC1 = T // C1
EPS_L2, EPS_RMS = 1e-6, 1e-5
DEPTH, H2, HD2, WIN = 2, 8, 64, 64
INNER = H2 * HD2
HID = int(D * 4 * 2 / 3)
HCH = [(0, 128), (128, 128), (256, HID - 256)]
KW = WIN + P


@contextmanager
def signals(nc, names):
    with ExitStack() as ctx:
        got = [ctx.enter_context(nc.semaphore(n)) for n in names.split()]
        yield got
        nums = sorted(s.num for s in got)
        while nums:
            run = next(k for k in range(1, len(nums) + 1) if k == len(nums) or nums[k] != nums[0] + k)
            nc.gpsimd.sem_clear(range(nums[0], nums[0] + run))
            nums = nums[run:]
        nc.all_engine_barrier()


class Chain:

    def __init__(self, eng, sem, base=0):
        self.eng, self.sem, self.base, self.n = eng, sem, base, 0

    def add(self, ins):
        self.n += 1
        ins.then_inc(self.sem, 1)

    def hold(self):
        self.eng.wait_ge(self.sem, self.base + self.n)

    def link(self, ins):
        self.add(ins)
        self.hold()


def bcast(ap, *shape):
    return ap.to_broadcast(list(shape))




def norm_stage(nc, m, src, out, outT, gain=None, shift=None):
    with signals(nc, "stats_step var_ready rstd_root normed turned outT_step") as (
            stats_step, var_ready, rstd_root, normed, turned, outT_step):
        with nc.Block() as block:
            @block.vector
            def _(dve):
                ch = Chain(dve, stats_step)
                for t in range(NT):
                    ch.add(nc.vector.bn_stats(m.bn[:, t, :], src[:, t, :]))
                ch.hold()
                for t in range(NT):
                    ch.add(nc.vector.bn_aggr(m.mv[:, t, :], m.bn[:, t, :]))
                ch.hold()
                nc.vector.tensor_scalar(m.rstd[:], m.mv[:, :, 1], LN_EPS, None, ALU.add).then_inc(var_ready, 1)
                dve.wait_ge(rstd_root, 1)
                ch.link(nc.vector.reciprocal(m.rstd[:], m.rstd[:]))
                for t in range(NT):
                    nc.vector.tensor_scalar(out[:, t, :], src[:, t, :], m.mv[:, t, 0:1], m.rstd[:, t:t + 1],
                                            ALU.subtract, ALU.mult).then_inc(normed, 1)

            @block.tensor
            def _(pe):
                for t in range(NT):
                    pe.wait_ge(normed, t + 1)
                    nc.tensor.transpose(m.ps[:, t // 4, (t % 4) * P:(t % 4 + 1) * P], out[:, t, :],
                                        m.ident[:]).then_inc(turned, 1)

            @block.scalar
            def _(act):
                act.wait_ge(var_ready, 1)
                nc.scalar.activation(m.rstd[:], m.rstd[:], ACT.Sqrt).then_inc(rstd_root, 1)
                for half in range(2):
                    act.wait_ge(turned, 4 * half + 4)
                    o = outT[:, half * HALF:(half + 1) * HALF]
                    if gain is None:
                        nc.scalar.activation(o, m.ps[:, half, :], ACT.Copy).then_inc(outT_step, 1)
                    else:
                        nc.scalar.activation(o, m.ps[:, half, :], ACT.Identity, bias=shift,
                                             scale=gain).then_inc(outT_step, 1)




def penalty_stage(nc, m, qkv_packs):
    with signals(nc, "pack_in qk_done qk_ready att_done relu_ready summed past_ready pen_ready ch padded") as (
            pack_in, qk_done, qk_ready, att_done, relu_ready, summed, past_ready, pen_ready, chs, padded):
        with nc.Block() as block:
            @block.sync
            def _(sp):
                sp.dma_start(m.wst[:], qkv_packs[0]).then_inc(pack_in, 16)

            @block.gpsimd
            def _(pool):
                nc.gpsimd.memset(m.past[:], 0.0).then_inc(past_ready, 1)
                for t in range(NT - 1):
                    w = P * (t + 1)
                    pool.wait_ge(summed, t + 1)
                    pool.wait_ge(past_ready, t + 1)
                    nc.gpsimd.tensor_tensor(m.past[:, 0:w], m.past[:, 0:w], m.srelu[:, t % 2, 0:w],
                                            ALU.add).then_inc(past_ready, 1)

            @block.tensor
            def _(pe):
                pe.wait_ge(pack_in, 16)
                for j in range(2):
                    for half in range(2):
                        nc.tensor.matmul(m.ps[:, 2 * j + half, :], m.wst[:, j * P:(j + 1) * P],
                                         m.xnT[:, half * HALF:(half + 1) * HALF], start=True,
                                         stop=True).then_inc(qk_done, 1)
                pe.wait_ge(qk_ready, 4)
                pe.wait_ge(padded, 1)

                def att(t):
                    w = P * (t + 1)
                    if t >= 2:
                        pe.wait_ge(relu_ready, t - 1)
                    for a in range(0, w, HALF):
                        b = min(w, a + HALF)
                        ins = nc.tensor.matmul(m.ps[:, 2 * (t % 2) + a // HALF, 0:b - a], m.qT[:, 0, t * P:(t + 1) * P],
                                               m.kT[:, a:b], start=True, stop=True)
                    ins.then_inc(att_done, 1)

                att(0)
                for t in range(NT):
                    w = P * (t + 1)
                    if t + 1 < NT:
                        att(t + 1)
                    pe.wait_ge(relu_ready, t + 1)
                    pe.wait_ge(past_ready, t + 1)
                    if t >= 2:
                        pe.wait_ge(pen_ready, t - 1)
                    for a in range(0, w, HALF):
                        b = min(w, a + HALF)
                        bank = 4 + 2 * (t % 2) + a // HALF
                        nc.tensor.matmul(m.ps[:, bank, 0:b - a], m.before[:], m.srelu[:, t % 2, a:b],
                                         start=True, stop=False)
                        ins = nc.tensor.matmul(m.ps[:, bank, 0:b - a], m.ones[:], m.past[:, a:b],
                                               start=False, stop=True)
                    ins.then_inc(summed, 1)

            @block.vector
            def _(dve):
                nc.vector.memset(m.qT[HD0:P, 0, :], 0.0).then_inc(padded, 1)
                for half in range(2):
                    dve.wait_ge(qk_done, half + 1)
                    nc.vector.tensor_scalar(m.qT[0:HD0, 0, half * HALF:(half + 1) * HALF], m.ps[0:HD0, half, :],
                                            m.qkvb[0:HD0, 0:1], -1.0 / 8, ALU.add, ALU.mult).then_inc(qk_ready, 1)
                for half in range(2):
                    dve.wait_ge(qk_done, half + 3)
                    nc.vector.tensor_scalar(m.kT[:, half * HALF:(half + 1) * HALF], m.ps[:, 2 + half, :],
                                            m.qkvb[:, 1:2], None, ALU.add).then_inc(qk_ready, 1)
                ch = Chain(dve, chs)

                def relu(t):
                    w = P * (t + 1)
                    dve.wait_ge(att_done, t + 1)
                    if t >= 2:
                        dve.wait_ge(summed, t - 1)
                        dve.wait_ge(past_ready, t)
                    ch.link(nc.vector.tensor_scalar(m.srelu[:, t % 2, 0:w], m.psf[:, 2 * (t % 2) * HALF:2 * (t % 2) * HALF + w],
                                                    -1.0, 0.0, ALU.mult, ALU.max))
                    ch.link(nc.vector.tensor_tensor(m.srelu[:, t % 2, t * P:w], m.srelu[:, t % 2, t * P:w],
                                                    m.below[:], ALU.mult))
                    nc.vector.memset(m.srelu[:, t % 2, 0:1], 0.0).then_inc(relu_ready, 1)

                relu(0)
                for t in range(NT):
                    w = P * (t + 1)
                    if t + 1 < NT:
                        relu(t + 1)
                    dve.wait_ge(summed, t + 1)
                    o = (4 + 2 * (t % 2)) * HALF
                    if t:
                        ch.add(nc.vector.tensor_copy(m.pen[:, t, 0:t * P], m.psf[:, o:o + t * P]))
                    nc.vector.tensor_tensor(m.pen[:, t, t * P:w], m.psf[:, o + t * P:o + w], m.later[:],
                                            ALU.add).then_inc(pen_ready, 1)


def joff(t):
    return P * t * (t + 1) // 2


class Selection:

    BITS = 31
    TILES = list(range(TSEL, NT))
    BY_ACT = TILES[:0:-2]
    BY_DVE = TILES[-2::-2] + TILES[:1]

    def __init__(self, nc, m, chain, cand_ready, act_counted):
        self.nc, self.m = nc, m
        self.chain, self.cand_ready, self.act_counted = chain, cand_ready, act_counted
        self.base, self.per = 3, len(self.BY_DVE) + 5

    def act_bit(self, act, bit):
        nc, m = self.nc, self.m
        act.wait_ge(self.cand_ready, bit + 1)
        for t in self.BY_ACT:
            i = t - TSEL
            nc.scalar.activation(m.junk[:, joff(t):joff(t) + P * (t + 1)], m.pen[:, t, 0:P * (t + 1)], ACT.Sign,
                                 bias=m.candf[:, i:i + 1], scale=-1.0,
                                 accum_out=m.count[:, i:i + 1]).then_inc(self.act_counted, 1)

    def dve_start(self, dve):
        nc, m = self.nc, self.m
        ch = Chain(dve, self.chain)
        ch.add(nc.vector.memset(m.bitf[:], float(2 ** (self.BITS - 1))))
        ch.add(nc.vector.memset(m.thr[:], 0))
        ch.hold()
        ch.link(nc.vector.tensor_copy(m.biti[:], m.bitf[:]))
        nc.vector.tensor_tensor(m.cand[:], m.thr[:], m.biti[:], ALU.bitwise_or).then_inc(self.cand_ready, 1)
        assert ch.n == self.base

    def dve_bit(self, dve, bit):
        nc, m = self.nc, self.m
        c = Chain(dve, self.chain, self.base + bit * self.per)
        dve.wait_ge(self.cand_ready, bit + 1)
        for t in self.BY_DVE:
            i = t - TSEL
            c.add(nc.vector.tensor_scalar(m.junk[:, joff(t):joff(t) + P * (t + 1)], m.pen[:, t, 0:P * (t + 1)],
                                          m.candf[:, i:i + 1], 0.0, ALU.is_lt, ALU.add,
                                          accum_out=m.count[:, i:i + 1]))
        c.add(nc.vector.tensor_scalar(m.nextbit[:], m.bitf[:], 0.5, None, ALU.mult))
        dve.wait_ge(self.act_counted, (bit + 1) * len(self.BY_ACT))
        c.hold()
        c.link(nc.vector.tensor_tensor(m.few[:], m.count[:], m.want[:, 0, :], ALU.is_lt))
        c.link(nc.vector.tensor_tensor(m.biti[:], m.few[:], m.bitf[:], ALU.mult))
        c.add(nc.vector.tensor_scalar(m.bitf[:], m.bitf[:], 0.5, None, ALU.mult))
        c.link(nc.vector.tensor_tensor(m.thr[:], m.thr[:], m.biti[:], ALU.bitwise_or))
        nc.vector.tensor_tensor(m.cand[:], m.thr[:], m.nextbit[:], ALU.bitwise_or).then_inc(self.cand_ready, 1)
        assert c.n == self.per

    def dve_finish(self, dve):
        nc, m = self.nc, self.m
        ch = Chain(dve, self.chain, self.base + self.BITS * self.per)
        for t in self.BY_ACT:
            i = t - TSEL
            ch.add(nc.vector.tensor_scalar(m.junk[:, joff(t):joff(t) + P * (t + 1)], m.pen[:, t, 0:P * (t + 1)],
                                           m.thrf[:, i:i + 1], 0.0, ALU.is_le, ALU.add,
                                           accum_out=m.count[:, i:i + 1]))
        ch.hold()
        ch.link(nc.vector.tensor_tensor(m.few[:], m.count[:], m.want[:, 1, :], ALU.is_lt))
        ch.link(nc.vector.tensor_tensor(m.biti[:], m.few[:], m.want[:, 2, :], ALU.mult))
        ch.link(nc.vector.tensor_tensor(m.thr[:], m.thr[:], m.biti[:], ALU.add))


def drop_keys(nc, m, ch, t):
    i = t - TSEL
    w = P * (t + 1)
    pen, thr = m.pen[:, t, 0:w], m.thrf[:, i:i + 1]
    same, drop = m.past[:, 0:w], m.srelu[:, 0, 0:w]
    ch.add(nc.vector.tensor_scalar(drop, pen, thr, 0.0, ALU.is_lt, ALU.add, accum_out=m.count[:, i:i + 1]))
    ch.link(nc.vector.tensor_scalar(same, pen, thr, None, ALU.is_equal))
    ch.add(nc.vector.tensor_tensor(m.need[:, i:i + 1], m.want[:, 1, i:i + 1], m.count[:, i:i + 1], ALU.subtract))
    ch.link(nc.vector.tensor_tensor_scan(m.srelu[:, 1, 0:w], bcast(m.ones[:, 0:1], P, w), same, 0.0,
                                         ALU.mult, ALU.add))
    ch.link(nc.vector.scalar_tensor_tensor(out=same, in0=m.srelu[:, 1, 0:w], scalar=m.need[:, i:i + 1],
                                           in1=same, op0=ALU.is_gt, op1=ALU.mult))
    ch.link(nc.vector.scalar_tensor_tensor(out=drop, in0=pen, scalar=thr, in1=same, op0=ALU.is_gt, op1=ALU.add))
    ch.link(nc.vector.tensor_tensor(drop[:, t * P:w], drop[:, t * P:w], m.ident[:], ALU.is_gt))
    ch.link(nc.vector.scalar_tensor_tensor(out=pen, in0=drop, scalar=BIG, in1=pen, op0=ALU.mult, op1=ALU.max))


def experts_stage(nc, m, packs):
    with signals(nc, "pack0 pack1 sq_ready root_ready dv logits_ready scores_ready topk_step combT_turned "
                     "combT_ready gates_ready silu_ready hidden_ready used_pack out_done out_ready "
                     "select_step cand_ready act_counted") as (
            pack0, pack1, sq_ready, root_ready, dv, logits_ready, scores_ready, topk_step, combT_turned,
            combT_ready, gates_ready, silu_ready, hidden_ready, used_pack, out_done, out_ready,
            select_step, cand_ready, act_counted):
        pack_sem = [pack0, pack1]
        nloop = PACKS // 2
        sel = Selection(nc, m, select_step, cand_ready, act_counted)
        bits = Selection.BITS // nloop
        over = Selection.BITS - bits * nloop
        with nc.Block() as block:
            @block.sync
            def _(sp):
                for s in range(2):
                    sp.dma_start(m.pack[:, s, :], packs[s]).then_inc(pack_sem[s], 16)
                with sp.Fori(1, nloop) as it:
                    for s in range(2):
                        sp.wait_ge(used_pack, it * 2 - 1 + s)
                        sp.dma_start(m.pack[:, s, :], packs[ds(it * 2 + s, 1)].rearrange("o p n -> (o p) n")
                                     ).then_inc(pack_sem[s], 16)
                sp.wait_ge(used_pack, PACKS - 2)
                sp.dma_start(m.pack[:, 0, :], packs[PACKS - 1]).then_inc(pack_sem[0], 16)

            def elementwise(dve, n, half, c):
                dve.wait_ge(silu_ready, n + 1)
                c.link(nc.vector.tensor_tensor(m.hid[:, half, :], m.ps[:, 2 + half, :], m.silu[:, half, :], ALU.mult))
                nc.vector.tensor_tensor(m.hid[:, half, :], m.ps[:, 4 + half, :], m.hid[:, half, :],
                                        ALU.mult).then_inc(hidden_ready, 1)

            @block.vector
            def _(dve):
                ch = Chain(dve, dv)
                dve.wait_ge(root_ready, 1)
                ch.link(nc.vector.tensor_scalar(m.rs8[:], m.rs8[:], 1e-12, None, ALU.max))
                ch.link(nc.vector.reciprocal(m.rs8[:], m.rs8[:]))
                dve.wait_ge(logits_ready, NT)
                nc.vector.tensor_tensor(m.score[:, :, 0:E0], m.ps[:, 0, 0:NT * E0].rearrange("p (t e) -> p t e", e=E0),
                                        bcast(m.rs8[:].unsqueeze(2), P, NT, E0), ALU.mult).then_inc(topk_step, 1)
                dve.wait_ge(scores_ready, 1)
                for t in range(NT):
                    ch.add(nc.vector.max(m.top8[:, t, :], m.score[:, t, 0:E0]))
                ch.hold()
                for t in range(NT):
                    ch.add(nc.vector.match_replace(m.rest[:, t, :], m.top8[:, t, :], m.score[:, t, 0:E0], -1.0))
                ch.hold()
                ch.link(nc.vector.scalar_tensor_tensor(out=m.rest[:], in0=m.rest[:], scalar=0.0,
                                                       in1=m.score[:, :, 0:E0], op0=ALU.is_lt, op1=ALU.mult))
                ch.link(nc.vector.tensor_reduce(m.rs8b[:], m.rest[:], AX, ALU.add))
                ch.link(nc.vector.reciprocal(m.rs8b[:], m.rs8b[:]))
                nc.vector.tensor_tensor(m.score[:, :, 0:E0], m.rest[:], bcast(m.rs8b[:].unsqueeze(2), P, NT, E0),
                                        ALU.mult).then_inc(topk_step, 1)
                base = ch.n
                sel.dve_start(dve)
                for bit in range(over):
                    sel.dve_bit(dve, bit)
                with dve.Fori(0, nloop) as it:
                    c = Chain(dve, dv, base + it * 4)
                    for j in range(bits):
                        sel.dve_bit(dve, it * bits + over + j)
                        if j < 4:
                            elementwise(dve, it * 4 + j, j % 2, c)
                    assert c.n == 4
                c = Chain(dve, dv, base + 4 * nloop)
                for k in range(2):
                    elementwise(dve, nloop * 4 + k, k, c)
                sel.dve_finish(dve)

            @block.scalar
            def _(act):
                for t in range(NT):
                    nc.scalar.activation(m.silu[:, t // 4, (t % 4) * P:(t % 4 + 1) * P], m.xn[:, t, :], ACT.Square,
                                         accum_out=m.rs8[:, t:t + 1]).then_inc(sq_ready, 1)
                act.wait_ge(sq_ready, NT)
                nc.scalar.activation(m.rs8[:], m.rs8[:], ACT.Sqrt).then_inc(root_ready, 1)
                act.wait_ge(topk_step, 1)
                nc.scalar.activation(m.score[:, :, 0:E0], m.score[:, :, 0:E0], ACT.Sigmoid).then_inc(scores_ready, 1)
                for half in range(2):
                    act.wait_ge(combT_turned, 4 * (half + 1))
                    nc.scalar.activation(m.combT[0:E0 + 1, half * HALF:(half + 1) * HALF],
                                         m.ps[0:E0 + 1, half, :], ACT.Copy).then_inc(combT_ready, 1)

                def silu(n, half):
                    act.wait_ge(gates_ready, n + 1)
                    nc.scalar.activation(m.silu[:, half, :], m.ps[:, half, :], ACT.Silu).then_inc(silu_ready, 1)

                for bit in range(over):
                    sel.act_bit(act, bit)
                with act.Fori(0, nloop) as it:
                    for j in range(bits):
                        if j < 4:
                            silu(it * 4 + j, j % 2)
                        sel.act_bit(act, it * bits + over + j)
                for k in range(2):
                    silu(nloop * 4 + k, k)
                for half in range(2):
                    act.wait_ge(out_done, 1)
                    nc.scalar.activation(m.ffnT[:, half * HALF:(half + 1) * HALF], m.ps[:, 6 + half, :],
                                         ACT.Copy).then_inc(out_ready, 1)

            @block.tensor
            def _(pe):
                for t in range(NT):
                    nc.tensor.matmul(m.ps[:, 0, t * E0:(t + 1) * E0], m.xnT[:, t * P:(t + 1) * P],
                                     m.gateT[:, 0:E0], start=True, stop=True).then_inc(logits_ready, 1)
                pe.wait_ge(topk_step, 2)
                for t in range(NT):
                    nc.tensor.transpose(m.ps[0:E0 + 1, t // 4, (t % 4) * P:(t % 4 + 1) * P], m.score[:, t, :],
                                        m.ident[:]).then_inc(combT_turned, 1)
                for half in range(2):
                    nc.tensor.matmul(m.ps[:, 6 + half, :], m.zeros[:, 0:P], m.xnT[:, half * HALF:(half + 1) * HALF],
                                     start=True, stop=False, skip_group_check=True)

                def up(n, s, half, wait_hidden):
                    if wait_hidden is not None:
                        pe.wait_ge(hidden_ready, wait_hidden)
                    x = m.xnT[:, half * HALF:(half + 1) * HALF]
                    nc.tensor.matmul(m.ps[:, 2 + half, :], m.pack[:, s, P:2 * P], x, start=True, stop=True)
                    nc.tensor.matmul(m.ps[:, 4 + half, :], m.pack[0:E0 + 1, s, 3 * P:4 * P],
                                     m.combT[0:E0 + 1, half * HALF:(half + 1) * HALF], start=True, stop=True)
                    nc.tensor.matmul(m.ps[:, half, :], m.pack[:, s, 0:P], x, start=True,
                                     stop=True).then_inc(gates_ready, 1)

                def down(n, s, half):
                    pe.wait_ge(hidden_ready, n + 1)
                    ins = nc.tensor.matmul(m.ps[:, 6 + half, :], m.pack[:, s, 2 * P:3 * P], m.hid[:, half, :],
                                           start=False, stop=False, skip_group_check=True)
                    if half == 1:
                        ins.then_inc(used_pack, 1)

                pe.wait_ge(combT_ready, 2)
                pe.wait_ge(pack0, 16)
                up(0, 0, 0, None)
                up(1, 0, 1, None)
                with pe.Fori(0, nloop) as it:
                    for k in range(4):
                        down(it * 4 + k, k // 2, k % 2)
                        s = (k // 2 + 1) % 2
                        if k % 2 == 0:
                            pe.wait_ge(pack_sem[s], (it + 1) * 16 if s == 1 else (it + 2) * 16)
                        up(it * 4 + k + 2, s, k % 2, it * 4 + k + 1)
                for k in range(2):
                    down(nloop * 4 + k, 0, k)
                nc.tensor.matmul(m.ps[:, 7, :], m.zeros[:, 0:P], m.xnT[:, 0:HALF], start=False, stop=True,
                                 skip_group_check=True).then_inc(out_done, 1)






def attention_stage(nc, m, qkv_packs):
    U = 2 * NT
    with signals(nc, "pack_in proj_done proj_ready scores_done shifted probs_ready turned_a turned_b "
                     "evac_a evac_d values_done y_ready yt_done yt_ready ch vproj_ready keys_ready padded drop_step") as (
            pack_in, proj_done, proj_ready, scores_done, shifted, probs_ready, turned_a, turned_b,
            evac_a, evac_d, values_done, y_ready, yt_done, yt_ready, chs, vproj_ready, keys_ready, padded, drop_step):
        groups = []
        for u in range(U):
            t = u // 2
            for g0 in range(0, t + 1, 4):
                groups.append((u, g0, min(t + 1, g0 + 4)))
        NG = len(groups)
        of = {u: [g for g in range(NG) if groups[g][0] == u] for u in range(U)}
        act_g = [g for g in range(NG) if g % 2 == 0]
        dve_g = [g for g in range(NG) if g % 2 == 1]
        NA, NDV = len(act_g), len(dve_g)

        def copied(eng, g, it):
            if g < 0:
                return
            if g % 2 == 0:
                eng.wait_ge(evac_a, it * NA + act_g.index(g) + 1)
            else:
                eng.wait_ge(evac_d, it * NDV + dve_g.index(g) + 1)

        SB, GB = [0, 2], [4, 5]
        YB, YTB = 6, 7
        with nc.Block() as block:
            @block.sync
            def _(sp):
                sp.dma_start(m.wst[:], qkv_packs[0]).then_inc(pack_in, 16)
                with sp.Fori(1, PAIRS) as it:
                    sp.wait_ge(proj_done, it * 6)
                    sp.dma_start(m.wst[:], qkv_packs[ds(it, 1)].rearrange("o p n -> (o p) n")).then_inc(pack_in, 16)

            @block.tensor
            def _(pe):
                pe.wait_ge(padded, 2)

                def queries_keys(pair):
                    pe.wait_ge(pack_in, pair * 16 + 16)
                    for j in range(2):
                        for half in range(2):
                            nc.tensor.matmul(m.ps[:, 2 * j + half, :], m.wst[:, j * P:(j + 1) * P],
                                             m.xnT[:, half * HALF:(half + 1) * HALF], start=True,
                                             stop=True).then_inc(proj_done, 1)

                def values_in():
                    for t in range(NT):
                        ins = nc.tensor.matmul(m.ps[:, 4 + t // 4, (t % 4) * P:(t % 4 + 1) * P],
                                               m.xnT[:, t * P:(t + 1) * P], m.wst[:, 2 * P:3 * P], start=True, stop=True)
                        if t % 4 == 3:
                            ins.then_inc(proj_done, 1)

                def scores(it, u):
                    t, h = u // 2, u % 2
                    w = P * (t + 1)
                    if u >= 2:
                        pe.wait_ge(shifted, it * U + u - 1)
                    for a in range(0, w, HALF):
                        b = min(w, a + HALF)
                        ins = nc.tensor.matmul(m.ps[:, SB[h] + a // HALF, 0:b - a],
                                               m.qT[:, h, t * P:(t + 1) * P], m.kT[:, a:b], start=True, stop=True)
                    ins.then_inc(scores_done, 1)

                def first_scores(it):
                    pe.wait_ge(proj_ready, it * 2 + 2)
                    pe.wait_ge(keys_ready, it * 2 + 2)
                    scores(it, 0)
                    scores(it, 1)

                def pair_turn(it, more):
                    def turn(u):
                        h = u % 2
                        pe.wait_ge(probs_ready, it * U + u + 1)
                        if u == 0:
                            pe.wait_ge(vproj_ready, it * 2 + 2)
                        for g in of[u]:
                            copied(pe, g - 2, it)
                            _, k0, k1 = groups[g]
                            for k in range(k0, k1):
                                ins = nc.tensor.transpose(m.ps[:, GB[g % 2], (k - k0) * P:(k - k0 + 1) * P],
                                                          m.prob[:, u % 4, k * P:(k + 1) * P], m.ident[:])
                            ins.then_inc(turned_a if g % 2 == 0 else turned_b, 1)

                    def values(u):
                        t, h = u // 2, u % 2
                        for g in of[u]:
                            copied(pe, g, it)
                        if u >= 1:
                            pe.wait_ge(y_ready, it * U + u)
                        for k in range(t + 1):
                            ins = nc.tensor.matmul(m.ps[:, YB, 0:HD0], m.pT[:, h, k, :],
                                                   m.v[:, k, h * HD0:(h + 1) * HD0], start=(k == 0), stop=(k == t))
                        ins.then_inc(values_done, 1)

                    def turn_y(t):
                        pe.wait_ge(y_ready, it * U + 2 * t + 2)
                        pe.wait_ge(yt_ready, it * NT + t + 1)
                        nc.tensor.transpose(m.ps[:, YTB, 0:P], m.y[:, t % 2, :], m.ident[:]).then_inc(yt_done, 1)

                    for n in range(2, U + 4):
                        if n < U:
                            scores(it, n)
                        if 0 <= n - 2 < U:
                            turn(n - 2)
                        if 0 <= n - 3 < U:
                            values(n - 3)
                        if n == U and more:
                            pe.wait_ge(shifted, it * U + U)
                            queries_keys(it + 1)
                        if n == U + 2 and more:
                            values_in()
                        if n >= 5 and n % 2 == 1:
                            turn_y((n - 5) // 2)
                    if more:
                        first_scores(it + 1)

                queries_keys(0)
                values_in()
                first_scores(0)
                with pe.Fori(0, PAIRS - 1) as it:
                    pair_turn(it, True)
                pair_turn(PAIRS - 1, False)

            @block.vector
            def _(dve):
                nc.vector.memset(m.qT[HD0:P, 0, :], 0.0).then_inc(padded, 1)
                nc.vector.memset(m.qT[0:HD0, 1, :], 0.0).then_inc(padded, 1)

                def queries(pair):
                    for half in range(2):
                        dve.wait_ge(proj_done, pair * 6 + half + 1)
                        for h in range(2):
                            r = slice(h * HD0, (h + 1) * HD0)
                            ins = nc.vector.tensor_scalar(m.qT[r, h, half * HALF:(half + 1) * HALF], m.ps[r, half, :],
                                                          m.qkvb[r, ds(pair * 3, 1)], -1.0 / 8, ALU.add, ALU.mult)
                        ins.then_inc(proj_ready, 1)

                def shift(it, u):
                    t, h = u // 2, u % 2
                    w = P * (t + 1)
                    if u >= 4:
                        for g in of[u - 4]:
                            dve.wait_ge(turned_a if g % 2 == 0 else turned_b,
                                        it * (NA if g % 2 == 0 else NDV) + (act_g if g % 2 == 0 else dve_g).index(g) + 1)
                    count = dve.to_reg(it * U + u + 1)
                    dve.wait_ge(keys_ready, 2)
                    dve.wait_ge(scores_done, count)
                    nc.vector.tensor_tensor_reduce(m.prob[:, u % 4, 0:w], m.psf[:, SB[h] * HALF:SB[h] * HALF + w],
                                                   m.pen[:, t, 0:w], 1.0, 3.0e38, ALU.add, ALU.min,
                                                   m.nmax[:, u % 4:u % 4 + 1]).then_inc(shifted, 1)

                def pair_turn(it, more, first=False):
                    c = Chain(dve, chs, it * U)

                    def evac(u):
                        for g in of[u]:
                            if g % 2 == 1:
                                _, k0, k1 = groups[g]
                                dve.wait_ge(turned_b, it * NDV + dve_g.index(g) + 1)
                                if u >= 2:
                                    dve.wait_ge(values_done, it * U + u - 1)
                                nc.vector.tensor_copy(m.pT[:, u % 2, k0:k1, :].rearrange("p k q -> p (k q)"),
                                                      m.ps[:, GB[1], 0:(k1 - k0) * P]).then_inc(evac_d, 1)

                    def finish(u):
                        t, h = u // 2, u % 2
                        dve.wait_ge(values_done, it * U + u + 1)
                        c.link(nc.vector.reciprocal(m.rsum[:, h:h + 1], m.esum[:, u % 8:u % 8 + 1]))
                        if t >= 2:
                            dve.wait_ge(yt_done, it * NT + t - 1)
                        nc.vector.tensor_scalar(m.y[:, t % 2, h * HD0:(h + 1) * HD0], m.ps[:, YB, 0:HD0],
                                                m.rsum[:, h:h + 1], None, ALU.mult).then_inc(y_ready, 1)

                    for n in range(2, U + 3):
                        if first and n % 2 == 0 and TSEL <= n // 2 < NT:
                            drop_keys(nc, m, dropping, n // 2)
                        if n < U:
                            shift(it, n)
                        if 0 <= n - 2 < U:
                            evac(n - 2)
                        if 0 <= n - 3 < U:
                            finish(n - 3)
                        if n == U and more:
                            queries(it + 1)
                    assert c.n == U
                    if more:
                        shift(it + 1, 0)
                        shift(it + 1, 1)

                queries(0)
                shift(0, 0)
                shift(0, 1)
                dropping = Chain(dve, drop_step)
                pair_turn(0, True, first=True)
                with dve.Fori(1, PAIRS - 1) as it:
                    pair_turn(it, True)
                pair_turn(PAIRS - 1, False)

            @block.scalar
            def _(act):
                act.sem_inc(yt_ready, 1)

                def keys(pair):
                    for half in range(2):
                        count = act.to_reg(pair * 6 + half + 3)
                        act.wait_ge(pack_in, 16)
                        act.wait_ge(proj_done, count)
                        nc.scalar.activation(m.kT[:, half * HALF:(half + 1) * HALF], m.ps[:, 2 + half, :], ACT.Identity,
                                             bias=m.qkvb[:, ds(pair * 3 + 1, 1)]).then_inc(keys_ready, 1)

                def values_out(pair):
                    for half in range(2):
                        act.wait_ge(proj_done, pair * 6 + 5 + half)
                        nc.scalar.activation(m.v[:, 4 * half:4 * half + 4, :].rearrange("p t c -> p (t c)"),
                                             m.ps[:, 4 + half, :], ACT.Copy).then_inc(vproj_ready, 1)

                def exp(it, u):
                    t, h = u // 2, u % 2
                    w = P * (t + 1)
                    act.wait_ge(shifted, it * U + u + 1)
                    if u >= 8:
                        act.wait_ge(y_ready, it * U + u - 7)
                    nc.scalar.activation(m.prob[:, u % 4, 0:w], m.prob[:, u % 4, 0:w], ACT.Exp,
                                         bias=m.nmax[:, u % 4:u % 4 + 1],
                                         scale=-1.0, accum_out=m.esum[:, u % 8:u % 8 + 1]).then_inc(probs_ready, 1)

                def pair_turn(it, more):
                    def evac(u):
                        for g in of[u]:
                            if g % 2 == 0:
                                _, k0, k1 = groups[g]
                                act.wait_ge(turned_a, it * NA + act_g.index(g) + 1)
                                if u >= 2:
                                    act.wait_ge(values_done, it * U + u - 1)
                                nc.scalar.activation(m.pT[:, u % 2, k0:k1, :].rearrange("p k q -> p (k q)"),
                                                     m.ps[:, GB[0], 0:(k1 - k0) * P], ACT.Copy).then_inc(evac_a, 1)

                    def out_y(t):
                        act.wait_ge(yt_done, it * NT + t + 1)
                        ins = nc.scalar.activation(m.yT[:, ds(it, 1), t * P:(t + 1) * P].rearrange("p o q -> p (o q)"),
                                                   m.ps[:, YTB, 0:P], ACT.Identity,
                                                   bias=m.qkvb[:, ds(it * 3 + 2, 1)])
                        ins.then_inc(yt_ready, 1)

                    for n in range(2, U + 4):
                        if 0 <= n - 2 < U:
                            evac(n - 2)
                        if n < U:
                            exp(it, n)
                        if n == U and more:
                            keys(it + 1)
                        if n == U + 2 and more:
                            act.wait_ge(values_done, it * U + U)
                            values_out(it + 1)
                        if n >= 5 and n % 2 == 1:
                            out_y((n - 5) // 2)
                    if more:
                        exp(it + 1, 0)
                        exp(it + 1, 1)

                keys(0)
                values_out(0)
                exp(0, 0)
                exp(0, 1)
                with act.Fori(0, PAIRS - 1) as it:
                    pair_turn(it, True)
                pair_turn(PAIRS - 1, False)


def project_stage(nc, m):
    with signals(nc, "proj_done sum_ready turned added") as (proj_done, sum_ready, turned, added):
        with nc.Block() as block:
            @block.tensor
            def _(pe):
                for half in range(2):
                    for p in range(PAIRS):
                        ins = nc.tensor.matmul(m.ps[:, half, :], m.wprojT[:, p, :],
                                               m.yT[:, p, half * HALF:(half + 1) * HALF],
                                               start=(p == 0), stop=(p == PAIRS - 1))
                    ins.then_inc(proj_done, 1)
                for t in range(NT):
                    pe.wait_ge(sum_ready, t // 4 + 1)
                    nc.tensor.transpose(m.ps[:, 2 + t // 4, (t % 4) * P:(t % 4 + 1) * P],
                                        m.ffnT[:, t * P:(t + 1) * P], m.ident[:]).then_inc(turned, 1)

            @block.vector
            def _(dve):
                for half in range(2):
                    dve.wait_ge(proj_done, half + 1)
                    f = m.ffnT[:, half * HALF:(half + 1) * HALF]
                    nc.vector.scalar_tensor_tensor(out=f, in0=m.ps[:, half, :], scalar=m.bproj[:, 0:1], in1=f,
                                                   op0=ALU.add, op1=ALU.add).then_inc(sum_ready, 1)
                for half in range(2):
                    dve.wait_ge(turned, 4 * half + 4)
                    xs = m.x[:, 4 * half:4 * half + 4, :].rearrange("p t c -> p (t c)")
                    nc.vector.tensor_tensor(xs, m.ps[:, 2 + half, :], xs, ALU.add).then_inc(added, 1)




def delta_prepare_stage(nc, m):
    with signals(nc, "sq_ready ss_ready root_ready xr_ready proj_done xv_ready beta_ready gate_ready xr_turned "
                     "wk_ready abs_ready e_ready decay_ready dec_done decE_done dec_ready decE_ready decT_done "
                     "decT_ready exp_ready conv_ready silu_ready diff_ready rest_ready vb_ready wkbd_ready "
                     "kd_ready rk_ready turned evac_done pad_ready ch") as (
            sq_ready, ss_ready, root_ready, xr_ready, proj_done, xv_ready, beta_ready, gate_ready, xr_turned,
            wk_ready, abs_ready, e_ready, decay_ready, dec_done, decE_done, dec_ready, decE_ready, decT_done,
            decT_ready, exp_ready, conv_ready, silu_ready, diff_ready, rest_ready, vb_ready, wkbd_ready,
            kd_ready, rk_ready, turned, evac_done, pad_ready, chs):
        halves = [(h, slice(h * HALF, (h + 1) * HALF)) for h in range(2)]
        NH = NT * H1
        with nc.Block() as block:
            @block.gpsimd
            def _(pool):
                nc.gpsimd.memset(m.wk[:, 0:1], 0.0).then_inc(pad_ready, 1)
                nc.gpsimd.memset(m.xv[:, 0:3], 0.0).then_inc(pad_ready, 1)
                pool.wait_ge(rk_ready, 1)
                pool.wait_ge(exp_ready, 2)
                nc.gpsimd.tensor_tensor(m.rkd, m.rk, m.grow, ALU.mult).then_inc(rk_ready, 1)
                pool.wait_ge(rest_ready, 1)
                nc.gpsimd.tensor_tensor(m.kdT, m.wk[:, 0:T], m.resto, ALU.mult).then_inc(kd_ready, 1)

            @block.tensor
            def _(pe):
                for h, s in halves:
                    nc.tensor.matmul(m.ps[:, h, :], m.wvT[:], m.xnT[:, s], start=True, stop=True).then_inc(proj_done, 1)
                for h, s in halves:
                    nc.tensor.matmul(m.ps[:, 2 + h, :], m.wbT16[:], m.xnT[:, s], start=True,
                                     stop=True).then_inc(proj_done, 1)
                for t in range(NT):
                    ins = nc.tensor.matmul(m.ps[:, 4, t * H1:(t + 1) * H1], m.xnT[:, t * P:(t + 1) * P], m.waT[:],
                                           start=True, stop=True)
                ins.then_inc(proj_done, 1)
                for t in range(NT):
                    ins = nc.tensor.matmul(m.ps[:, 5 + t // 4, (t % 4) * P:(t % 4 + 1) * P], m.xnT[:, t * P:(t + 1) * P],
                                           m.wgT[:], start=True, stop=True)
                    if t % 4 == 3:
                        ins.then_inc(proj_done, 1)
                for t in range(NT):
                    pe.wait_ge(xr_ready, t // 4 + 1)
                    if t == 4:
                        pe.wait_ge(xv_ready, 1)
                    ins = nc.tensor.transpose(m.ps[:, 7 if t < 4 else 0, (t % 4) * P:(t % 4 + 1) * P], m.xr[:, t, :],
                                              m.ident[:])
                    if t % 4 == 3:
                        ins.then_inc(xr_turned, 1)
                pe.wait_ge(decay_ready, 1)
                nc.tensor.matmul(m.ps[:, 4, 0:NH], m.chunk_upto[:], m.decay[:], start=True, stop=True).then_inc(dec_done, 1)
                pe.wait_ge(gate_ready, 2)
                for t in range(NT):
                    ins = nc.tensor.matmul(m.ps[:, 5 + t // 4, (t % 4) * P:(t % 4 + 1) * P], m.decay16[:, t, :],
                                           m.chunk_upto[:], start=True, stop=True)
                    if t % 4 == 3:
                        ins.then_inc(decE_done, 1)
                pe.wait_ge(dec_ready, 1)
                pe.wait_ge(beta_ready, 2)
                for t in range(NT):
                    ins = nc.tensor.transpose(m.ps[0:H1, 2 + t // 4, (t % 4) * P:(t % 4 + 1) * P],
                                              m.dec[:, t * H1:(t + 1) * H1], m.ident[:])
                ins.then_inc(decT_done, 1)
                pe.wait_ge(wk_ready, 2)
                pe.wait_ge(xv_ready, 2)
                pe.wait_ge(decT_ready, 2)
                pe.wait_ge(exp_ready, 2)
                for src, ready, bank in ((m.vb, vb_ready, 0), (m.wkbd, wkbd_ready, 2), (m.kdT, kd_ready, 5)):
                    pe.wait_ge(ready, 1)
                    for t in range(NT):
                        ins = nc.tensor.transpose(m.ps[:, bank + t // 4, (t % 4) * P:(t % 4 + 1) * P],
                                                  src[:, t * P:(t + 1) * P], m.ident[:])
                        if t % 4 == 3:
                            ins.then_inc(turned, 1)

            @block.scalar
            def _(act):
                nc.scalar.activation(m.sq, m.xn[:].rearrange("p t c -> p (t c)"), ACT.Square).then_inc(sq_ready, 1)
                act.wait_ge(ss_ready, 1)
                nc.scalar.activation(m.rn[:], m.rn[:], ACT.Sqrt).then_inc(root_ready, 1)
                for h, s in halves:
                    act.wait_ge(proj_done, 1 + h)
                    nc.scalar.activation(m.xv[:, 3 + h * HALF:3 + (h + 1) * HALF], m.ps[:, h, :],
                                         ACT.Copy).then_inc(xv_ready, 1)
                for h, s in halves:
                    act.wait_ge(proj_done, 3 + h)
                    nc.scalar.activation(m.beta[:, s], m.ps[:, 2 + h, :], ACT.Sigmoid).then_inc(beta_ready, 1)
                for h, s in halves:
                    act.wait_ge(proj_done, 6 + h)
                    nc.scalar.activation(m.gate[:, 4 * h:4 * h + 4, :].rearrange("p t c -> p (t c)"),
                                         m.ps[:, 5 + h, :], ACT.Silu).then_inc(gate_ready, 1)
                for h, s in halves:
                    act.wait_ge(xr_turned, 1 + h)
                    nc.scalar.activation(m.wk[:, 1 + h * HALF:1 + (h + 1) * HALF] if h == 0 else
                                         m.wk[:, 1 + HALF:1 + T], m.ps[:, 7 if h == 0 else 0, :],
                                         ACT.Copy).then_inc(wk_ready, 1)
                act.wait_ge(conv_ready, 1)
                nc.scalar.activation(m.vb, m.vb, ACT.Silu).then_inc(silu_ready, 1)
                act.wait_ge(abs_ready, 1)
                nc.scalar.activation(m.e64[:], m.e64[:], ACT.Exp, scale=-1.0).then_inc(e_ready, 1)
                for h, s in halves:
                    act.wait_ge(decE_done, 1 + h)
                    nc.scalar.activation(m.decE[:, s], m.ps[:, 5 + h, :], ACT.Copy).then_inc(decE_ready, 1)
                for h, s in halves:
                    nc.scalar.activation(m.grow[:, s], m.ps[:, 5 + h, :], ACT.Exp).then_inc(exp_ready, 1)
                act.wait_ge(decE_ready, 2)
                nc.scalar.activation(m.sdecay[:], m.decE.rearrange("p (n c) -> p n c", c=C1)[:, :, C1 - 1],
                                     ACT.Exp).then_inc(exp_ready, 1)
                act.wait_ge(decT_done, 1)
                for h, s in halves:
                    nc.scalar.activation(m.decT[:, s], m.ps[0:H1, 2 + h, :], ACT.Copy).then_inc(decT_ready, 1)
                act.wait_ge(diff_ready, 1)
                nc.scalar.activation(m.resto, m.resto, ACT.Exp).then_inc(rest_ready, 1)
                for h in range(2):
                    act.wait_ge(turned, 5 + h)
                    nc.scalar.activation(m.kd[:, 4 * h:4 * h + 4, :].rearrange("p t c -> p (t c)"), m.ps[:, 5 + h, :],
                                         ACT.Copy).then_inc(evac_done, 1)

            @block.vector
            def _(dve):
                ch = Chain(dve, chs)
                dve.wait_ge(sq_ready, 1)
                ch.link(nc.vector.tensor_reduce(m.rn[:], m.sq.rearrange("p (n k) -> p n k", k=K1), AX, ALU.add))
                nc.vector.tensor_scalar(m.rn[:], m.rn[:], EPS_L2, None, ALU.add).then_inc(ss_ready, 1)
                dve.wait_ge(root_ready, 1)
                ch.link(nc.vector.reciprocal(m.rn[:], m.rn[:]))
                for h in range(2):
                    v = lambda z: z[:, 4 * h:4 * h + 4, :].rearrange("p t (g k) -> p (t g) k", k=K1)
                    nc.vector.tensor_tensor(v(m.xr), v(m.xn), bcast(m.rn[:, h * NH // 2:(h + 1) * NH // 2].unsqueeze(2),
                                                                   P, NH // 2, K1), ALU.mult).then_inc(xr_ready, 1)
                dve.wait_ge(proj_done, 5)
                ch.link(nc.vector.tensor_tensor(m.z64[:].rearrange("p (t h) -> p t h", h=H1),
                                                m.ps[:, 4, 0:NH].rearrange("p (t h) -> p t h", h=H1),
                                                bcast(m.dtb[:].unsqueeze(1), P, NT, H1), ALU.add))
                nc.vector.scalar_tensor_tensor(out=m.e64[:], in0=m.z64[:], scalar=-1.0, in1=m.z64[:], op0=ALU.mult,
                                               op1=ALU.max).then_inc(abs_ready, 1)
                dve.wait_ge(xv_ready, 2)
                dve.wait_ge(pad_ready, 2)
                ch.link(nc.vector.tensor_scalar(m.vb, m.xv[:, 0:T], m.convw[:, 0:1], m.convw[:, 4:5], ALU.mult, ALU.add))
                for j in range(1, 4):
                    ins = nc.vector.scalar_tensor_tensor(out=m.vb, in0=m.xv[:, j:j + T], scalar=m.convw[:, j:j + 1],
                                                         in1=m.vb, op0=ALU.mult, op1=ALU.add)
                    if j < 3:
                        ch.link(ins)
                    else:
                        ins.then_inc(conv_ready, 1)
                dve.wait_ge(e_ready, 1)
                e, r, r2, q = m.e64[:], m.r64[:], m.rr64[:], m.q64[:]
                ch.link(nc.vector.tensor_scalar(r, e, 2.0, None, ALU.add))
                ch.link(nc.vector.reciprocal(r, r))
                ch.link(nc.vector.tensor_tensor(r, r, e, ALU.mult))
                ch.link(nc.vector.tensor_tensor(r2, r, r, ALU.mult))
                ch.link(nc.vector.tensor_scalar(q, r2, 1.0 / 17, None, ALU.mult))
                for k in range(15, 1, -2):
                    ch.link(nc.vector.scalar_tensor_tensor(out=q, in0=q, scalar=1.0 / k, in1=r2, op0=ALU.add, op1=ALU.mult))
                ch.link(nc.vector.scalar_tensor_tensor(out=q, in0=q, scalar=1.0, in1=r, op0=ALU.add, op1=ALU.mult))
                ch.link(nc.vector.tensor_scalar(m.z64[:], m.z64[:], 0.0, None, ALU.max))
                ch.link(nc.vector.scalar_tensor_tensor(out=q, in0=q, scalar=2.0, in1=m.z64[:], op0=ALU.mult, op1=ALU.add))
                ch.link(nc.vector.tensor_tensor(m.decay[:].rearrange("p (t h) -> p t h", h=H1),
                                                q.rearrange("p (t h) -> p t h", h=H1),
                                                bcast(m.nega[:].unsqueeze(1), P, NT, H1), ALU.mult))
                nc.vector.tensor_copy(m.decay16[:].rearrange("p t (h k) -> p (t h) k", k=K1),
                                      bcast(m.decay[:].unsqueeze(2), P, NH, K1)).then_inc(decay_ready, 1)
                dve.wait_ge(dec_done, 1)
                nc.vector.tensor_copy(m.dec[:], m.ps[:, 4, 0:NH]).then_inc(dec_ready, 1)
                dve.wait_ge(wk_ready, 2)
                nc.vector.tensor_scalar(m.rk, m.wk[:, 1:1 + T], 1.0 / K1 ** 0.5, None, ALU.mult).then_inc(rk_ready, 1)
                dve.wait_ge(beta_ready, 2)
                ch.link(nc.vector.tensor_tensor(m.wkb, m.wk[:, 0:T], m.beta, ALU.mult))
                dve.wait_ge(silu_ready, 1)
                nc.vector.tensor_tensor(m.vb, m.vb, m.beta, ALU.mult).then_inc(vb_ready, 1)
                dve.wait_ge(exp_ready, 2)
                nc.vector.tensor_tensor(m.wkbd, m.wkb, m.grow, ALU.mult).then_inc(wkbd_ready, 1)
                dve.wait_ge(decE_ready, 2)
                dv = m.decE.rearrange("p (n c) -> p n c", c=C1)
                ch.link(nc.vector.tensor_tensor(m.resto.rearrange("p (n c) -> p n c", c=C1),
                                                bcast(dv[:, :, C1 - 1:C1], P, NC1, C1), dv, ALU.subtract))
                nc.vector.tensor_scalar(m.resto, m.resto, 0.0, None, ALU.min).then_inc(diff_ready, 1)
                for i, off in ((0, 0), (1, 0), (2, K1), (3, K1)):
                    dve.wait_ge(turned, i + 1)
                    h = i % 2
                    for t in range(4):
                        nc.vector.tensor_copy(m.rhs[:, 4 * h + t, :, off:off + K1],
                                              m.ps[:, (0 if off == 0 else 2) + h, t * P:(t + 1) * P].rearrange(
                                                  "p (g k) -> p g k", k=K1)).then_inc(evac_done, 1)


def delta_stage(nc, m):
    LV = [2, 4, 8, 16]
    G = 4
    with signals(nc, "staged padded walk_staged state_ready dec_done gram_done diff_ready lt_ready lmask_ready nt_ready "
                     "xt_ready x_turned x_ready y_done ym_ready z_done x_next u_done u_ready ntm_ready w_done w_ready "
                     "v2_done solved wt_done wt_ready read_done vnew_ready o_ready upd_done s_ready oi_done out_ready ch"
                 ) as (
            staged, padded, walk_staged, state_ready, dec_done, gram_done, diff_ready, lt_ready, lmask_ready, nt_ready,
            xt_ready, x_turned, x_ready, y_done, ym_ready, z_done, x_next, u_done, u_ready, ntm_ready, w_done, w_ready,
            v2_done, solved, wt_done, wt_ready, read_done, vnew_ready, o_ready, upd_done, s_ready, oi_done, out_ready,
            chs):
        def heads(buf, g):
            return buf[:, g * G:(g + 1) * G, :]

        def bank(k, g):
            return m.ps[:, 2 * k + g, :].rearrange("p (h c) -> p h c", h=G)

        def over_heads(mask):
            return bcast(mask.unsqueeze(1), P, G, P)

        def tile(buf, it):
            return buf[:, ds(it * P, P)]

        def four(k, g, lhs, rhs, n=P):
            for h in range(G):
                ins = nc.tensor.matmul(m.ps[:, 2 * k + g, h * n:(h + 1) * n], lhs(g * G + h), rhs(g * G + h),
                                       start=True, stop=True)
            return ins

        def side(ap, l, odd):
            return ap.rearrange("p (a two s) -> p a two s", two=2, s=LV[l])[:, :, odd, :]

        WT, READ, UPD = (m.ps[:, 6, k * P:(k + 1) * P] for k in range(3))
        READO, INTRA = (m.ps[:, 7, k * P:(k + 1) * P] for k in range(2))
        with nc.Block() as block:
            @block.gpsimd
            def _(pool):
                nc.gpsimd.memset(m.state[:], 0.0).then_inc(state_ready, 1)
                pool.wait_ge(state_ready, 1)

                def stage_gram(t):
                    nc.gpsimd.tensor_copy(m.wk_t[:], tile(m.wk[:, 0:T], t)).then_inc(staged, 1)
                    nc.gpsimd.tensor_tensor(m.wkb_h[:], bcast(tile(m.wkb, t).unsqueeze(1), P, H1, P),
                                            bcast(m.hmask[:].unsqueeze(2), P, H1, P), ALU.mult).then_inc(staged, 1)
                    nc.gpsimd.tensor_tensor(m.rk_h[:], bcast(tile(m.rk, t).unsqueeze(1), P, H1, P),
                                            bcast(m.hmask[:].unsqueeze(2), P, H1, P), ALU.mult).then_inc(staged, 1)

                def stage_walk(t):
                    nc.gpsimd.tensor_copy(m.rkd_t[:], tile(m.rkd, t)).then_inc(walk_staged, 1)
                    nc.gpsimd.tensor_copy(m.kd_t[:], m.kd[:, ds(t, 1), :].rearrange("p o c -> p (o c)")
                                          ).then_inc(walk_staged, 1)
                    nc.gpsimd.tensor_copy(m.sd_t[:], m.sdecay[:, ds(t * 2, 2)]).then_inc(walk_staged, 1)

                def masks(t):
                    for buf, mask in ((m.lts, m.strictT[:]), (m.lti, m.chunk_upto[:])):
                        for g in range(2):
                            pool.wait_ge(lt_ready, t * 2 + g + 1)
                            nc.gpsimd.tensor_tensor(heads(buf, g), heads(m.lt, g), over_heads(mask),
                                                    ALU.mult).then_inc(lmask_ready, 1)

                def far_blocks(t):
                    for g in range(2):
                        pool.wait_ge(nt_ready, t * 2 + g + 1)
                        nc.gpsimd.tensor_tensor(heads(m.ntm, g), heads(m.nt, g), over_heads(m.levT[:, 1, :]),
                                                ALU.mult).then_inc(ntm_ready, 1)

                def turn(t, more):
                    far_blocks(t)
                    if more:
                        pool.wait_ge(gram_done, t * 2 + 2)
                        stage_gram(t + 1)
                        masks(t + 1)
                        pool.wait_ge(state_ready, 1)
                        pool.wait_ge(out_ready, t + 2)
                        stage_walk(t + 1)

                stage_gram(0)
                stage_walk(0)
                masks(0)
                with pool.Fori(0, NT - 1) as it:
                    turn(it, True)
                turn(NT - 1, False)

            @block.tensor
            def _(pe):
                pe.wait_ge(state_ready, 1)

                def decays(t, g):
                    for h in range(G):
                        ins = nc.tensor.matmul(m.ps[:, g, h * P:(h + 1) * P], m.sel8[:, g * G + h, :],
                                               m.decT[:, ds(t * P, P)], start=True, stop=True)
                    ins.then_inc(dec_done, 1)

                def gram(t, g):
                    pe.wait_ge(staged, t * 3 + 3)
                    nc.tensor.matmul(m.ps[:, 2 + g, :], m.wk_t[:],
                                     heads(m.wkb_h, g).rearrange("p h c -> p (h c)"), start=True, stop=True)
                    nc.tensor.matmul(m.ps[:, 4 + g, :], m.wk_t[:],
                                     heads(m.rk_h, g).rearrange("p h c -> p (h c)"), start=True,
                                     stop=True).then_inc(gram_done, 1)

                def turn_x(t, g):
                    pe.wait_ge(xt_ready, t * 2 + g + 1)
                    for h in range(G):
                        ins = nc.tensor.transpose(m.ps[:, g, h * P:(h + 1) * P], m.xt[:, g * G + h, :], m.ident[:])
                    ins.then_inc(x_turned, 1)

                def solve(t, more):
                    for l in range(len(LV)):
                        for g in range(2):
                            if l == 0:
                                pe.wait_ge(x_ready, t * 2 + g + 1)
                            else:
                                pe.wait_ge(x_next, t * 8 + (l - 1) * 2 + g + 1)
                            four(1, g, lambda h: m.nt[:, h, :], lambda h: m.xi[:, h, :]).then_inc(y_done, 1)
                        for g in range(2):
                            pe.wait_ge(ym_ready, t * 8 + l * 2 + g + 1)
                            if l < len(LV) - 1:
                                four(2, g, lambda h: m.xt[:, h, :], lambda h: m.ym[l][:, h, :])
                            if l == 0 and g == 0:
                                pe.wait_ge(out_ready, t + 1)
                            four(3, g, lambda h: m.ym[l][:, h, :], lambda h: m.xt[:, h, :]).then_inc(z_done, 1)
                        if more and l < 2:
                            decays(t + 1, l)
                    for g in range(2):
                        pe.wait_ge(x_next, t * 8 + 6 + g + 1)
                        four(0, g, lambda h: m.xt[:, h, :],
                             lambda h: m.rhs[:, ds(t, 1), h, :].rearrange("p o k -> p (o k)"), 2 * K1).then_inc(u_done, 1)
                    for g in range(2):
                        pe.wait_ge(u_ready, t * 2 + g + 1)
                        pe.wait_ge(ntm_ready, t * 2 + g + 1)
                        four(1, g, lambda h: m.ntm[:, h, :], lambda h: m.u[:, h, :], 2 * K1).then_inc(w_done, 1)
                    for g in range(2):
                        pe.wait_ge(w_ready, t * 2 + g + 1)
                        four(2, g, lambda h: m.xt[:, h, :], lambda h: m.w[:, h, :], 2 * K1).then_inc(v2_done, 1)

                def read_state(t, c):
                    if c:
                        pe.wait_ge(s_ready, t * 2 + c)
                        pe.wait_ge(o_ready, t * 2 + c)
                    nc.tensor.matmul(READ, m.wcT[:], m.state[:], start=True, stop=True).then_inc(read_done, 1)
                    nc.tensor.matmul(READO, m.rkd_t[:], m.state[:], start=True, stop=True).then_inc(read_done, 1)

                def update(t, c):
                    pe.wait_ge(vnew_ready, t * 2 + c + 1)
                    nc.tensor.matmul(UPD, m.kd_t[c * C1:(c + 1) * C1, :],
                                     m.vnew[c * C1:(c + 1) * C1, :], start=True, stop=True).then_inc(upd_done, 1)

                def turn(t, more):
                    solve(t, more)
                    pe.wait_ge(solved, t * 2 + 2)
                    nc.tensor.transpose(WT, m.wsol[:], m.ident[:]).then_inc(wt_done, 1)
                    if more:
                        gram(t + 1, 0)
                    pe.wait_ge(wt_ready, t + 1)
                    pe.wait_ge(walk_staged, t * 3 + 3)
                    read_state(t, 0)
                    if more:
                        gram(t + 1, 1)
                    update(t, 0)
                    if more:
                        turn_x(t + 1, 0)
                    read_state(t, 1)
                    update(t, 1)
                    pe.wait_ge(o_ready, t * 2 + 2)
                    for h in range(H1):
                        ins = nc.tensor.matmul(INTRA[:, h * K1:(h + 1) * K1], m.at[:, h, :],
                                               m.vnew[:, h * K1:(h + 1) * K1], start=True, stop=True)
                    ins.then_inc(oi_done, 1)
                    if more:
                        turn_x(t + 1, 1)

                for g in range(2):
                    decays(0, g)
                for g in range(2):
                    gram(0, g)
                for g in range(2):
                    turn_x(0, g)
                with pe.Fori(0, NT - 1) as it:
                    turn(it, True)
                turn(NT - 1, False)

            @block.scalar
            def _(act):
                def decay(t, g):
                    act.wait_ge(diff_ready, t * 2 + g + 1)
                    nc.scalar.activation(heads(m.lt, g), heads(m.lt, g), ACT.Exp).then_inc(lt_ready, 1)

                def take_x(t, g):
                    act.wait_ge(x_turned, t * 2 + g + 1)
                    nc.scalar.activation(heads(m.xi, g), bank(0, g), ACT.Copy).then_inc(x_ready, 1)

                def turn(t, more):
                    if more:
                        for g in range(2):
                            decay(t + 1, g)
                    for g in range(2):
                        act.wait_ge(u_done, t * 2 + g + 1)
                        nc.scalar.activation(heads(m.u, g).rearrange("p h k -> p (h k)"), m.ps[:, g, 0:G * 2 * K1],
                                             ACT.Copy).then_inc(u_ready, 1)
                    for g in range(2):
                        act.wait_ge(w_done, t * 2 + g + 1)
                        nc.scalar.activation(heads(m.w, g).rearrange("p h k -> p (h k)"), m.ps[:, 2 + g, 0:G * 2 * K1],
                                             ACT.Copy).then_inc(w_ready, 1)
                    act.wait_ge(wt_done, t + 1)
                    nc.scalar.activation(m.wcT[:], WT, ACT.Copy).then_inc(wt_ready, 1)
                    for c in range(2):
                        r = slice(c * C1, (c + 1) * C1)
                        act.wait_ge(read_done, t * 4 + 2 * c + 2)
                        nc.scalar.activation(m.ointer[r, :], READO[r, :], ACT.Copy).then_inc(o_ready, 1)
                        if more:
                            take_x(t + 1, c)

                for g in range(2):
                    decay(0, g)
                for g in range(2):
                    take_x(0, g)
                with act.Fori(0, NT - 1) as it:
                    turn(it, True)
                turn(NT - 1, False)

            @block.vector
            def _(dve):
                def decay(t, g, c_):
                    dve.wait_ge(dec_done, t * 2 + g + 1)
                    c_.link(nc.vector.tensor_tensor(heads(m.lt, g), bank(0, g),
                                                    bcast(m.dec[:, ds(t * H1 + g * G, G)].unsqueeze(2), P, G, P),
                                                    ALU.subtract))
                    lt = heads(m.lt, g).rearrange("p h c -> p (h c)")
                    nc.vector.tensor_scalar(lt, lt, 0.0, None, ALU.min).then_inc(diff_ready, 1)

                def systems(t, g, c_):
                    dve.wait_ge(gram_done, t * 2 + g + 1)
                    dve.wait_ge(lmask_ready, t * 4 + g + 1)
                    nc.vector.tensor_tensor(heads(m.nt, g), bank(1, g), heads(m.lts, g), ALU.mult).then_inc(nt_ready, 1)
                    dve.wait_ge(nt_ready, t * 2 + g + 1)
                    c_.link(nc.vector.tensor_tensor(heads(m.xt, g), heads(m.nt, g), over_heads(m.levT[:, 0, :]), ALU.mult))
                    nc.vector.tensor_tensor(heads(m.xt, g), over_heads(m.ident[:]), heads(m.xt, g),
                                            ALU.subtract).then_inc(xt_ready, 1)

                def intra(t, c_):
                    for g in range(2):
                        dve.wait_ge(lmask_ready, t * 4 + g + 3)
                        c_.add(nc.vector.tensor_tensor(heads(m.at, g), bank(2, g), heads(m.lti, g), ALU.mult))
                    assert c_.n == 6

                def turn(t, more):
                    c_ = Chain(dve, chs, (t + 1) * 6)
                    for l in range(len(LV)):
                        for g in range(2):
                            dve.wait_ge(y_done, t * 8 + l * 2 + g + 1)
                            s, a = LV[l], P // 2 // LV[l]
                            nc.vector.tensor_tensor(
                                heads(m.ym[l], g).rearrange("p h (a two s) -> p h a two s", two=2, s=s)[:, :, :, 0, :],
                                bank(1, g).rearrange("p h (a two s) -> p h a two s", two=2, s=s)[:, :, :, 0, :],
                                bcast(side(m.lev[:, l, :], l, 0).unsqueeze(1), P, G, a, s), ALU.mult).then_inc(ym_ready, 1)
                        for g in range(2):
                            dve.wait_ge(z_done, t * 8 + l * 2 + g + 1)
                            if l < len(LV) - 1:
                                joined = side(heads(m.xi, g).rearrange("p h c -> p (h c)"), l, 0)
                                nc.vector.tensor_tensor(joined, joined, side(m.ps[:, 4 + g, :], l, 0), ALU.subtract)
                            joined = side(heads(m.xt, g).rearrange("p h c -> p (h c)"), l, 1)
                            nc.vector.tensor_tensor(joined, joined, side(m.ps[:, 6 + g, :], l, 1), ALU.subtract).then_inc(x_next, 1)
                        if more and l < 2:
                            decay(t + 1, l, c_)
                    for g in range(2):
                        dve.wait_ge(v2_done, t * 2 + g + 1)
                        o = m.ps[:, 4 + g, 0:G * 2 * K1].rearrange("p (h k) -> p h k", k=2 * K1)
                        nc.vector.tensor_tensor(m.vsol[:].rearrange("p (h k) -> p h k", k=K1)[:, g * G:(g + 1) * G, :],
                                                heads(m.u, g)[:, :, 0:K1], o[:, :, 0:K1], ALU.subtract)
                        nc.vector.tensor_tensor(m.wsol[:].rearrange("p (h k) -> p h k", k=K1)[:, g * G:(g + 1) * G, :],
                                                heads(m.u, g)[:, :, K1:2 * K1], o[:, :, K1:2 * K1],
                                                ALU.subtract).then_inc(solved, 1)
                    dve.wait_ge(solved, t * 2 + 2)
                    for c in range(2):
                        r = slice(c * C1, (c + 1) * C1)
                        dve.wait_ge(read_done, t * 4 + 2 * c + 1)
                        nc.vector.tensor_tensor(m.vnew[r, :], m.vsol[r, :], READ[r, :], ALU.subtract).then_inc(vnew_ready, 1)
                        if more:
                            systems(t + 1, c, c_)
                        dve.wait_ge(upd_done, t * 2 + c + 1)
                        nc.vector.tensor_tensor(m.supd[:, c, :], UPD, m.bdiag[:], ALU.mult).then_inc(state_ready, 1)
                        dve.wait_ge(state_ready, t * 2 + c + 2)
                        nc.vector.scalar_tensor_tensor(out=m.state[:], in0=m.state[:], scalar=m.sd_t[:, c:c + 1],
                                                       in1=m.supd[:, c, :], op0=ALU.mult, op1=ALU.add).then_inc(s_ready, 1)
                    dve.wait_ge(oi_done, t + 1)
                    dve.wait_ge(o_ready, t * 2 + 2)
                    nc.vector.tensor_tensor(m.o[:, ds(t, 1), :].rearrange("p o c -> p (o c)"), m.ointer[:],
                                            INTRA, ALU.add).then_inc(out_ready, 1)
                    if more:
                        intra(t + 1, c_)

                for z in m.ym:
                    nc.vector.memset(z, 0.0).then_inc(padded, 1)
                dve.wait_ge(padded, 4)
                dve.sem_inc(out_ready, 1)
                first = Chain(dve, chs)
                for g in range(2):
                    decay(0, g, first)
                for g in range(2):
                    systems(0, g, first)
                intra(0, first)
                with dve.Fori(0, NT - 1) as it:
                    turn(it, True)
                turn(NT - 1, False)


def delta_out_stage(nc, m):
    NH = NT * H1
    with signals(nc, "sq_ready ms_ready root_ready o_ready turned oT_ready out_done added ch") as (
            sq_ready, ms_ready, root_ready, o_ready, turned, oT_ready, out_done, added, chs):
        with nc.Block() as block:
            @block.scalar
            def _(act):
                nc.scalar.activation(m.sq, m.o.rearrange("p t c -> p (t c)"), ACT.Square).then_inc(sq_ready, 1)
                act.wait_ge(ms_ready, 1)
                nc.scalar.activation(m.rn[:], m.rn[:], ACT.Sqrt).then_inc(root_ready, 1)
                for h in range(2):
                    act.wait_ge(turned, h + 1)
                    nc.scalar.activation(m.kdT[:, h * HALF:(h + 1) * HALF], m.ps[:, h, :], ACT.Copy).then_inc(oT_ready, 1)

            @block.vector
            def _(dve):
                ch = Chain(dve, chs)
                dve.wait_ge(sq_ready, 1)
                ch.link(nc.vector.tensor_reduce(m.rn[:], m.sq.rearrange("p (n k) -> p n k", k=K1), AX, ALU.add))
                nc.vector.tensor_scalar(m.rn[:], m.rn[:], 1.0 / K1, EPS_RMS, ALU.mult, ALU.add).then_inc(ms_ready, 1)
                dve.wait_ge(root_ready, 1)
                ch.link(nc.vector.reciprocal(m.rn[:], m.rn[:]))
                ov = m.o.rearrange("p t (h k) -> p (t h) k", k=K1)
                ch.link(nc.vector.tensor_tensor(ov, ov, bcast(m.rn[:].unsqueeze(2), P, NH, K1), ALU.mult))
                ch.link(nc.vector.tensor_tensor(ov, ov, bcast(m.normw[:].unsqueeze(1), P, NH, K1), ALU.mult))
                nc.vector.tensor_tensor(m.o, m.o, m.gate, ALU.mult).then_inc(o_ready, 1)
                for h in range(2):
                    dve.wait_ge(out_done, h + 1)
                    xs = m.x[:, 4 * h:4 * h + 4, :].rearrange("p t c -> p (t c)")
                    nc.vector.tensor_tensor(xs, m.ps[:, 2 + h, :], xs, ALU.add).then_inc(added, 1)

            @block.tensor
            def _(pe):
                pe.wait_ge(o_ready, 1)
                for t in range(NT):
                    ins = nc.tensor.transpose(m.ps[:, t // 4, (t % 4) * P:(t % 4 + 1) * P], m.o[:, t, :], m.ident[:])
                    if t % 4 == 3:
                        ins.then_inc(turned, 1)
                for t in range(NT):
                    pe.wait_ge(oT_ready, t // 4 + 1)
                    ins = nc.tensor.matmul(m.ps[:, 2 + t // 4, (t % 4) * P:(t % 4 + 1) * P], m.kdT[:, t * P:(t + 1) * P],
                                           m.woT[:], start=True, stop=True)
                    if t % 4 == 3:
                        ins.then_inc(out_done, 1)




def layer_prepare_stage(nc, m, a, l):
    with signals(nc, "loaded tables_in pad_ready turned hT_ready folded") as (
            loaded, tables_in, pad_ready, turned, hT_ready, folded):
        with nc.Block() as block:
            @block.sync
            def _(sp):
                sp.dma_start(m.rope, a["rope"]).then_inc(tables_in, 16)
                load_layer(sp, m, a, l, ["qks"], tables_in)
                load_layer(sp, m, a, l, ["wqkv", "wo"], loaded)
                sp.wait_ge(loaded, 16 * 2)

            @block.gpsimd
            def _(pool):
                nc.gpsimd.memset(m.kwin, 0.0).then_inc(pad_ready, 1)
                nc.gpsimd.memset(m.va[:, 0, :], 0.0).then_inc(pad_ready, 1)
                nc.gpsimd.memset(m.pw[:, :, 0:P - WIN], 0.0).then_inc(pad_ready, 1)

            @block.vector
            def _(dve):
                nc.vector.memset(m.hT[P // 2:P, 0:1], 0.0).then_inc(pad_ready, 1)
                dve.wait_ge(tables_in, 16 * 2)
                for j in range(4):
                    nc.vector.tensor_tensor(m.rope[:, j, :, :], m.rope[:, j, :, :],
                                            bcast(m.qks[:, j, :].unsqueeze(1), P, NT, HD2), ALU.mult).then_inc(folded, 1)

            @block.tensor
            def _(pe):
                for t in range(NT):
                    ins = nc.tensor.transpose(m.ps[:, t // 4, (t % 4) * P:(t % 4 + 1) * P], m.hc[:, t, :], m.ident[:])
                    if t % 4 == 3:
                        ins.then_inc(turned, 1)

            @block.scalar
            def _(act):
                for h in range(2):
                    act.wait_ge(turned, h + 1)
                    nc.scalar.activation(m.hT[0:P // 2, h * HALF:(h + 1) * HALF], m.ps[0:P // 2, h, :],
                                         ACT.Copy).then_inc(hT_ready, 1)
                    nc.scalar.activation(m.hT[P // 2:P, 1 + h * HALF:1 + (h + 1) * HALF], m.ps[P // 2:P, h, :],
                                         ACT.Copy).then_inc(hT_ready, 1)


def load_layer(sp, m, a, l, names, loaded):
    for name in names:
        ap = a[name][ds(l, 1)]
        dims = " ".join("abc"[:len(ap.shape) - 2])
        sp.dma_start(m.named[name][:], ap.rearrange(f"o p {dims} -> (o p) {dims}")).then_inc(loaded, 16)


def window_stage(nc, m, a, l):
    with signals(nc, "staged qkv_done sq_ready ss_ready prod_ready v_ready rot_ready qk_turned qT_ready "
                     "kT_ready scores_done shifted probs_ready p_turned evac_a evac_d values_done y_ready "
                     "o_turned oT_ready wo_done hc_ready ch rn_ready window_moved band_ready padded bounded "
                     "terms_ready loaded") as (
            staged, qkv_done, sq_ready, ss_ready, prod_ready, v_ready, rot_ready, qk_turned, qT_ready,
            kT_ready, scores_done, shifted, probs_ready, p_turned, evac_a, evac_d, values_done, y_ready,
            o_turned, oT_ready, wo_done, hc_ready, chs, rn_ready, window_moved, band_ready, padded, bounded,
            terms_ready, loaded):
        HD = HD2 // 2
        QB, OB, VB, TB, SB, YB = 0, 1, 2, 3, 5, 7
        pairs = m.qT_t.rearrange("p (a b) q -> p a b q", b=2)
        with nc.Block() as block:
            @block.sync
            def _(sp):
                load_layer(sp, m, a, l, ["w1", "w2", "lgb", "b1", "b2"], loaded)
                sp.wait_ge(loaded, 16 * 5)

            @block.gpsimd
            def _(pool):
                def stage(t):
                    nc.gpsimd.tensor_copy(m.hT_t[:], m.hT[:, ds(t * P, P)]).then_inc(staged, 1)

                def wait_apart(sem, count):
                    count = pool.to_reg(count)
                    pool.wait_ge(staged, 1)
                    pool.wait_ge(sem, count)

                def rotate(t):
                    wait_apart(ss_ready, t * 2 + 2)
                    nc.gpsimd.tensor_scalar(m.qkn[:], m.qkn[:], 1e-24, None, ALU.max).then_inc(bounded, 1)
                    pool.wait_ge(bounded, t + 1)
                    nc.gpsimd.tensor_tensor(m.qkn[:], m.qkn[:], bcast(m.minus_half[:], P, 2 * H2),
                                            ALU.pow).then_inc(rn_ready, 1)
                    for j in range(2):
                        qv = m.rot[:, j, :, :]
                        pool.wait_ge(prod_ready, t * 2 + j + 1)
                        pool.wait_ge(rn_ready, t + 1)
                        nc.gpsimd.tensor_tensor(qv, qv, bcast(m.qkn[:, j * H2:(j + 1) * H2].unsqueeze(2), P, H2, HD2),
                                                ALU.mult).then_inc(rot_ready, 1)

                def turn(t):
                    wait_apart(qkv_done, t * 3 + 3)
                    stage(t + 1)
                    rotate(t + 1)
                    wait_apart(scores_done, t * H2 + H2)
                    nc.gpsimd.tensor_copy(m.kwin[:, :, 0:WIN], m.kwin[:, :, P:KW]).then_inc(window_moved, 1)
                    wait_apart(shifted, t * H2 + H2)
                    nc.gpsimd.tensor_copy(m.band_t[:], m.band[:, 1, :]).then_inc(band_ready, 1)

                stage(0)
                nc.gpsimd.tensor_copy(m.band_t[:], m.band[:, 0, :]).then_inc(band_ready, 1)
                pool.wait_ge(band_ready, 1)
                nc.gpsimd.memset(pairs[HD2:P, :, 0, :], 0.0).then_inc(padded, 1)
                pool.wait_ge(padded, 1)
                nc.gpsimd.memset(pairs[0:HD2, :, 1, :], 0.0).then_inc(padded, 1)
                pool.wait_ge(padded, 2)
                rotate(0)
                with pool.Fori(0, NT - 1) as it:
                    turn(it)

            @block.tensor
            def _(pe):
                def project(t, j):
                    if j == 0:
                        pe.wait_ge(staged, t + 1)
                    nc.tensor.matmul(m.ps[:, QB + j, :], m.hT_t[:], m.wqkv[:, j * INNER:(j + 1) * INNER], start=True,
                                     stop=True).then_inc(qkv_done, 1)

                def turn_qk(t):
                    for j in range(2):
                        pe.wait_ge(rot_ready, t * 2 + j + 1)
                        for p in range(4):
                            ins = nc.tensor.transpose(m.ps[:, TB + j, p * P:(p + 1) * P],
                                                      m.rot[:, j, 2 * p:2 * p + 2, :].rearrange("p h d -> p (h d)"),
                                                      m.ident[:])
                        ins.then_inc(qk_turned, 1)

                def scores(t, h):
                    if h >= 2:
                        pe.wait_ge(shifted, t * H2 + h - 1)
                    nc.tensor.matmul(m.ps[:, SB + h % 2, 0:KW], m.qT_t[:, h, :], m.kwin[:, h // 2, :], start=True,
                                     stop=True).then_inc(scores_done, 1)

                def first_scores(t):
                    pe.wait_ge(qT_ready, t * 2 + 2)
                    pe.wait_ge(kT_ready, t + 1)
                    pe.wait_ge(v_ready, t + 1)
                    scores(t, 0)
                    scores(t, 1)

                def turn(t, more):
                    def copied(h):
                        pe.wait_ge(evac_a if h % 2 else evac_d, t * 4 + h // 2 + 1)

                    def turn_probs(h):
                        pe.wait_ge(probs_ready, t * H2 + h + 1)
                        if h >= 2:
                            copied(h - 2)
                        for k in range(2):
                            ins = nc.tensor.transpose(m.ps[:, TB + h % 2, k * P:(k + 1) * P],
                                                      m.pw[:, h % 4, k * P:(k + 1) * P], m.ident[:])
                        ins.then_inc(p_turned, 1)

                    def values(h):
                        copied(h)
                        for k in range(2):
                            ins = nc.tensor.matmul(m.ps[:, YB, h * HD2:(h + 1) * HD2], m.pwT[:, h % 2, k, :],
                                                   m.va[:, ds(t + k, 1), h * HD2:(h + 1) * HD2].rearrange("p o c -> p (o c)"),
                                                   start=(k == 0), stop=(k == 1))
                        ins.then_inc(values_done, 1)

                    for n in range(2, H2 + 3):
                        if n < H2:
                            scores(t, n)
                        if n - 2 < H2:
                            turn_probs(n - 2)
                        if more and n <= 4:
                            if n - 2 == OB:
                                pe.wait_ge(hc_ready, t + 1)
                            project(t + 1, n - 2)
                        if n >= 3:
                            values(n - 3)
                    if more:
                        turn_qk(t + 1)
                        pe.wait_ge(v_ready, t + 2)
                    pe.wait_ge(y_ready, t + 1)
                    for p in range(4):
                        ins = nc.tensor.transpose(m.ps[:, VB, p * P:(p + 1) * P], m.ow[:, p * P:(p + 1) * P], m.ident[:])
                    ins.then_inc(o_turned, 1)
                    if more:
                        first_scores(t + 1)
                    pe.wait_ge(oT_ready, t + 1)
                    for p in range(4):
                        ins = nc.tensor.matmul(m.ps[:, OB, 0:P], m.oT[:, p * P:(p + 1) * P], m.wo[:, p, :],
                                               start=(p == 0), stop=(p == 3))
                    ins.then_inc(wo_done, 1)

                for j in range(3):
                    project(0, j)
                turn_qk(0)
                pe.wait_ge(padded, 2)
                first_scores(0)
                with pe.Fori(0, NT - 1) as it:
                    turn(it, True)
                turn(NT - 1, False)

            @block.scalar
            def _(act):
                def square(t, j):
                    act.wait_ge(qkv_done, t * 3 + j + 1)
                    nc.scalar.activation(m.sqw[:, j, :], m.ps[:, QB + j, :], ACT.Square).then_inc(sq_ready, 1)

                def take_values(t):
                    act.wait_ge(qkv_done, t * 3 + 3)
                    nc.scalar.activation(m.va[:, ds(t + 1, 1), :].rearrange("p o c -> p (o c)"), m.ps[:, VB, :],
                                         ACT.Copy).then_inc(v_ready, 1)

                def take_queries(t):
                    act.wait_ge(qk_turned, t * 2 + 1)
                    for j in range(2):
                        r = slice(j * HD2, (j + 1) * HD2)
                        nc.scalar.activation(pairs[r, :, j, :], m.ps[r, TB, :].rearrange("p (a q) -> p a q", a=4), ACT.Copy
                                             ).then_inc(qT_ready, 1)

                def take_keys(t):
                    act.wait_ge(qk_turned, t * 2 + 2)
                    nc.scalar.activation(m.kwin[:, :, WIN:KW], m.ps[:, TB + 1, :].rearrange("p (h q) -> p h q", h=4),
                                         ACT.Copy).then_inc(kT_ready, 1)

                def exp(t, h):
                    act.wait_ge(shifted, t * H2 + h + 1)
                    nc.scalar.activation(m.pw[:, h % 4, P - WIN:2 * P], m.pw[:, h % 4, P - WIN:2 * P], ACT.Exp,
                                         bias=m.nmaxw[:, h:h + 1], scale=-1.0,
                                         accum_out=m.esumw[:, h:h + 1]).then_inc(probs_ready, 1)

                def turn(t, more):
                    for n in range(2, H2 + 2):
                        h = n - 2
                        if h % 2 == 1:
                            act.wait_ge(p_turned, t * H2 + h + 1)
                            if h >= 2:
                                act.wait_ge(values_done, t * H2 + h - 1)
                            nc.scalar.activation(m.pwT[:, 1, :, :].rearrange("p k q -> p (k q)"), m.ps[:, TB + 1, 0:2 * P],
                                                 ACT.Copy).then_inc(evac_a, 1)
                        if n < H2:
                            exp(t, n)
                        if more and n in (3, 4):
                            square(t + 1, n - 3)
                        if more and n == 5:
                            take_values(t + 1)
                    if more:
                        take_queries(t + 1)
                        act.wait_ge(window_moved, t + 1)
                        take_keys(t + 1)
                    act.wait_ge(o_turned, t + 1)
                    nc.scalar.activation(m.oT, m.ps[:, VB, :], ACT.Copy).then_inc(oT_ready, 1)
                    if more:
                        exp(t + 1, 0)
                        exp(t + 1, 1)

                for j in range(2):
                    square(0, j)
                take_values(0)
                take_queries(0)
                take_keys(0)
                exp(0, 0)
                exp(0, 1)
                with act.Fori(0, NT - 1) as it:
                    turn(it, True)
                turn(NT - 1, False)

            @block.vector
            def _(dve):
                def norm(t, j):
                    dve.wait_ge(sq_ready, t * 2 + j + 1)
                    nc.vector.tensor_reduce(m.qkn[:, j * H2:(j + 1) * H2],
                                            m.sqw[:, j, :].rearrange("p (h d) -> p h d", h=H2), AX, ALU.add
                                            ).then_inc(ss_ready, 1)

                def products(t, j):
                    src = m.ps[:, QB + j, :].rearrange("p (h d) -> p h d", h=H2)

                    def table(i, a, b):
                        return bcast(m.rope[:, 2 * j + i, ds(t, 1), a:b], P, H2, b - a)

                    dve.wait_ge(sq_ready, t * 2 + 2)
                    nc.vector.tensor_tensor(m.rot[:, j, :, :], src, table(0, 0, HD2), ALU.mult)
                    nc.vector.tensor_tensor(m.rot2[:, j, :, 0:HD], src[:, :, HD:HD2], table(1, 0, HD), ALU.mult)
                    nc.vector.tensor_tensor(m.rot2[:, j, :, HD:HD2], src[:, :, 0:HD], table(1, HD, HD2),
                                            ALU.mult).then_inc(terms_ready, 1)
                    dve.wait_ge(terms_ready, t * 2 + j + 1)
                    nc.vector.tensor_tensor(m.rot[:, j, :, :], m.rot[:, j, :, :], m.rot2[:, j, :, :],
                                            ALU.add).then_inc(prod_ready, 1)

                def shift(t, h):
                    if h >= 4:
                        dve.wait_ge(p_turned, t * H2 + h - 3)
                    if h == 0:
                        dve.wait_ge(band_ready, t + 1)
                    count = dve.to_reg(t * H2 + h + 1)
                    dve.wait_ge(band_ready, 1)
                    dve.wait_ge(scores_done, count)
                    nc.vector.tensor_tensor_reduce(m.pw[:, h % 4, P - WIN:2 * P], m.ps[:, SB + h % 2, 0:KW],
                                                   m.band_t[:], 1.0, 3.0e38,
                                                   ALU.add, ALU.min, m.nmaxw[:, h:h + 1]).then_inc(shifted, 1)

                def turn(t, more):
                    for n in range(2, H2 + 3):
                        if n < H2:
                            shift(t, n)
                        h = n - 2
                        if h < H2 and h % 2 == 0:
                            dve.wait_ge(p_turned, t * H2 + h + 1)
                            if h >= 2:
                                dve.wait_ge(values_done, t * H2 + h - 1)
                            nc.vector.tensor_copy(m.pwT[:, 0, :, :].rearrange("p k q -> p (k q)"),
                                                  m.ps[:, TB, 0:2 * P]).then_inc(evac_d, 1)
                        if more and n in (4, 5):
                            norm(t + 1, n - 4)
                        if more and n in (6, 8):
                            products(t + 1, n // 2 - 3)
                    dve.wait_ge(values_done, t * H2 + H2)
                    Chain(dve, chs, t).link(nc.vector.reciprocal(m.rsumw[:], m.esumw[:]))
                    nc.vector.tensor_tensor(m.ow.rearrange("p (h d) -> p h d", h=H2),
                                            m.ps[:, YB, :].rearrange("p (h d) -> p h d", h=H2),
                                            bcast(m.rsumw[:].unsqueeze(2), P, H2, HD2), ALU.mult).then_inc(y_ready, 1)
                    if more:
                        shift(t + 1, 0)
                        shift(t + 1, 1)
                    dve.wait_ge(wo_done, t + 1)
                    hv = m.hc[:, ds(t, 1), :].rearrange("p o c -> p (o c)")
                    nc.vector.tensor_tensor(hv, m.ps[:, OB, 0:P], hv, ALU.add).then_inc(hc_ready, 1)

                dve.sem_inc(hc_ready, 1)
                for j in range(2):
                    norm(0, j)
                for j in range(2):
                    products(0, j)
                shift(0, 0)
                shift(0, 1)
                with dve.Fori(0, NT - 1) as it:
                    turn(it, True)
                turn(NT - 1, False)


def shift_stage(nc, m):
    U = P // 2
    with signals(nc, "shifted low_ready high_ready") as (shifted, low_ready, high_ready):
        with nc.Block() as block:
            @block.tensor
            def _(pe):
                for t in range(NT):
                    ins = nc.tensor.matmul(m.ps[:, 0, t * U:(t + 1) * U], m.late[:], m.hc[:, t, U:P], start=True,
                                           stop=(t == 0))
                    if t:
                        ins = nc.tensor.matmul(m.ps[:, 0, t * U:(t + 1) * U], m.carry[:], m.hc[:, t - 1, U:P],
                                               start=False, stop=True)
                ins.then_inc(shifted, 1)

            @block.vector
            def _(dve):
                nc.vector.tensor_copy(m.hs[:, :, 0:U], m.hc[:, :, 0:U]).then_inc(low_ready, 1)
                dve.wait_ge(shifted, 1)
                nc.vector.tensor_copy(m.hs[:, :, U:P], m.ps[:, 0, :].rearrange("p (t c) -> p t c", t=NT)).then_inc(
                    high_ready, 1)


def mlp_stage(nc, m):
    NCH = len(HCH)
    with signals(nc, "up_done gelu_ready hid_ready down_done biased added") as (
            up_done, gelu_ready, hid_ready, down_done, biased, added):
        with nc.Block() as block:
            @block.tensor
            def _(pe):
                def up(half):
                    for i, (c0, n) in enumerate(HCH):
                        if half:
                            pe.wait_ge(hid_ready, i + 1)
                        for j in range(2):
                            ins = nc.tensor.matmul(m.ps[0:n, 3 * j + i, :], m.w1[:, j * HID + c0:j * HID + c0 + n],
                                                   m.hnT[:, half * HALF:(half + 1) * HALF], start=True, stop=True)
                        ins.then_inc(up_done, 1)

                def down(half):
                    pe.wait_ge(hid_ready, NCH * (half + 1))
                    for t in range(4):
                        for i, (c0, n) in enumerate(HCH):
                            ins = nc.tensor.matmul(m.ps[:, 6 + half, t * P:(t + 1) * P], m.hidm[0:n, half, i, t * P:(t + 1) * P],
                                                   m.w2[0:n, i, :], start=(i == 0), stop=(i == NCH - 1))
                    ins.then_inc(down_done, 1)

                up(0)
                up(1)
                down(0)
                down(1)

            @block.scalar
            def _(act):
                for half in range(2):
                    for i, (c0, n) in enumerate(HCH):
                        act.wait_ge(up_done, half * NCH + i + 1)
                        nc.scalar.activation(m.gel[0:n, half, i, :], m.ps[0:n, 3 + i, :], ACT.Gelu,
                                             bias=m.b1[0:n, i, 1:2]).then_inc(gelu_ready, 1)

            @block.vector
            def _(dve):
                nc.vector.tensor_tensor(m.hc, m.hc, bcast(m.b2[:].unsqueeze(1), P, NT, D), ALU.add).then_inc(biased, 1)
                for half in range(2):
                    for i, (c0, n) in enumerate(HCH):
                        dve.wait_ge(gelu_ready, half * NCH + i + 1)
                        nc.vector.scalar_tensor_tensor(out=m.hidm[0:n, half, i, :], in0=m.ps[0:n, i, :],
                                                       scalar=m.b1[0:n, i, 0:1], in1=m.gel[0:n, half, i, :],
                                                       op0=ALU.add, op1=ALU.mult).then_inc(hid_ready, 1)
                dve.wait_ge(biased, 1)
                for half in range(2):
                    dve.wait_ge(down_done, half + 1)
                    hv = m.hc[:, 4 * half:4 * half + 4, :].rearrange("p t c -> p (t c)")
                    nc.vector.tensor_tensor(hv, m.ps[:, 6 + half, :], hv, ALU.add).then_inc(added, 1)




SBUF = {
    "ident": [P, P], "ones": [P, P], "zeros": [P, P],
    "before": [P, P],
    "below": [P, P],
    "later": [P, P],
    "want": [P, 3, NSEL],
    "gateT": [P, E0], "wprojT": [P, PAIRS, P], "bproj": [P, 1],
    "pack": [P, 2, 4 * P], "wst": [P, 3 * P], "qkvb": [P, PAIRS * 3],
    "x": [P, NT, D], "xn": [P, NT, D], "xnT": [P, T], "ffnT": [P, T],
    "bn": [P, NT, 6], "mv": [P, NT, 2], "rstd": [P, NT],
    "rs8": [P, NT], "rs8b": [P, NT], 
    "score": [P, NT, E0 + 1], "rest": [P, NT, E0], "top8": [P, NT, 8],
    "combT": [E0 + 1, T], "silu": [P, 2, HALF], "hid": [P, 2, HALF],
    "qT": [P, 2, T], "kT": [P, T], "v": [P, NT, P], "srelu": [P, 2, T], "past": [P, T],
    "pen": [P, NT, T], "bitf": [P, NSEL], "few": [P, NSEL], "count": [P, NSEL], "need": [P, NSEL],
    "prob": [P, 4, T], "nmax": [P, 4], "esum": [P, 8], "rsum": [P, 4], "pT": [P, 2, NT, P],
    "y": [P, 2, P], "yT": [P, PAIRS, T],
    "chunk_upto": [P, P],
    "strictT": [P, P],
    "bdiag": [P, P],
    "hmask": [P, H1],
    "lev": [P, 4, P],
    "levT": [P, 2, P],
    "sel8": [H1, H1, P], "wvT": [P, D], "wbT16": [P, D], "waT": [P, H1], "wgT": [P, D], "woT": [P, D],
    "dtb": [P, H1], "nega": [P, H1], "convw": [P, 5], "normw": [P, K1],
    "wk": [P, 1 + T], "xv": [P, 3 + T], "rn": [P, NT * H1], "z64": [P, NT * H1], "e64": [P, NT * H1],
    "r64": [P, NT * H1], "rr64": [P, NT * H1], "q64": [P, NT * H1], "decay": [P, NT * H1], "dec": [P, NT * H1],
    "sdecay": [P, NC1], "sd_t": [P, 2],
    "wk_t": [P, P], "rkd_t": [P, P], "kd_t": [P, P], "wcT": [P, P], "ointer": [P, P], "vnew": [P, P],
    "vsol": [P, P], "wsol": [P, P], "state": [P, P], "supd": [P, 2, P], "u": [P, H1, 2 * K1], "w": [P, H1, 2 * K1],
    "late": [P, P],
    "carry": [P, P],
    "band": [P, 2, KW],
    "band_t": [P, KW],
    "wqkv": [P, 3 * INNER], "wo": [P, 4, D], "w1": [P, 2 * HID], "w2": [P, len(HCH), D],
    "lgb": [P, 2], "b1": [P, len(HCH), 2], "b2": [P, D], "qks": [P, 4, HD2],
    "hT_t": [P, P], "minus_half": [P, 1], "qkn": [P, 2 * H2],
    "nmaxw": [P, H2], "esumw": [P, H2], "rsumw": [P, H2],
}
SBUF_INT = {"biti": [P, NSEL], "nextbit": [P, NSEL], "thr": [P, NSEL], "cand": [P, NSEL]}


class Memory:

    def __init__(self, named):
        self.named = named
        self.minus_half, self.nextbit = named["minus_half"], named["nextbit"]
        self.ident, self.ones, self.zeros, self.before, self.below, self.later = (
            named[n] for n in "ident ones zeros before below later".split())
        self.qkvb = named["qkvb"]
        self.want, self.gateT, self.wprojT, self.bproj, self.pack, self.wst = (
            named[n] for n in "want gateT wprojT bproj pack wst".split())
        self.x, self.xn, self.xnT, self.ffnT, self.bn, self.mv = (
            named[n] for n in "x xn xnT ffnT bn mv".split())
        self.rstd, self.rs8, self.rs8b, self.score, self.rest, self.top8 = (
            named[n] for n in "rstd rs8 rs8b score rest top8".split())
        self.combT, self.silu, self.hid, self.qT, self.kT, self.v = (
            named[n] for n in "combT silu hid qT kT v".split())
        self.srelu, self.past, self.pen, self.bitf, self.few, self.count = (
            named[n] for n in "srelu past pen bitf few count".split())
        self.need, self.prob, self.nmax, self.esum, self.rsum, self.pT = (
            named[n] for n in "need prob nmax esum rsum pT".split())
        self.y, self.yT, self.chunk_upto, self.strictT, self.bdiag, self.hmask = (
            named[n] for n in "y yT chunk_upto strictT bdiag hmask".split())
        self.lev, self.levT, self.sel8, self.wvT, self.wbT16, self.waT = (
            named[n] for n in "lev levT sel8 wvT wbT16 waT".split())
        self.wgT, self.woT, self.dtb, self.nega, self.convw, self.normw = (
            named[n] for n in "wgT woT dtb nega convw normw".split())
        self.wk, self.xv, self.rn, self.z64, self.e64, self.r64 = (
            named[n] for n in "wk xv rn z64 e64 r64".split())
        self.rr64, self.q64, self.decay, self.dec, self.sdecay, self.sd_t = (
            named[n] for n in "rr64 q64 decay dec sdecay sd_t".split())
        self.wk_t, self.rkd_t, self.kd_t, self.wcT, self.ointer, self.vnew = (
            named[n] for n in "wk_t rkd_t kd_t wcT ointer vnew".split())
        self.vsol, self.wsol, self.state, self.supd, self.u, self.w = (
            named[n] for n in "vsol wsol state supd u w".split())
        self.late, self.carry, self.band, self.band_t, self.wqkv, self.wo = (
            named[n] for n in "late carry band band_t wqkv wo".split())
        self.w1, self.w2, self.lgb, self.b1, self.b2, self.qks = (
            named[n] for n in "w1 w2 lgb b1 b2 qks".split())
        self.hT_t, self.qkn, self.nmaxw, self.esumw, self.rsumw, self.biti = (
            named[n] for n in "hT_t qkn nmaxw esumw rsumw biti".split())
        self.thr, self.cand = (
            named[n] for n in "thr cand".split())


def share_buffers(m):
    flat = {n: m.named[n][:].rearrange("p a b -> p (a b)") for n in ("pen", "yT", "srelu", "prob", "pack", "silu", "hid")}
    flat["pT"] = m.pT[:].rearrange("p a b c -> p (a b c)")

    def part(name, at, *shape):
        n = int(np.prod(shape))
        ap = flat[name][:, at:at + n]
        if len(shape) == 2:
            return ap.rearrange("p (a b) -> p a b", a=shape[0])
        if len(shape) == 4:
            return ap.rearrange("p (a b c d) -> p a b c d", a=shape[0], b=shape[1], c=shape[2])
        if len(shape) == 3:
            return ap.rearrange("p (a b c) -> p a b c", a=shape[0], b=shape[1])
        return ap

    m.junk = flat["yT"].bitcast(BF16)
    m.sq, m.vb, m.beta, m.decE, m.grow, m.wkb, m.wkbd, m.resto = (part("pen", i * T, T) for i in range(8))
    m.rk, m.rkd, m.kdT = (part("yT", i * T, T) for i in range(3))
    m.xr, m.gate, m.o = (part("yT", (3 + i) * T, NT, D) for i in range(3))
    m.rhs = part("yT", 6 * T, NT, H1, 2 * K1)
    m.kd, m.decT, m.decay16 = m.v, m.combT[0:H1, :], m.kT[:].rearrange("p (t c) -> p t c", t=NT)
    m.lt, m.lts = part("pT", 0, H1, P), part("pT", T, H1, P)
    m.lti, m.nt = part("prob", 0, H1, P), part("prob", T, H1, P)
    m.at, m.xt = part("srelu", 0, H1, P), part("srelu", T, H1, P)
    m.xi, m.wkb_h = part("silu", 0, H1, P), part("pack", 0, H1, P)
    m.ym = [part("hid", 0, H1, P), part("prob", 2 * T, H1, P), part("prob", 3 * T, H1, P),
            m.qT[:, 1, :].rearrange("p (h c) -> p h c", h=H1)]
    m.rk_h, m.ntm = (z.rearrange("p (t c) -> p t c", t=NT) for z in (m.qT[:, 0, :], m.past[:]))
    m.hc = m.ffnT[:].rearrange("p (t c) -> p t c", t=NT)
    m.hT = m.xv
    m.rope = flat["srelu"].rearrange("p (j t d) -> p j t d", j=4, t=NT)
    KE = 4 * (P + T)
    m.kwin = part("pen", 0, 4, KW)
    m.va = part("yT", 0, NT + 1, INNER)
    m.rot, m.rot2, m.sqw = part("pen", KE, 2, H2, HD2), part("pen", KE + 2 * INNER, 2, H2, HD2), part("pen", KE + 4 * INNER, 2, INNER)
    m.pw, m.pwT = part("yT", KE, 4, 2 * P), part("yT", KE + 4 * INNER, 2, 2, P)
    m.qT_t, m.ow, m.oT = part("yT", KE + 5 * INNER, H2, P), part("yT", KE + 2 * INNER, INNER), part("yT", KE + 3 * INNER, INNER)
    m.hs, m.hn, m.hnT = part("pT", 0, NT, D), part("pT", T, NT, D), m.past[:]
    m.gel, m.hidm = part("pen", 0, 2, len(HCH), HALF), part("yT", 0, 2, len(HCH), HALF)


def build(nc, a, out):
    with ExitStack() as ctx:
        named = {n: ctx.enter_context(nc.sbuf_tensor(n, shape, F32)) for n, shape in SBUF.items()}
        named.update({n: ctx.enter_context(nc.sbuf_tensor(n, shape, I32)) for n, shape in SBUF_INT.items()})
        m = Memory(named)
        m.ps = ctx.enter_context(nc.psum_tensor("ps", [P, 8, HALF], F32))
        m.psf = m.ps[:].rearrange("p b c -> p (b c)")
        share_buffers(m)
        m.candf, m.thrf = m.cand[:].bitcast(F32), m.thr[:].bitcast(F32)
        setup_stage(nc, m, a)
        with nc.Fori(0, B) as b:
            batch_row(nc, m, a, out, b)


def setup_stage(nc, m, a):
    loads = ["ident", "ones", "before", "below", "later", "want", "wprojT", "bproj", "qkvb", "chunk_upto", "strictT", "bdiag",
             "hmask", "lev", "levT", "sel8", "wvT", "wbT16", "waT", "wgT", "woT", "dtb", "nega", "convw", "normw",
             "late", "carry", "band"]
    with signals(nc, "loaded cleared gate_in sq_ready root_ready ch turned") as (
            loaded, cleared, gate_in, sq_ready, root_ready, chs, turned):
        with nc.Block() as block:
            @block.sync
            def _(sp):
                for name in loads:
                    sp.dma_start(m.named[name][:], a[name]).then_inc(loaded, 16)
                sp.dma_start(m.y[0:E0, 0, :], a["gate_w"]).then_inc(gate_in, 16)
                sp.wait_ge(loaded, 16 * len(loads))

            @block.gpsimd
            def _(pool):
                nc.gpsimd.memset(m.zeros[:], 0.0)
                nc.gpsimd.memset(m.minus_half[:], -0.5)
                nc.gpsimd.memset(m.score[:], 1.0)

            @block.scalar
            def _(act):
                act.wait_ge(loaded, 16 * len(loads))
                nc.scalar.activation(m.nega[:], m.nega[:], ACT.Exp).then_inc(cleared, 1)
                act.wait_ge(gate_in, 16)
                nc.scalar.activation(m.y[0:E0, 1, :], m.y[0:E0, 0, :], ACT.Square,
                                     accum_out=m.rs8[0:E0, 0:1]).then_inc(sq_ready, 1)
                act.wait_ge(sq_ready, 1)
                nc.scalar.activation(m.rs8b[0:E0, 0:1], m.rs8[0:E0, 0:1], ACT.Sqrt).then_inc(root_ready, 1)

            @block.vector
            def _(dve):
                ch = Chain(dve, chs)
                dve.wait_ge(root_ready, 1)
                r = m.rs8b[0:E0, 0:1]
                ch.link(nc.vector.tensor_scalar(r, r, 1e-12, None, ALU.max))
                ch.link(nc.vector.reciprocal(r, r))
                ch.link(nc.vector.tensor_scalar(m.y[0:E0, 0, :], m.y[0:E0, 0, :], r, None, ALU.mult))
                dve.wait_ge(cleared, 1)
                ch.add(nc.vector.tensor_scalar(m.nega[:], m.nega[:], -1.0, None, ALU.mult))
                dve.wait_ge(turned, 1)
                nc.vector.tensor_copy(m.gateT[:], m.ps[:, 0, 0:E0])

            @block.tensor
            def _(pe):
                pe.wait_ge(chs, 3)
                pe.wait_ge(loaded, 16 * len(loads))
                nc.tensor.transpose(m.ps[:, 0, 0:E0], m.y[0:E0, 0, :], m.ident[0:E0, 0:E0]).then_inc(turned, 1)


def copy_stage(nc, m):
    with nc.Block() as block:
        @block.vector
        def _(dve):
            nc.vector.tensor_copy(m.hc, m.xn[:])


def add_stage(nc, m):
    with nc.Block() as block:
        @block.vector
        def _(dve):
            nc.vector.tensor_tensor(m.x[:], m.x[:], m.hc, ALU.add)


def batch_row(nc, m, a, out, b):
    with signals(nc, "x_in") as (x_in,):
        with nc.Block() as block:
            @block.sync
            def _(sp):
                sp.dma_start(m.x[:], a["x"][ds(b, 1)].rearrange("o (t p) d -> p (o t) d", p=P)).then_inc(x_in, 16)
                sp.wait_ge(x_in, 16)
    norm_stage(nc, m, m.x, m.xn, m.xnT)
    penalty_stage(nc, m, a["qkv_packs"])
    experts_stage(nc, m, a["packs"])
    attention_stage(nc, m, a["qkv_packs"])
    project_stage(nc, m)
    norm_stage(nc, m, m.x, m.xn, m.xnT)
    delta_prepare_stage(nc, m)
    delta_stage(nc, m)
    delta_out_stage(nc, m)
    copy_stage(nc, m)
    with nc.Fori(0, DEPTH) as l:
        layer_prepare_stage(nc, m, a, l)
        window_stage(nc, m, a, l)
        shift_stage(nc, m)
        norm_stage(nc, m, m.hs, m.hn, m.hnT, m.lgb[:, 0:1], m.lgb[:, 1:2])
        mlp_stage(nc, m)
    add_stage(nc, m)
    with signals(nc, "x_out") as (x_out,):
        with nc.Block() as block:
            @block.sync
            def _(sp):
                sp.dma_start(out[ds(b, 1)].rearrange("o (t p) d -> p (o t) d", p=P), m.x[:]).then_inc(x_out, 16)
                sp.wait_ge(x_out, 16)




def shape_constants():
    i = np.arange(P)
    r, c = i[:, None], i[None, :]
    f = lambda z: np.ascontiguousarray(z, dtype=np.float32)
    row = np.arange(TSEL, NT)[None, :] * P + r
    k = np.minimum(KEEP, row + 1)
    width = (np.arange(TSEL, NT) + 1)[None, :] * P
    act = np.zeros(NSEL, bool)
    act[:0:-2] = True
    want = np.stack([np.where(act[None, :], 2 * k - width, k), k, np.broadcast_to(act[None, :], k.shape)], axis=1)
    same = r // C1 == c // C1

    def joins(rows, cols, s):
        return same & ((rows // s) % 2 == 1) & (cols // s == rows // s - 1)

    half = np.arange(0, HD2, 2, dtype=np.float32)
    inv = (1.0 / np.float32(10000.0) ** (half / np.float32(HD2))).astype(np.float32)
    tt = np.arange(T, dtype=np.float32)
    ang = (tt[:, None] * inv[None, :]).astype(np.float32).astype(np.float64)
    grown = ((half + 0.4 * HD2) / (1.4 * HD2)).astype(np.float64)[None, :] ** ((tt.astype(np.float64) - T // 2) / (WIN // 2))[:, None]
    two = lambda z: np.concatenate([z, z], -1)
    signed = lambda z: np.concatenate([-z, z], -1)
    rope = np.stack([-8 * two(np.cos(ang) * grown), -8 * signed(np.sin(ang) * grown), two(np.cos(ang) / grown),
                     signed(np.sin(ang) / grown)])
    key = np.arange(KW)[None, None, :] - WIN
    tile = np.arange(2)[None, :, None]
    off = r[:, :, None] - key
    seen = (off >= 0) & (off <= WIN) & (tile * P + key >= 0)
    return {
        "chunk_upto": f(same & (r <= c)), "strictT": f(same & (r < c)), "bdiag": f(r // K1 == c // K1),
        "hmask": f(r // K1 == np.arange(H1)[None, :]),
        "lev": f(np.stack([joins(r, c, s) for s in (2, 4, 8, 16)], 1)),
        "levT": f(np.stack([joins(c, r, s) for s in (1, 32)], 1)),
        "sel8": f(np.broadcast_to(np.eye(H1)[:, :, None], (H1, H1, P))),
        "late": f(r == c - 1), "carry": f((r == P - 1) & (c == 0)), "band": f(np.where(seen, 0.0, BIG)),
        "rope": f(rope.reshape(4, NT, P, HD2).transpose(2, 0, 1, 3)),
        "ident": f(r == c), "ones": f(np.ones((P, P))), "before": f(r < c), "below": f(c < r),
        "later": f((c > r) * BIG), "want": f(want),
    }


def layouts(i):
    f32 = np.float32
    w = np.asarray(i["L0_attn_W_attn"]).reshape(3, PAIRS, P, D)
    bias = np.asarray(i["L0_attn_b_attn"]).reshape(3, PAIRS, P)
    qkv, qkvb = np.zeros((PAIRS, P, 3 * P), f32), np.zeros((P, PAIRS, 3), f32)
    for j in range(3):
        qkv[:, :, j * P:(j + 1) * P] = w[j].transpose(0, 2, 1)
        qkvb[:, :, j] = bias[j].T
    packs = np.zeros((PACKS, P, 4 * P), f32)
    for p in range(PACKS - 1):
        for e in range(2):
            packs[p, :, e * HE0:(e + 1) * HE0] = i["L0_ffn_w_gate"][2 * p + e]
            packs[p, :, P + e * HE0:P + (e + 1) * HE0] = i["L0_ffn_w_up"][2 * p + e]
            packs[p, e * HE0:(e + 1) * HE0, 2 * P:3 * P] = i["L0_ffn_w_down"][2 * p + e]
            packs[p, 2 * p + e, 3 * P + e * HE0:3 * P + (e + 1) * HE0] = 1.0
    packs[-1, :, 0:HE0] = i["L0_ffn_sw_gate"]
    packs[-1, :, P:P + HE0] = i["L0_ffn_sw_up"]
    packs[-1, 0:HE0, 2 * P:3 * P] = i["L0_ffn_sw_down"]
    packs[-1, E0, 3 * P:4 * P] = 1.0
    c = np.ascontiguousarray
    wproj = np.asarray(i["L0_attn_W_proj"]).reshape(D, PAIRS, P).transpose(2, 1, 0)
    g = {n: np.asarray(v) for n, v in i.items()}
    rows = lambda z: c(np.broadcast_to(z[..., None, :], (*z.shape[:-1], P, z.shape[-1])))
    qs, ks = g["L1_ffn_q_scale"], g["L1_ffn_k_scale"]
    qks = np.stack([qs, np.roll(qs, HD2 // 2, -1), ks, np.roll(ks, HD2 // 2, -1)], 1)
    w2, b1 = np.zeros((DEPTH, P, len(HCH), D), f32), np.zeros((DEPTH, P, len(HCH), 2), f32)
    for j, (c0, n) in enumerate(HCH):
        w2[:, 0:n, j, :] = g["L1_ffn_w2"][:, c0:c0 + n, :]
        for k in range(2):
            b1[:, 0:n, j, k] = g["L1_ffn_b1"][:, k * HID + c0:k * HID + c0 + n]
    return {
        "wvT": c(g["L1_attn_Wv"].T), "wgT": c(g["L1_attn_Wg"].T), "woT": c(g["L1_attn_Wo"].T),
        "waT": c(g["L1_attn_Wa"].T), "wbT16": c(np.repeat(g["L1_attn_Wb"].T, K1, axis=1)),
        "dtb": rows(g["L1_attn_dt_bias"]), "nega": rows(g["L1_attn_A_log"]), "normw": rows(g["L1_attn_norm_w"]),
        "convw": c(np.concatenate([g["L1_attn_conv_w"], g["L1_attn_conv_b"][:, None]], 1)),
        "wqkv": c(g["L1_ffn_wqkv"]), "w1": c(g["L1_ffn_w1"]), "w2": w2, "b1": b1, "b2": rows(g["L1_ffn_b2"]),
        "wo": c(g["L1_ffn_wo"].reshape(DEPTH, 4, P, D).transpose(0, 2, 1, 3)),
        "lgb": c(np.stack([g["L1_ffn_ln_g"], g["L1_ffn_ln_b"]], -1)),
        "qks": c(np.broadcast_to(qks[:, None], (DEPTH, P, 4, HD2))),
        "x": c(i["L0_attn_x"]), "gate_w": c(i["L0_ffn_gate_w"]), "qkv_packs": qkv, "qkvb": qkvb.reshape(P, PAIRS * 3), "packs": packs,
        "wprojT": c(wproj), "bproj": c(np.asarray(i["L0_attn_b_proj"]).reshape(D, 1)),
    }


def kernel(**inputs):
    import concourse.bacc as bacc
    from concourse.bass_utils import run_bass_kernel_spmd

    nc = bacc.Bacc("TRN2", target_bir_lowering=False, num_devices=1)
    arrays = {n: np.asarray(v) for n, v in {**shape_constants(), **layouts(inputs)}.items()}
    a = {n: nc.dram_tensor(f"in_{n}", v.shape, mybir.dt.from_np(v.dtype), kind="ExternalInput").ap()
         for n, v in arrays.items()}
    out = nc.dram_tensor("out", (B, T, D), F32, kind="ExternalOutput").ap()
    build(nc, a, out)
    r = run_bass_kernel_spmd(nc, [{f"in_{n}": v for n, v in arrays.items()}], core_ids=[0])
    return r.results[0]["out"]
```
